# Optimizing a Trainium2 kernel written in Bass

```python
import numpy as np
import jax
import jax.numpy as jnp

def _softmax(x, axis=-1):
    return jax.nn.softmax(x, axis=axis)

def _gelu(x):
    return jax.nn.gelu(x, approximate=True)

def _silu(x):
    return jax.nn.silu(x)

def _sigmoid(x):
    return jax.nn.sigmoid(x)

def _layernorm(x, axis=-1, eps=1e-05):
    m = jnp.mean(x, axis=axis, keepdims=True)
    v = jnp.var(x, axis=axis, keepdims=True)
    return (x - m) / jnp.sqrt(v + eps)

def _scatter_add(tgt, idx, src, axis=0):
    return tgt.at[idx].add(src)

def _segment_sum(src, seg, n):
    return jax.ops.segment_sum(src, seg, n)
kernel_name = 'mk_sandwich_d1_jaxref_r8_7ae69b'

def setup_inputs(seed: int=0):
    np.random.seed(seed)
    _w = jnp.asarray

    def _L0_attn_setup():
        import jax, jax.numpy as jnp
        import numpy as np
        D_MODEL = 128
        N_HEADS = 16
        HEAD_DIM = D_MODEL // N_HEADS
        WINDOW = 128
        LOCAL_BLOCK = 32
        LATENT_TOKENS = 64
        LATENT_D = 32
        LATENT_HEADS = 4
        LATENT_HD = LATENT_D // LATENT_HEADS
        NEG = -1000000000.0

        def _local_attention(q, k, v):
            B, H, S, hd = q.shape
            bs = min(S, max(WINDOW, LOCAL_BLOCK))
            nb = S // bs
            w = WINDOW
            L = bs + w - 1
            k_pad = jnp.pad(k, ((0, 0), (0, 0), (w - 1, 0), (0, 0)))
            v_pad = jnp.pad(v, ((0, 0), (0, 0), (w - 1, 0), (0, 0)))
            starts = jnp.arange(nb) * bs
            idx = starts[:, None] + jnp.arange(L)[None, :]
            kb = k_pad[:, :, idx]
            vb = v_pad[:, :, idx]
            qb = q.reshape(B, H, nb, bs, hd)
            q_pos = starts[:, None] + jnp.arange(bs)[None, :]
            k_gpos = starts[:, None] + jnp.arange(L)[None, :] - (w - 1)
            dist = q_pos[:, :, None] - k_gpos[:, None, :]
            allowed = (dist > 0) & (dist <= w) & (k_gpos[:, None, :] >= 0)
            scale = 1.0 / np.sqrt(hd)
            scores = jnp.einsum('bhnqd,bhnkd->bhnqk', qb, kb) * scale
            scores = jnp.where(allowed, scores, NEG)
            attn = jax.nn.softmax(scores, axis=-1)
            attn = jnp.where(allowed.any(-1)[None, None, :, :, None], attn, 0.0)
            out = jnp.einsum('bhnqk,bhnkd->bhnqd', attn, vb)
            return out.reshape(B, H, S, hd)
        key = jax.random.key(seed)
        ks = jax.random.split(key, 14)
        B, S = (2, 512)
        s = 0.02
        f32 = jnp.float32
        return {'x': jax.random.normal(ks[0], (B, S, D_MODEL), f32), 'qkv_w': jax.random.normal(ks[1], (D_MODEL, 3 * D_MODEL), f32) * s, 'qkv_b': jnp.zeros((3 * D_MODEL,), f32), 'rq_w': jax.random.normal(ks[2], (D_MODEL, LATENT_D), f32) * s, 'rq_b': jnp.zeros((LATENT_D,), f32), 'rkv_w': jax.random.normal(ks[3], (D_MODEL, 2 * LATENT_D), f32) * s, 'rkv_b': jnp.zeros((2 * LATENT_D,), f32), 'rout_w': jax.random.normal(ks[4], (LATENT_D, D_MODEL), f32) * s, 'rout_b': jnp.zeros((D_MODEL,), f32), 'out_w': jax.random.normal(ks[5], (D_MODEL, D_MODEL), f32) * s, 'out_b': jnp.zeros((D_MODEL,), f32), 'gl_w': jax.random.normal(ks[6], (HEAD_DIM, 1), f32) * s, 'gr_w': jax.random.normal(ks[7], (HEAD_DIM, 1), f32) * s}
    _L0_attn_in = _L0_attn_setup()

    def _L0_ffn_setup():
        import jax, jax.numpy as jnp
        import numpy as np
        H = 128
        I = 512
        E = 4
        LN_EPS = 1e-12

        def _layer_norm(x, gamma, beta, eps=LN_EPS):
            mu = jnp.mean(x, axis=-1, keepdims=True)
            var = jnp.mean(jnp.square(x - mu), axis=-1, keepdims=True)
            return (x - mu) * jax.lax.rsqrt(var + eps) * gamma + beta
        key = jax.random.key(seed)
        ks = jax.random.split(key, 8)
        B, S = (4, 64)
        scale = 0.02
        return {'hidden_states': jax.random.normal(ks[0], (B, S, H), jnp.float32), 'W_router': jax.random.normal(ks[1], (H, E), jnp.float32) * scale, 'W1': jax.random.normal(ks[2], (E, H, I), jnp.float32) * scale, 'b1': jax.random.normal(ks[3], (E, I), jnp.float32) * scale, 'Wo': jax.random.normal(ks[4], (I, H), jnp.float32) * scale, 'bo': jax.random.normal(ks[5], (H,), jnp.float32) * scale, 'ln_gamma': jnp.ones((H,), jnp.float32), 'ln_beta': jnp.zeros((H,), jnp.float32)}
    _L0_ffn_in = _L0_ffn_setup()
    _d = {'L0_attn_x': _L0_attn_in['x'], 'L0_attn_qkv_w': _L0_attn_in['qkv_w'], 'L0_attn_qkv_b': _L0_attn_in['qkv_b'], 'L0_attn_rq_w': _L0_attn_in['rq_w'], 'L0_attn_rq_b': _L0_attn_in['rq_b'], 'L0_attn_rkv_w': _L0_attn_in['rkv_w'], 'L0_attn_rkv_b': _L0_attn_in['rkv_b'], 'L0_attn_rout_w': _L0_attn_in['rout_w'], 'L0_attn_rout_b': _L0_attn_in['rout_b'], 'L0_attn_out_w': _L0_attn_in['out_w'], 'L0_attn_out_b': _L0_attn_in['out_b'], 'L0_attn_gl_w': _L0_attn_in['gl_w'], 'L0_attn_gr_w': _L0_attn_in['gr_w'], 'L0_ffn_W_router': _L0_ffn_in['W_router'], 'L0_ffn_W1': _L0_ffn_in['W1'], 'L0_ffn_b1': _L0_ffn_in['b1'], 'L0_ffn_Wo': _L0_ffn_in['Wo'], 'L0_ffn_bo': _L0_ffn_in['bo'], 'L0_ffn_ln_gamma': _L0_ffn_in['ln_gamma'], 'L0_ffn_ln_beta': _L0_ffn_in['ln_beta']}
    _x0 = _d['L0_attn_x']
    _d['L0_attn_x'] = jax.random.normal(jax.random.fold_in(jax.random.key(seed), 1), (2, 2048, 128), dtype=_x0.dtype)
    del _x0
    return _d

def reference(L0_attn_x, L0_attn_qkv_w, L0_attn_qkv_b, L0_attn_rq_w, L0_attn_rq_b, L0_attn_rkv_w, L0_attn_rkv_b, L0_attn_rout_w, L0_attn_rout_b, L0_attn_out_w, L0_attn_out_b, L0_attn_gl_w, L0_attn_gr_w, L0_ffn_W_router, L0_ffn_W1, L0_ffn_b1, L0_ffn_Wo, L0_ffn_bo, L0_ffn_ln_gamma, L0_ffn_ln_beta):

    def _L0_attn_ref(x, qkv_w, qkv_b, rq_w, rq_b, rkv_w, rkv_b, rout_w, rout_b, out_w, out_b, gl_w, gr_w):
        import jax, jax.numpy as jnp
        import numpy as np
        D_MODEL = 128
        N_HEADS = 16
        HEAD_DIM = D_MODEL // N_HEADS
        WINDOW = 128
        LOCAL_BLOCK = 32
        LATENT_TOKENS = 64
        LATENT_D = 32
        LATENT_HEADS = 4
        LATENT_HD = LATENT_D // LATENT_HEADS
        NEG = -1000000000.0

        def _local_attention(q, k, v):
            B, H, S, hd = q.shape
            bs = min(S, max(WINDOW, LOCAL_BLOCK))
            nb = S // bs
            w = WINDOW
            L = bs + w - 1
            k_pad = jnp.pad(k, ((0, 0), (0, 0), (w - 1, 0), (0, 0)))
            v_pad = jnp.pad(v, ((0, 0), (0, 0), (w - 1, 0), (0, 0)))
            starts = jnp.arange(nb) * bs
            idx = starts[:, None] + jnp.arange(L)[None, :]
            kb = k_pad[:, :, idx]
            vb = v_pad[:, :, idx]
            qb = q.reshape(B, H, nb, bs, hd)
            q_pos = starts[:, None] + jnp.arange(bs)[None, :]
            k_gpos = starts[:, None] + jnp.arange(L)[None, :] - (w - 1)
            dist = q_pos[:, :, None] - k_gpos[:, None, :]
            allowed = (dist > 0) & (dist <= w) & (k_gpos[:, None, :] >= 0)
            scale = 1.0 / np.sqrt(hd)
            scores = jnp.einsum('bhnqd,bhnkd->bhnqk', qb, kb) * scale
            scores = jnp.where(allowed, scores, NEG)
            attn = jax.nn.softmax(scores, axis=-1)
            attn = jnp.where(allowed.any(-1)[None, None, :, :, None], attn, 0.0)
            out = jnp.einsum('bhnqk,bhnkd->bhnqd', attn, vb)
            return out.reshape(B, H, S, hd)
        B, S, D = x.shape
        qkv = x @ qkv_w + qkv_b
        q, k, v = jnp.split(qkv, 3, axis=-1)

        def heads(t):
            return t.reshape(B, S, N_HEADS, HEAD_DIM).transpose(0, 2, 1, 3)
        local = _local_attention(heads(q), heads(k), heads(v))
        chunk = -(-S // min(LATENT_TOKENS, S))
        nlat = S // chunk
        pooled = x.reshape(B, nlat, chunk, D).mean(axis=2)
        chunk_ids = jnp.arange(S) // chunk
        rq = (x @ rq_w + rq_b).reshape(B, S, LATENT_HEADS, LATENT_HD).transpose(0, 2, 1, 3)
        rkv = pooled @ rkv_w + rkv_b
        rk, rv = jnp.split(rkv, 2, axis=-1)
        rk = rk.reshape(B, nlat, LATENT_HEADS, LATENT_HD).transpose(0, 2, 1, 3)
        rv = rv.reshape(B, nlat, LATENT_HEADS, LATENT_HD).transpose(0, 2, 1, 3)
        lscale = 1.0 / np.sqrt(LATENT_HD)
        lscores = jnp.einsum('bhsd,bhld->bhsl', rq, rk) * lscale
        lat_allowed = jnp.arange(nlat)[None, :] < chunk_ids[:, None]
        lscores = jnp.where(lat_allowed[None, None], lscores, NEG)
        lattn = jax.nn.softmax(lscores, axis=-1)
        lattn = jnp.where(lat_allowed.any(-1)[None, None, :, None], lattn, 0.0)
        lat_out = jnp.einsum('bhsl,bhld->bhsd', lattn, rv)
        lat_out = lat_out.transpose(0, 2, 1, 3).reshape(B, S, LATENT_D)
        remote = lat_out @ rout_w + rout_b
        remote_h = remote.reshape(B, S, N_HEADS, HEAD_DIM).transpose(0, 2, 1, 3)
        gate = jax.nn.sigmoid(local @ gl_w + remote_h @ gr_w)
        mixed = gate * local + (1.0 - gate) * remote_h
        mixed = mixed.transpose(0, 2, 1, 3).reshape(B, S, D)
        return mixed @ out_w + out_b

    def _L0_ffn_ref(hidden_states, W_router, W1, b1, Wo, bo, ln_gamma, ln_beta):
        import jax, jax.numpy as jnp
        import numpy as np
        H = 128
        I = 512
        E = 4
        LN_EPS = 1e-12

        def _layer_norm(x, gamma, beta, eps=LN_EPS):
            mu = jnp.mean(x, axis=-1, keepdims=True)
            var = jnp.mean(jnp.square(x - mu), axis=-1, keepdims=True)
            return (x - mu) * jax.lax.rsqrt(var + eps) * gamma + beta
        B, S, _ = hidden_states.shape
        x = hidden_states.reshape(-1, H)
        logits = x @ W_router
        expert_idx = jnp.argmax(logits, axis=-1)
        h = jnp.einsum('th,ehi->tei', x, W1) + b1
        h = jax.nn.gelu(h, approximate=False)
        onehot = jax.nn.one_hot(expert_idx, E, dtype=x.dtype)
        intermediate = jnp.einsum('te,tei->ti', onehot, h)
        y = intermediate @ Wo + bo + x
        y = _layer_norm(y, ln_gamma, ln_beta)
        return y.reshape(B, S, H)
    x = L0_attn_x
    x = x + _layernorm(_L0_attn_ref(_layernorm(x, axis=-1), L0_attn_qkv_w, L0_attn_qkv_b, L0_attn_rq_w, L0_attn_rq_b, L0_attn_rkv_w, L0_attn_rkv_b, L0_attn_rout_w, L0_attn_rout_b, L0_attn_out_w, L0_attn_out_b, L0_attn_gl_w, L0_attn_gr_w), axis=-1)
    x = x + _layernorm(_L0_ffn_ref(_layernorm(x, axis=-1), L0_ffn_W_router, L0_ffn_W1, L0_ffn_b1, L0_ffn_Wo, L0_ffn_bo, L0_ffn_ln_gamma, L0_ffn_ln_beta), axis=-1)
    return x

_drawn_inputs = setup_inputs


def setup_inputs(seed=0):
    import zlib

    import numpy as np

    out = dict(_drawn_inputs(seed))
    spreads = {'L0_attn_qkv_b': (0.0, 0.1),
     'L0_attn_rq_b': (0.0, 2.0),
     'L0_attn_rkv_b': (0.0, 0.8),
     'L0_attn_rout_b': (0.0, 0.1),
     'L0_attn_out_b': (0.0, 0.1),
     'L0_ffn_ln_gamma': (1.0, 0.2),
     'L0_ffn_ln_beta': (0.0, 0.1)}
    factors = {'L0_attn_qkv_w': 3.034,
     'L0_attn_rq_w': 8.0,
     'L0_attn_rkv_w': 8.0,
     'L0_attn_rout_w': 6.227,
     'L0_attn_gl_w': 30.308,
     'L0_attn_gr_w': 8.0,
     'L0_ffn_W_router': 2.747,
     'L0_ffn_b1': 29.711,
     'L0_ffn_bo': 5.688}
    for name, (base, spread) in spreads.items():
        noise = np.random.default_rng([zlib.crc32(name.encode()), seed]).standard_normal(out[name].shape)
        drawn = base * np.exp(spread * noise) if base else spread * noise
        out[name] = jnp.asarray(drawn.astype(out[name].dtype))
    for name, factor in factors.items():
        out[name] = (out[name] * factor).astype(out[name].dtype)
    return out
```

```python
from contextlib import ExitStack

import concourse.bass as bass
from concourse import mybir

F32 = mybir.dt.float32
BF16 = mybir.dt.bfloat16
ACT = mybir.ActivationFunctionType
ALU = mybir.AluOpType
AX = mybir.AxisListType

P = 128
B, S, D = 2, 2048, 128
T = B * S
NB = T // P
BB = S // P
H, HD = 16, 8
LH, LHD, LD = 4, 8, 32
NLAT = 64
LCH = S // NLAT
PC = P // LCH
E, I = 4, 512
IT = I // P
CH = 512
NCH = T // CH
CT = CH // P
RING = 8
OCT = NB // RING
LATW = PC * (RING - 1) + NLAT
LC = 2
STORES = 16 * 4
LOADS = 14
PARTS_Q = [0, 0, 0, 1, 1, 2]
PARTS_K = [0, 1, 2, 0, 1, 0]
KPROD = 68
MROW = 96
KALL = MROW + 2
NEG = -float(2 ** 100)
SCALE = HD ** -0.5
VW = HD + 1
UN = H // 2
EPS = 1e-5
LN_EPS = 1e-12


class Step:

    def __init__(self, i, k, period, count):
        self.i, self.k, self.period, self.count = i, k, period, count

    def __add__(self, d):
        return Step(self.i, self.k + d, self.period, self.count)

    def __sub__(self, d):
        return self + (-d)

    def mod(self, m):
        return self.k % m

    def times(self, a, b=0):
        if isinstance(self.i, int):
            return a * (self.period * self.i + self.k) + b
        return self.i * (a * self.period) + (a * self.k + b)

    def over(self, m, a=1, b=0):
        whole = a * (self.k // m) + b
        return whole if isinstance(self.i, int) else self.i * (a * self.period // m) + whole

    @property
    def live(self):
        return not isinstance(self.i, int) or 0 <= self.period * self.i + self.k < self.count


LAG = 5


class Signal:

    def __init__(self, sem, owner, per=1):
        self.sem, self.owner, self.per, self.credit = sem, owner, per, LAG * per

    def after(self, step, k=None):
        k = self.per if k is None else k
        if isinstance(step.i, int) and step.times(1) >= step.count:
            step, k = Step(0, step.count - 1, step.period, step.count), self.per
        value = step.times(self.per, k + self.credit)
        return max(value, 0) if isinstance(value, int) else value


def stand(eng, passed):
    eng.sem_inc(passed, 1)


def open_signals(eng, name, signals):
    for sig in signals:
        if sig.owner == name:
            eng.sem_inc(sig.sem, sig.credit)


def sandwich(nc, x, qkv_w, qkv_b, rq_w, rq_b, rkv_w, rkv_b, rout_w, rout_b, out_w, out_b, gl_w, gr_w,
             W_router, W1, b1, Wo, bo, ln_gamma, ln_beta,
             c_ident, c_maskq, c_maskk, c_valid, c_heads, c_latrow, c_latcol, c_sel, c_third, c_prio, out):
    with ExitStack() as ctx:
        def sb(name, shape, dt=F32):
            return ctx.enter_context(nc.sbuf_tensor(name, shape, dt))

        q_parts = nc.dram_tensor("q_parts", [3, P, T], BF16, kind="Internal").ap()
        k_parts = nc.dram_tensor("k_parts", [3, P, T], BF16, kind="Internal").ap()
        v_tok = nc.dram_tensor("v_tok", [T, H * VW], F32, kind="Internal").ap()
        rq_t = nc.dram_tensor("rq_t", [LD, T], F32, kind="Internal").ap()

        x_dram = x.rearrange("b (t p) d -> p (b t) d", p=P)
        out_dram = out.rearrange("b (t p) d -> p (b t) d", p=P)

        ident = sb("ident", [P, P])
        identb = sb("identb", [P, P], BF16)
        eps_col = sb("eps_col", [P, CT])
        eps12_col = sb("eps12_col", [P, CT])
        mhalf = sb("mhalf", [P, CT])
        X = sb("X", [P, NB, D])
        lat_k = sb("lat_k", [LD, OCT, LH * NLAT])
        lat_v = sb("lat_v", [P, OCT, 2, D])
        tensors = (q_parts, k_parts, v_tok, rq_t)

        project(nc, x_dram, qkv_w, qkv_b, rq_w, rq_b, rkv_w, rkv_b, rout_w, c_ident, c_heads,
                ident, identb, eps_col, eps12_col, mhalf, X, lat_k, lat_v, *tensors)
        attend(nc, rout_b, out_w, out_b, gl_w, gr_w, c_maskq, c_maskk, c_valid, c_latrow, c_latcol,
               ident, identb, eps_col, mhalf, X, lat_k, lat_v, *tensors)
        ffn(nc, W_router, W1, b1, Wo, bo, ln_gamma, ln_beta, c_sel, c_third, c_prio,
            ident, eps_col, eps12_col, mhalf, X, out_dram)


def bcast_rows(ap):
    return ap.partition_broadcast(P)


def project(nc, x_dram, qkv_w, qkv_b, rq_w, rq_b, rkv_w, rkv_b, rout_w, c_ident, c_heads,
            ident, identb, eps_col, eps12_col, mhalf, X, lat_k, lat_v, q_parts, k_parts, v_tok, rq_t):
    with ExitStack() as ctx:
        def sb(name, shape, dt=F32):
            return ctx.enter_context(nc.sbuf_tensor(name, shape, dt))

        def ps(name, shape, dt=F32):
            return ctx.enter_context(nc.psum_tensor(name, shape, dt))

        def sem(name):
            return ctx.enter_context(nc.semaphore(name))

        signals = []

        def signal(name, owner, per=1):
            signals.append(Signal(sem(name), owner, per))
            return signals[-1]

        wqkv = sb("wqkv", [D, 3 * D])
        wrq = sb("wrq", [D, LD])
        wrkv = sb("wrkv", [D, 2 * LD])
        wrout = sb("wrout", [LD, D])
        bq = sb("bq", [P, 1])
        bk = sb("bk", [P, 1])
        bv = sb("bv", [P, D])
        brq = sb("brq", [LD, 1])
        brk = sb("brk", [LD, 1])
        brv = sb("brv", [LD, 1])
        head_rows = sb("head_rows", [LD, LH])

        stats = sb("stats", [P, 2, CT, 6])
        mv = sb("mv", [P, 2, CT, 2])
        var_eps = sb("var_eps", [P, 2, CT])
        rstd = sb("rstd", [P, 2, CT])
        xn = sb("xn", [P, 2, CT, D])
        xnT = sb("xnT", [D, 2, CH])
        split = sb("split", [P, 2, 2, 3, CH], BF16)
        resid = sb("resid", [P, 2, 2, CH])
        vt = sb("vt", [P, 2, CT, H, VW])
        rqs = sb("rqs", [LD, 2, CH])
        pooled = sb("pooled", [D, B * NLAT])
        rkT = sb("rkT", [LD, B * NLAT])
        rvT = sb("rvT", [LD, B * NLAT])
        rv_bd = sb("rv_bd", [LD, B, LH, NLAT])

        psT = [ps(f"psT{u}", [P, CH]) for u in range(2)]
        psQ = ps("psQ", [P, CH])
        psK = ps("psK", [P, CH])
        psV = ps("psV", [P, CH])
        psR = ps("psR", [P, CH])
        psL = ps("psL", [P, CH])

        s_w = sem("s_w")
        s_x = [sem(f"s_x{u}") for u in range(2)]
        s_out = [sem(f"s_out{u}") for u in range(2)]
        s_consts = sem("s_consts")
        s_pass_dve, s_pass_sp = sem("s_pass_dve"), sem("s_pass_sp")
        s_stats = signal("s_stats", "dve", 2 * CT)
        s_rstd = signal("s_rstd", "pool", 2)
        s_xn = signal("s_xn", "dve")
        s_xT = signal("s_xT", "pe")
        s_xTc = signal("s_xTc", "act")
        s_q = signal("s_q", "pe")
        s_k = signal("s_k", "pe")
        s_v = signal("s_v", "pe")
        s_r = signal("s_r", "pe")
        s_hi = signal("s_hi", "act", 2)
        s_res = signal("s_res", "dve", 2)
        s_mid = signal("s_mid", "act", 2)
        s_lo = signal("s_lo", "pool", 2)
        s_vt = signal("s_vt", "dve")
        s_rqs = signal("s_rqs", "act")
        s_pool = signal("s_pool", "dve")
        s_lat = sem("s_lat")
        s_latc = sem("s_latc")

        weights = [
            (wqkv[:], qkv_w), (bq[:], qkv_b[0:D].unsqueeze(1)), (bk[:], qkv_b[D:2 * D].unsqueeze(1)),
            (bv[:], bcast_rows(qkv_b[2 * D:3 * D])), (wrq[:], rq_w), (brq[:], rq_b.unsqueeze(1)),
            (wrkv[:], rkv_w), (brk[:], rkv_b[0:LD].unsqueeze(1)), (brv[:], rkv_b[LD:2 * LD].unsqueeze(1)),
            (wrout[:], rout_w), (ident[:], c_ident), (head_rows[:], c_heads),
        ]
        all_weights = 16 * len(weights)

        def chunk(i, k):
            return Step(i, k, 2, NCH)

        block = ctx.enter_context(nc.Block())

        @block.sync
        def _(sp):
            for u in range(2):
                sp.sem_inc(s_out[u], STORES)

            def load(c):
                u = c.mod(2)
                sp.dma_start(X[:, bass.ds(c.times(CT), CT), :],
                             x_dram[:, bass.ds(c.times(CT), CT), :]).then_inc(s_x[u], 16)

            for k in range(2):
                load(chunk(0, k))
            for dst, src in weights:
                sp.dma_start(dst, src).then_inc(s_w, 16)

            def store(c):
                u = c.mod(2)
                cols = bass.ds(c.times(CH), CH)
                for side, parts in enumerate((q_parts, k_parts)):
                    sp.wait_ge(s_lo.sem, s_lo.after(c, side + 1))
                    sp.dma_start(parts[:, :, cols].rearrange("a p t -> p a t"),
                                 split[:, u, side]).then_inc(s_out[u], 16)
                sp.wait_ge(s_vt.sem, s_vt.after(c))
                sp.dma_start(v_tok[cols, :].rearrange("(t p) n -> p t n", p=P),
                             vt[:, u].rearrange("p t h e -> p t (h e)")).then_inc(s_out[u], 16)
                sp.wait_ge(s_rqs.sem, s_rqs.after(c))
                stand(sp, s_pass_sp)
                sp.dma_start(rq_t[:, cols], rqs[:, u]).then_inc(s_out[u], 16)

            with sp.Fori(0, NCH // 2 - 1) as i:
                for k in range(2):
                    sp.wait_ge(s_stats.sem, s_stats.after(chunk(i, k)))
                    load(chunk(i, k + 2))
                    store(chunk(i, k))
            for k in range(2):
                store(chunk(0, NCH - 2 + k))
            for u in range(2):
                sp.wait_ge(s_out[u], STORES * (1 + NCH // 2))

        @block.vector
        def _(dve):
            open_signals(dve, "dve", signals)
            nc.vector.memset(eps_col[:], EPS).then_inc(s_consts, 1)
            nc.vector.memset(eps12_col[:], LN_EPS).then_inc(s_consts, 1)
            nc.vector.memset(mhalf[:], -0.5).then_inc(s_consts, 1)
            nc.vector.memset(vt[:], 1.0).then_inc(s_consts, 1)
            dve.wait_ge(s_w, all_weights)
            nc.vector.tensor_copy(identb[:], ident[:]).then_inc(s_consts, 1)
            dve.wait_ge(s_consts, 5)

            def norm(c):
                u = c.mod(2)
                dve.wait_ge(s_x[u], c.over(2, 16, 16))
                dve.wait_ge(s_rstd.sem, s_rstd.after(c - 2))
                for t in range(CT):
                    nc.vector.bn_stats(stats[:, u, t, :], X[:, c.times(CT, t), :]).then_inc(s_stats.sem, 1)
                dve.wait_ge(s_stats.sem, s_stats.after(c, CT))
                stand(dve, s_pass_dve)
                for t in range(CT):
                    nc.vector.bn_aggr(mv[:, u, t, :], stats[:, u, t, :]).then_inc(s_stats.sem, 1)
                dve.wait_ge(s_rstd.sem, s_rstd.after(c))
                for t in range(CT):
                    last = nc.vector.tensor_scalar(xn[:, u, t, :], X[:, c.times(CT, t), :], mv[:, u, t, 0:1],
                                                   rstd[:, u, t:t + 1], ALU.subtract, ALU.mult)
                last.then_inc(s_xn.sem, 1)

            def evacuate(c):
                u = c.mod(2)
                for side, (bias, bank, ready) in enumerate(((bq, psQ, s_q), (bk, psK, s_k))):
                    dve.wait_ge(s_hi.sem, s_hi.after(c, side + 1))
                    dve.wait_ge(s_lo.sem, s_lo.after(c - 2, side + 1))
                    nc.vector.scalar_tensor_tensor(out=resid[:, u, side], in0=bank[:], scalar=bias[:, 0:1],
                                                   in1=split[:, u, side, 0], op0=ALU.add,
                                                   op1=ALU.subtract).then_inc(s_res.sem, 1)
                dve.wait_ge(s_v.sem, s_v.after(c))
                dve.wait_ge(s_out[u], c.over(2, STORES, STORES))
                nc.vector.tensor_tensor(
                    vt[:, u, :, :, 0:HD], psV[:].rearrange("p (t h e) -> p t h e", t=CT, h=H),
                    bv[:].rearrange("p (h e) -> p h e", h=H).unsqueeze(1).broadcast_to([P, CT, H, HD]),
                    ALU.add).then_inc(s_vt.sem, 1)
                dve.wait_ge(s_xTc.sem, s_xTc.after(c))
                nc.vector.tensor_reduce(pooled[:, bass.ds(c.times(CH // LCH), CH // LCH)],
                                        xnT[:, u].rearrange("p (l s) -> p l s", s=LCH), AX.X,
                                        ALU.add).then_inc(s_pool.sem, 1)

            norm(chunk(0, 0))
            with dve.Fori(0, NCH // 2 - 1) as i:
                for k in range(2):
                    norm(chunk(i, k + 1))
                    evacuate(chunk(i, k))
            norm(chunk(0, NCH - 1))
            evacuate(chunk(0, NCH - 2))
            evacuate(chunk(0, NCH - 1))

            dve.wait_ge(s_pool.sem, s_pool.credit + NCH)
            nc.vector.tensor_scalar(pooled[:], pooled[:], 1.0 / LCH, None, ALU.mult).then_inc(s_latc, 1)
            dve.wait_ge(s_lat, 2)
            nc.vector.tensor_scalar(rkT[:], psL[0:LD, 0:B * NLAT], brk[:, 0:1], None,
                                    ALU.add).then_inc(s_latc, 1)
            nc.vector.tensor_scalar(rvT[:], psL[0:LD, P:P + B * NLAT], brv[:, 0:1], None,
                                    ALU.add).then_inc(s_latc, 1)
            dve.wait_ge(s_latc, 3)
            rows = head_rows[:].unsqueeze(2).broadcast_to([LD, LH, NLAT])
            for b in range(B):
                lat = slice(b * NLAT, (b + 1) * NLAT)
                for o in range(b * OCT // B, (b + 1) * OCT // B):
                    nc.vector.tensor_tensor(lat_k[:, o].rearrange("r (h l) -> r h l", h=LH), rkT[:, lat].unsqueeze(1).broadcast_to([LD, LH, NLAT]),
                                            rows, ALU.mult).then_inc(s_latc, 1)
                nc.vector.tensor_tensor(rv_bd[:, b], rvT[:, lat].unsqueeze(1).broadcast_to([LD, LH, NLAT]),
                                        rows, ALU.mult).then_inc(s_latc, 1)
            dve.wait_ge(s_lat, 3)
            for o in range(OCT):
                b = o * B // OCT
                nc.vector.tensor_copy(lat_v[:, o], psR[:].rearrange("p (b g d) -> p b g d", b=B, g=2)[:, b])\
                  .then_inc(s_latc, 1)

        @block.gpsimd
        def _(pool):
            open_signals(pool, "pool", signals)
            pool.wait_ge(s_consts, 5)

            def deviations(c):
                u = c.mod(2)
                pool.wait_ge(s_stats.sem, s_stats.after(c))
                pool.wait_ge(s_xn.sem, s_xn.after(c - 2))
                nc.gpsimd.tensor_tensor(var_eps[:, u], mv[:, u, :, 1], eps_col[:], ALU.add).then_inc(s_rstd.sem, 1)
                pool.wait_ge(s_rstd.sem, s_rstd.after(c, 1))
                nc.gpsimd.tensor_tensor(rstd[:, u], var_eps[:, u], mhalf[:], ALU.pow).then_inc(s_rstd.sem, 1)

            def low_parts(c):
                u = c.mod(2)
                for side in range(2):
                    pool.wait_ge(s_mid.sem, s_mid.after(c, side + 1))
                    nc.gpsimd.tensor_tensor(split[:, u, side, 2], resid[:, u, side], split[:, u, side, 1],
                                            ALU.subtract).then_inc(s_lo.sem, 1)

            deviations(chunk(0, 0))
            with pool.Fori(0, NCH // 2 - 1) as i:
                for k in range(2):
                    deviations(chunk(i, k + 1))
                    low_parts(chunk(i, k))
            deviations(chunk(0, NCH - 1))
            low_parts(chunk(0, NCH - 2))
            low_parts(chunk(0, NCH - 1))

        @block.scalar
        def _(act):
            open_signals(act, "act", signals)
            act.wait_ge(s_w, all_weights)

            def transposed(c):
                u = c.mod(2)
                act.wait_ge(s_xT.sem, s_xT.after(c))
                act.wait_ge(s_pool.sem, s_pool.after(c - 2))
                nc.scalar.activation(xnT[:, u], psT[u][:], ACT.Copy).then_inc(s_xTc.sem, 1)

            def evacuate(c):
                u = c.mod(2)
                act.wait_ge(s_out[u], c.over(2, STORES, STORES))
                for side, (bias, bank, ready) in enumerate(((bq, psQ, s_q), (bk, psK, s_k))):
                    act.wait_ge(ready.sem, ready.after(c))
                    nc.scalar.activation(split[:, u, side, 0], bank[:], ACT.Identity,
                                         bias=bias[:, 0:1]).then_inc(s_hi.sem, 1)
                act.wait_ge(s_r.sem, s_r.after(c))
                nc.scalar.activation(rqs[:, u], psR[0:LD, :], ACT.Identity, bias=brq[:, 0:1])\
                  .then_inc(s_rqs.sem, 1)
                for side in range(2):
                    act.wait_ge(s_res.sem, s_res.after(c, side + 1))
                    nc.scalar.activation(split[:, u, side, 1], resid[:, u, side], ACT.Copy)\
                      .then_inc(s_mid.sem, 1)

            transposed(chunk(0, 0))
            with act.Fori(0, NCH // 2 - 1) as i:
                for k in range(2):
                    transposed(chunk(i, k + 1))
                    evacuate(chunk(i, k))
            transposed(chunk(0, NCH - 1))
            evacuate(chunk(0, NCH - 2))
            evacuate(chunk(0, NCH - 1))

        @block.tensor
        def _(pe):
            open_signals(pe, "pe", signals)
            pe.wait_ge(s_w, all_weights)

            def transpose(c):
                u = c.mod(2)
                pe.wait_ge(s_xn.sem, s_xn.after(c))
                pe.wait_ge(s_xTc.sem, s_xTc.after(c - 2))
                for t in range(CT):
                    last = nc.tensor.transpose(psT[u][:, t * P:(t + 1) * P], xn[:, u, t, :], ident[:])
                last.then_inc(s_xT.sem, 1)

            def products(c):
                u = c.mod(2)
                pe.wait_ge(s_xTc.sem, s_xTc.after(c))
                pe.wait_ge(s_res.sem, s_res.after(c - 1, 1))
                nc.tensor.matmul(psQ[:], wqkv[:, 0:D], xnT[:, u], start=True, stop=True).then_inc(s_q.sem, 1)
                pe.wait_ge(s_res.sem, s_res.after(c - 1, 2))
                nc.tensor.matmul(psK[:], wqkv[:, D:2 * D], xnT[:, u], start=True, stop=True).then_inc(s_k.sem, 1)
                pe.wait_ge(s_vt.sem, s_vt.after(c - 1))
                for t in range(CT):
                    last = nc.tensor.matmul(psV[:, t * P:(t + 1) * P], xnT[:, u, t * P:(t + 1) * P],
                                            wqkv[:, 2 * D:3 * D], start=True, stop=True)
                last.then_inc(s_v.sem, 1)
                pe.wait_ge(s_rqs.sem, s_rqs.after(c - 1))
                nc.tensor.matmul(psR[0:LD, :], wrq[:], xnT[:, u], start=True, stop=True).then_inc(s_r.sem, 1)

            transpose(chunk(0, 0))
            with pe.Fori(0, NCH // 2 - 1) as i:
                for k in range(2):
                    transpose(chunk(i, k + 1))
                    products(chunk(i, k))
            transpose(chunk(0, NCH - 1))
            products(chunk(0, NCH - 2))
            products(chunk(0, NCH - 1))

            pe.wait_ge(s_latc, 1)
            nc.tensor.matmul(psL[0:LD, 0:B * NLAT], wrkv[:, 0:LD], pooled[:], start=True,
                             stop=True).then_inc(s_lat, 1)
            nc.tensor.matmul(psL[0:LD, P:P + B * NLAT], wrkv[:, LD:2 * LD], pooled[:], start=True,
                             stop=True).then_inc(s_lat, 1)
            pe.wait_ge(s_latc, 3 + OCT + B)
            pe.wait_ge(s_rqs.sem, s_rqs.credit + NCH)
            for b in range(B):
                for g in range(2):
                    last = nc.tensor.matmul(psR[:, (2 * b + g) * D:(2 * b + g + 1) * D],
                                            rv_bd[:, b, 2 * g:2 * g + 2].rearrange("r h l -> r (h l)"),
                                            wrout[:], start=True, stop=True)
            last.then_inc(s_lat, 1)


def attend(nc, rout_b, out_w, out_b, gl_w, gr_w, c_maskq, c_maskk, c_valid, c_latrow, c_latcol,
           ident, identb, eps_col, mhalf, X, lat_k, lat_v, q_parts, k_parts, v_tok, rq_t):
    with ExitStack() as ctx:
        def sb(name, shape, dt=F32):
            return ctx.enter_context(nc.sbuf_tensor(name, shape, dt))

        def ps(name, shape, dt=F32):
            return ctx.enter_context(nc.psum_tensor(name, shape, dt))

        def sem(name):
            return ctx.enter_context(nc.semaphore(name))

        signals = []

        def signal(name, owner, per=1):
            signals.append(Signal(sem(name), owner, per))
            return signals[-1]

        wout = sb("wout", [D, D])
        bout = sb("bout", [P, D])
        brout = sb("brout", [P, D])
        gl = sb("gl", [P, HD])
        gr = sb("gr", [P, HD])
        maskq_tab = sb("maskq_tab", [P, OCT, 2 * P])
        maskq = sb("maskq", [P, 2 * P])
        maskq0 = sb("maskq0", [P, 2 * P])
        maskk_f = sb("maskk_f", [P, OCT + 1, 2 * P])
        maskk = sb("maskk", [P, OCT + 1, 2 * P], BF16)
        valid = sb("valid", [P, 2, OCT])
        lat_row_f = sb("lat_row_f", [PC, P])
        lat_col_f = sb("lat_col_f", [PC, OCT, LATW])
        lat_row = sb("lat_row", [PC, P], BF16)
        lat_col = sb("lat_col", [PC, OCT, LATW], BF16)

        qst = sb("qst", [P, H, RING * P], BF16)
        kst = sb("kst", [P, H, RING * P], BF16)
        vst = sb("vst", [P, RING, H, VW])
        rqT = sb("rqT", [LD, RING * P])
        added = sb("added", [P, H, 2 * P], BF16)
        rowmax = sb("rowmax", [P, 2, H])
        minus1 = sb("minus1", [P, H])
        mparts = sb("mparts", [P, 2, 2, H], BF16)
        mrest = sb("mrest", [P, H])
        mT = sb("mT", [2 * H, 2, P], BF16)
        probs = sb("probs", [P, UN, 2 * 2 * P])
        pvs = sb("pvs", [P, 2, 4 * P])
        den = sb("den", [P, 2, H])
        rden = sb("rden", [P, 2, H])
        local = sb("local", [P, 2, D])
        lmax = sb("lmax", [P, LH])
        lbias = sb("lbias", [P, 2, LH])
        lexp = sb("lexp", [P, LH, NLAT])
        lsum = sb("lsum", [P, LH])
        lrs = sb("lrs", [P, LH])
        lprob = sb("lprob", [P, LH * NLAT])
        lprobT = sb("lprobT", [P, 2, P])
        remote = sb("remote", [P, 4, D])
        gR = sb("gR", [P, D])
        gL = sb("gL", [P, D])
        gsum = sb("gsum", [P, D])
        z = sb("z", [P, H])
        ez = sb("ez", [P, H])
        ez1 = sb("ez1", [P, H])
        gate = sb("gate", [P, 2, H])
        diff = sb("diff", [P, D])
        gdiff = sb("gdiff", [P, D])
        mixed = sb("mixed", [P, D])
        mixedT = sb("mixedT", [P, P])
        y = sb("y", [P, 2, D])
        ystats = sb("ystats", [P, 6])
        ymv = sb("ymv", [P, 2, 2])
        yve = sb("yve", [P, 1])
        yrstd = sb("yrstd", [P, 1])
        yn = sb("yn", [P, D])

        psS = [ps(f"psS{u}", [P, 2, 2 * P]) for u in range(2)]
        psST = [ps(f"psST{u}", [P, 2, 2 * P]) for u in range(2)]
        psPV = ps("psPV", [P, 4 * P])
        psA = ps("psA", [P, 512])
        psB = ps("psB", [P, 512])
        psC = ps("psC", [P, 512])
        psB_bf = psB[:, 0:P // 2].bitcast(BF16)

        s_w = sem("s_w2")
        s_consts = sem("s_consts2")
        s_pass_dve, s_pass_pe = sem("s_pass_dve2"), sem("s_pass_pe2")
        s_load = [sem(f"s_load{r}") for r in range(RING // LC)]
        s_mrow = [sem(f"s_mrow{u}") for u in range(2)]
        s_fill = sem("s_fill")
        s_dval = sem("s_dval")
        s_lval = sem("s_lval")
        s_S = signal("s_S", "pe", UN)
        s_max = signal("s_max", "dve", UN)
        s_neg = signal("s_neg", "pool", 3)
        s_mT = signal("s_mT", "pe")
        s_mTc = signal("s_mTc", "act")
        s_ST = signal("s_ST", "pe", UN)
        s_exp = signal("s_exp", "act", UN)
        s_pv = signal("s_pv", "pe", 4)
        s_pvs = signal("s_pvs", "act")
        s_pvT = signal("s_pvT", "pe")
        s_den = signal("s_den", "dve", 2)
        s_local = signal("s_local", "dve")
        s_lsc = signal("s_lsc", "pe")
        s_lmax = signal("s_lmax", "dve", 2)
        s_lexp = signal("s_lexp", "act", LH)
        s_lrs = signal("s_lrs", "dve")
        s_lprob = signal("s_lprob", "pool")
        s_lpT = signal("s_lpT", "pe")
        s_lpTc = signal("s_lpTc", "act")
        s_rem = signal("s_rem", "pe")
        s_remote = signal("s_remote", "dve")
        s_gR = signal("s_gR", "pool")
        s_gL = signal("s_gL", "pool", 2)
        s_z = signal("s_z", "dve")
        s_ez = signal("s_ez", "act")
        s_gate = signal("s_gate", "dve", 2)
        s_mix = signal("s_mix", "pool", 3)
        s_mixT = signal("s_mixT", "pe")
        s_mixTc = signal("s_mixTc", "act")
        s_proj = signal("s_proj", "pe")
        s_y = signal("s_y", "dve")
        s_ystats = signal("s_ystats", "dve", 2)
        s_yrstd = signal("s_yrstd", "pool", 2)
        s_x1 = signal("s_x1", "dve", 2)

        weights = [(wout[:], out_w), (bout[:], bcast_rows(out_b)), (brout[:], bcast_rows(rout_b)),
                   (gl[:], bcast_rows(gl_w.rearrange("d o -> (d o)"))),
                   (gr[:], bcast_rows(gr_w.rearrange("d o -> (d o)"))),
                   (maskq_tab[:], c_maskq[:, 1:]), (maskq[:], c_maskq[:, 0]), (maskq0[:], c_maskq[:, 1]),
                   (maskk_f[:], c_maskk), (valid[:], c_valid),
                   (lat_row_f[:], c_latrow), (lat_col_f[:], c_latcol)]
        all_weights = 16 * len(weights)
        CONSTS = 10

        def step(i, k):
            return Step(i, k, RING, NB)

        def ring(n, count=1):
            return slice(n.mod(RING) * P, (n.mod(RING) + count) * P)

        FIRST, LAST = -2, NB + 2
        LOOP = 3

        def schedule(eng, emit):
            for s in range(FIRST, LOOP):
                emit(step(0, s))
            with eng.Fori(0, OCT - 1) as i:
                for k in range(LOOP, LOOP + RING):
                    emit(step(i, k))
            for s in range(LOOP + (OCT - 1) * RING, LAST + 1):
                emit(step(0, s))

        block = ctx.enter_context(nc.Block())

        @block.sync
        def _(sp):
            def load(n):
                sem = s_load[n.mod(RING) // LC]
                src = bass.ds(n.times(P), LC * P)
                dst = ring(n, LC)
                for parts, tile, order in ((q_parts, qst, PARTS_Q), (k_parts, kst, PARTS_K)):
                    for row, part in enumerate(order):
                        sp.dma_start(tile[row * HD:(row + 1) * HD, :, dst],
                                     parts[part, :, src].rearrange("(h d) t -> d h t", d=HD)).then_inc(sem, 16)
                r = n.mod(RING)
                sp.dma_start(vst[:, r:r + LC].rearrange("p t h e -> p t (h e)"),
                             v_tok[src, :].rearrange("(t p) n -> p t n", p=P)).then_inc(sem, 16)
                sp.dma_start(rqT[:, dst], rq_t[:, src]).then_inc(sem, 16)

            sp.wait_ge(s_consts, CONSTS)
            for k in range(0, 6, LC):
                load(step(0, k))

            def emit(s):
                n = s + 5
                if n.mod(LC) == 0 and n.live and (s - 1).live:
                    sp.wait_ge(s_pv.sem, s_pv.after(s - 1))
                    load(n)
                n = s + 1
                if n.live:
                    u = n.mod(2)
                    sp.wait_ge(s_mTc.sem, s_mTc.after(n))
                    for part in range(2):
                        sp.dma_start(qst[MROW + part:MROW + part + 1, :, ring(n)],
                                     mT[part * H:(part + 1) * H, u, :]).then_inc(s_mrow[u], 16)

            schedule(sp, emit)

        @block.tensor
        def _(pe):
            open_signals(pe, "pe", signals)
            pe.wait_ge(s_w, all_weights)
            pe.wait_ge(s_consts, CONSTS)

            def scores(n, g):
                pe.wait_ge(s_max.sem, s_max.after(n, g + 1 - 2))
                bank = psS[g % 2]
                for a in range(2):
                    h = 2 * g + a
                    q = qst[0:KPROD, h, ring(n)]
                    if n.mod(RING):
                        last = nc.tensor.matmul(bank[:, a], q, kst[0:KPROD, h, ring(n - 1, 2)],
                                                start=True, stop=True)
                    else:
                        nc.tensor.matmul(bank[:, a, 0:P], q, kst[0:KPROD, h, ring(n - 1)], start=True, stop=True)
                        last = nc.tensor.matmul(bank[:, a, P:2 * P], q, kst[0:KPROD, h, ring(n)],
                                                start=True, stop=True)
                last.then_inc(s_S.sem, 1)

            def scores_t(n, g):
                pe.wait_ge(s_exp.sem, s_exp.after(n, g + 1 - 2))
                bank = psST[g % 2]
                which = n.over(RING, 1, 1) if n.mod(RING) == 0 else 0
                nc.tensor.matmul(bank[:], identb[:],
                                 maskk[:, which, :].unsqueeze(1).broadcast_to([P, 2, 2 * P]),
                                 start=True, stop=False)
                for a in range(2):
                    h = 2 * g + a
                    for side in range(2):
                        last = nc.tensor.matmul(bank[:, a, side * P:(side + 1) * P],
                                                kst[0:KALL, h, ring(n - 1 + side)], qst[0:KALL, h, ring(n)],
                                                start=False, stop=(a == 1 and side == 1))
                last.then_inc(s_ST.sem, 1)

            def values(n, G):
                pe.wait_ge(s_exp.sem, s_exp.after(n, 2 * G + 2))
                if G == 0:
                    pe.wait_ge(s_pvs.sem, s_pvs.after(n - 1))
                for side in range(2):
                    for t in range(4):
                        unit, a = 2 * G + t // 2, t % 2
                        last = nc.tensor.matmul(
                            psPV[32 * t:32 * t + VW, G * P:(G + 1) * P],
                            vst[:, (n - 1 + side).mod(RING), 4 * G + t, :],
                            probs[:, unit, (2 * a + side) * P:(2 * a + side + 1) * P],
                            start=(side == 0), stop=(side == 1), skip_group_check=True)
                last.then_inc(s_pv.sem, 1)

            def emit(s):
                for g in range(UN):
                    if (s + 2).live:
                        n = s + 2
                        if g == 0 and n.mod(LC) == 0:
                            pe.wait_ge(s_load[n.mod(RING) // LC], n.over(RING, 16 * LOADS, 16 * LOADS))
                        scores(n, g)
                    if s.live:
                        if g == 0:
                            pe.wait_ge(s_mrow[s.mod(2)], s.over(2, 32, 32))
                        scores_t(s, g)
                    if g == 0 and (s - 1).live:
                        n = s - 1
                        pe.wait_ge(s_lpTc.sem, s_lpTc.after(n))
                        for f in range(2):
                            last = nc.tensor.matmul(psA[:, 0:D], lprobT[:, f, :],
                                                    lat_v[:, n.over(RING), f, :],
                                                    start=(f == 0), stop=(f == 1))
                        last.then_inc(s_rem.sem, 1)
                    if g == 1 and (s - 1).live:
                        values(s - 1, 3)
                    if g == 2 and s.live:
                        pe.wait_ge(s_remote.sem, s_remote.after(s - 1))
                        stand(pe, s_pass_pe)
                        nc.tensor.matmul(psA[:, 0:LH * NLAT], rqT[:, ring(s)],
                                         lat_k[:, s.over(RING), :],
                                         start=True, stop=False)
                        first = PC * (RING - 1 - s.mod(RING))
                        window = lat_col[:, s.over(RING), first:first + NLAT]
                        nc.tensor.matmul(psA[:, 0:LH * NLAT], lat_row[:],
                                         window.unsqueeze(1).broadcast_to([PC, LH, NLAT]),
                                         start=False, stop=True).then_inc(s_lsc.sem, 1)
                    if g == 2 and (s - 2).live:
                        n = s - 2
                        pe.wait_ge(s_mix.sem, s_mix.after(n))
                        pe.wait_ge(s_lpTc.sem, s_lpTc.after(n + 1))
                        nc.tensor.transpose(psB[:, 0:P], mixed[:], ident[:]).then_inc(s_mixT.sem, 1)
                    if g == 3 and (s + 1).live:
                        n = s + 1
                        pe.wait_ge(s_neg.sem, s_neg.after(n))
                        pe.wait_ge(s_mixTc.sem, s_mixTc.after(s - 2))
                        pe.wait_ge(s_lpTc.sem, s_lpTc.after(s - 1))
                        nc.tensor.transpose(psB_bf[0:2 * H, :],
                                            mparts[:, n.mod(2)].rearrange("p a h -> p (a h)"),
                                            identb[:]).then_inc(s_mT.sem, 1)
                    if g == 3 and s.live:
                        values(s, 0)
                    if g == 4 and (s - 1).live:
                        n = s - 1
                        pe.wait_ge(s_pvs.sem, s_pvs.after(n))
                        pe.wait_ge(s_y.sem, s_y.after(n - 2))
                        for G in range(4):
                            last = nc.tensor.transpose(psC[:, G * P:(G + 1) * P],
                                                       pvs[:, n.mod(2), G * P:(G + 1) * P], ident[:])
                        last.then_inc(s_pvT.sem, 1)
                    if g == 5 and s.live:
                        values(s, 1)
                    if g == 6 and (s - 2).live:
                        n = s - 2
                        pe.wait_ge(s_mixTc.sem, s_mixTc.after(n))
                        pe.wait_ge(s_local.sem, s_local.after(n + 1))
                        nc.tensor.matmul(psC[:, 0:D], mixedT[:], wout[:], start=True,
                                         stop=True).then_inc(s_proj.sem, 1)
                    if g == 7 and s.live:
                        values(s, 2)
                        pe.wait_ge(s_lprob.sem, s_lprob.after(s))
                        if (s + 1).live:
                            pe.wait_ge(s_mTc.sem, s_mTc.after(s + 1))
                        for f in range(2):
                            last = nc.tensor.transpose(psB[:, f * P:(f + 1) * P], lprob[:, f * P:(f + 1) * P],
                                                       ident[:])
                        last.then_inc(s_lpT.sem, 1)

            schedule(pe, emit)

        @block.vector
        def _(dve):
            open_signals(dve, "dve", signals)
            nc.vector.memset(qst[:], 0.0).then_inc(s_consts, 1)
            nc.vector.memset(kst[:], 0.0).then_inc(s_consts, 1)
            nc.vector.memset(vst[:], 0.0).then_inc(s_consts, 1)
            nc.vector.memset(psPV[:], 0.0).then_inc(s_consts, 1)
            nc.vector.memset(minus1[:], -1.0).then_inc(s_consts, 1)
            dve.wait_ge(s_consts, 5)
            nc.vector.memset(kst[MROW:MROW + 2], 1.0).then_inc(s_consts, 1)
            dve.wait_ge(s_w, all_weights)
            nc.vector.tensor_copy(maskk[:], maskk_f[:]).then_inc(s_consts, 1)
            nc.vector.tensor_copy(lat_row[:], lat_row_f[:]).then_inc(s_consts, 1)
            nc.vector.tensor_copy(lat_col[:], lat_col_f[:]).then_inc(s_consts, 1)
            nc.vector.tensor_scalar(brout[:], brout[:], 0.0, None, ALU.add).then_inc(s_consts, 1)
            dve.wait_ge(s_consts, CONSTS)

            def maxima(n, g):
                dve.wait_ge(s_S.sem, s_S.after(n, g + 1))
                if g == 0:
                    dve.wait_ge(s_neg.sem, s_neg.after(n - 2))
                mask = maskq
                if n.mod(RING) == 0:
                    mask = maskq0
                    if g == 0:
                        dve.wait_ge(s_fill, n.over(RING, 1, 1))
                stand(dve, s_pass_dve)
                for a in range(2):
                    h = 2 * g + a
                    last = nc.vector.tensor_tensor_reduce(added[:, h], psS[g % 2][:, a], mask[:], 1.0, NEG * 4,
                                                          ALU.add, ALU.max, rowmax[:, n.mod(2), h:h + 1])
                last.then_inc(s_max.sem, 1)

            def emit(s):
                for g in range(UN):
                    if (s + 2).live:
                        maxima(s + 2, g)
                    if g == 1 and (s - 1).live:
                        n = s - 1
                        dve.wait_ge(s_rem.sem, s_rem.after(n))
                        dve.wait_ge(s_mix.sem, s_mix.after(n - 4))
                        nc.vector.tensor_tensor(remote[:, n.mod(4)], psA[:, 0:D], brout[:],
                                                ALU.add).then_inc(s_remote.sem, 1)
                    if g == 1 and (s - 3).live:
                        n = s - 3
                        dve.wait_ge(s_yrstd.sem, s_yrstd.after(n))
                        nc.vector.tensor_scalar(yn[:], y[:, n.mod(2)], ymv[:, n.mod(2), 0:1], yrstd[:, 0:1],
                                                ALU.subtract, ALU.mult).then_inc(s_x1.sem, 1)
                    if g == 3 and s.live:
                        dve.wait_ge(s_lsc.sem, s_lsc.after(s))
                        nc.vector.tensor_reduce(lmax[:], psA[:, 0:LH * NLAT].rearrange("p (h l) -> p h l", h=LH),
                                                AX.X, ALU.max).then_inc(s_lmax.sem, 1)
                        dve.wait_ge(s_lmax.sem, s_lmax.after(s, 1))
                        nc.vector.tensor_scalar(lbias[:, s.mod(2)], lmax[:], -SCALE, None,
                                                ALU.mult).then_inc(s_lmax.sem, 1)
                    if g == 2 and (s - 3).live:
                        n = s - 3
                        dve.wait_ge(s_x1.sem, s_x1.after(n, 1))
                        nc.vector.tensor_tensor(X[:, n.times(1), :], X[:, n.times(1), :], yn[:],
                                                ALU.add).then_inc(s_x1.sem, 1)
                    if g == 4 and (s - 1).live:
                        n = s - 1
                        u = n.mod(2)
                        heads = psC[:].rearrange("p (h e) -> p h e", h=H)
                        dve.wait_ge(s_pvT.sem, s_pvT.after(n))
                        nc.vector.tensor_scalar(den[:, u].unsqueeze(2), heads[:, :, HD:HD + 1], 1e-30, None,
                                                ALU.max).then_inc(s_den.sem, 1)
                        dve.wait_ge(s_den.sem, s_den.after(n, 1))
                        nc.vector.reciprocal(rden[:, u], den[:, u]).then_inc(s_den.sem, 1)
                        dve.wait_ge(s_den.sem, s_den.after(n, 2))
                        if n.mod(RING) == 0:
                            nc.vector.tensor_scalar(rden[:, u], rden[:, u],
                                                    valid[:, 0, bass.ds(n.over(RING), 1)],
                                                    None, ALU.mult).then_inc(s_dval, 1)
                            dve.wait_ge(s_dval, n.over(RING, 1, 1))
                        nc.vector.tensor_tensor(local[:, u].rearrange("p (h e) -> p h e", h=H),
                                                heads[:, :, 0:HD],
                                                rden[:, u].unsqueeze(2).broadcast_to([P, H, HD]),
                                                ALU.mult).then_inc(s_local.sem, 1)
                    if g == 5 and s.live:
                        dve.wait_ge(s_lexp.sem, s_lexp.after(s))
                        dve.wait_ge(s_lprob.sem, s_lprob.after(s - 1))
                        nc.vector.reciprocal(lrs[:], lsum[:]).then_inc(s_lrs.sem, 1)
                        if s.mod(RING) == 0:
                            dve.wait_ge(s_lrs.sem, s_lrs.after(s))
                            nc.vector.tensor_scalar(lrs[:], lrs[:], valid[:, 1, bass.ds(s.over(RING), 1)],
                                                    None, ALU.mult).then_inc(s_lval, 1)
                    if g == 6 and (s - 1).live:
                        n = s - 1
                        dve.wait_ge(s_gL.sem, s_gL.after(n))
                        nc.vector.tensor_reduce(z[:], gsum[:].rearrange("p (h e) -> p h e", h=H), AX.X,
                                                ALU.add).then_inc(s_z.sem, 1)
                    if g == 7 and (s - 2).live:
                        n = s - 2
                        u = n.mod(2)
                        dve.wait_ge(s_proj.sem, s_proj.after(n))
                        nc.vector.tensor_tensor(y[:, u], psC[:, 0:D], bout[:], ALU.add).then_inc(s_y.sem, 1)
                        dve.wait_ge(s_y.sem, s_y.after(n))
                        nc.vector.bn_stats(ystats[:], y[:, u]).then_inc(s_ystats.sem, 1)
                        dve.wait_ge(s_ystats.sem, s_ystats.after(n, 1))
                        stand(dve, s_pass_dve)
                        nc.vector.bn_aggr(ymv[:, u], ystats[:]).then_inc(s_ystats.sem, 1)
                    if g == 7 and (s - 1).live:
                        n = s - 1
                        dve.wait_ge(s_ez.sem, s_ez.after(n))
                        nc.vector.tensor_scalar(ez1[:], ez[:], 1.0, None, ALU.add).then_inc(s_gate.sem, 1)
                        dve.wait_ge(s_gate.sem, s_gate.after(n, 1))
                        nc.vector.reciprocal(gate[:, n.mod(2)], ez1[:]).then_inc(s_gate.sem, 1)

            schedule(dve, emit)

        @block.gpsimd
        def _(pool):
            open_signals(pool, "pool", signals)
            pool.wait_ge(s_w, all_weights)
            pool.wait_ge(s_consts, CONSTS)
            pool.sem_inc(s_fill, 1)

            def emit(s):
                if (s - 3).live:
                    n = s - 3
                    pool.wait_ge(s_ystats.sem, s_ystats.after(n))
                    pool.wait_ge(s_x1.sem, s_x1.after(n - 1, 1))
                    nc.gpsimd.tensor_tensor(yve[:], ymv[:, n.mod(2), 1:2], eps_col[:, 0:1],
                                            ALU.add).then_inc(s_yrstd.sem, 1)
                    pool.wait_ge(s_yrstd.sem, s_yrstd.after(n, 1))
                    nc.gpsimd.tensor_tensor(yrstd[:], yve[:], mhalf[:, 0:1], ALU.pow).then_inc(s_yrstd.sem, 1)
                if (s - 2).live:
                    n = s - 2
                    u = n.mod(2)
                    rem = remote[:, n.mod(4)]
                    pool.wait_ge(s_local.sem, s_local.after(n))
                    pool.wait_ge(s_remote.sem, s_remote.after(n))
                    nc.gpsimd.tensor_tensor(diff[:], local[:, u], rem, ALU.subtract).then_inc(s_mix.sem, 1)
                    pool.wait_ge(s_gate.sem, s_gate.after(n))
                    pool.wait_ge(s_mix.sem, s_mix.after(n, 1))
                    nc.gpsimd.tensor_tensor(gdiff[:].rearrange("p (h e) -> p h e", h=H),
                                            diff[:].rearrange("p (h e) -> p h e", h=H),
                                            gate[:, u].unsqueeze(2).broadcast_to([P, H, HD]),
                                            ALU.mult).then_inc(s_mix.sem, 1)
                    pool.wait_ge(s_mix.sem, s_mix.after(n, 2))
                    pool.wait_ge(s_mixT.sem, s_mixT.after(n - 1))
                    nc.gpsimd.tensor_tensor(mixed[:], gdiff[:], rem, ALU.add).then_inc(s_mix.sem, 1)
                if (s + 1).live:
                    n = s + 1
                    u = n.mod(2)
                    pool.wait_ge(s_max.sem, s_max.after(n))
                    pool.wait_ge(s_mT.sem, s_mT.after(n - 2))
                    nc.gpsimd.tensor_tensor(mparts[:, u, 0], rowmax[:, u], minus1[:], ALU.mult)\
                      .then_inc(s_neg.sem, 1)
                    pool.wait_ge(s_neg.sem, s_neg.after(n, 1))
                    nc.gpsimd.tensor_tensor(mrest[:], rowmax[:, u], mparts[:, u, 0], ALU.add).then_inc(s_neg.sem, 1)
                    pool.wait_ge(s_neg.sem, s_neg.after(n, 2))
                    nc.gpsimd.tensor_tensor(mparts[:, u, 1], mrest[:], minus1[:], ALU.mult).then_inc(s_neg.sem, 1)
                if (s + 3).mod(RING) == 0 and (s + 3).live:
                    nc.gpsimd.tensor_copy(maskq0[:], maskq_tab[:, (s + 3).over(RING), :])\
                      .then_inc(s_fill, 1)
                if (s - 1).live:
                    n = s - 1
                    pool.wait_ge(s_remote.sem, s_remote.after(n))
                    nc.gpsimd.tensor_tensor(gR[:].rearrange("p (h e) -> p h e", h=H),
                                            remote[:, n.mod(4)].rearrange("p (h e) -> p h e", h=H),
                                            gr[:].unsqueeze(1).broadcast_to([P, H, HD]),
                                            ALU.mult).then_inc(s_gR.sem, 1)
                    pool.wait_ge(s_local.sem, s_local.after(n))
                    nc.gpsimd.tensor_tensor(gL[:].rearrange("p (h e) -> p h e", h=H),
                                            local[:, n.mod(2)].rearrange("p (h e) -> p h e", h=H),
                                            gl[:].unsqueeze(1).broadcast_to([P, H, HD]),
                                            ALU.mult).then_inc(s_gL.sem, 1)
                    pool.wait_ge(s_gL.sem, s_gL.after(n, 1))
                    pool.wait_ge(s_gR.sem, s_gR.after(n))
                    pool.wait_ge(s_z.sem, s_z.after(n - 1))
                    nc.gpsimd.tensor_tensor(gsum[:], gL[:], gR[:], ALU.add).then_inc(s_gL.sem, 1)
                if s.live:
                    pool.wait_ge(s_lrs.sem, s_lrs.after(s))
                    if s.mod(RING) == 0:
                        pool.wait_ge(s_lval, s.over(RING, 1, 1))
                    pool.wait_ge(s_lpT.sem, s_lpT.after(s - 1))
                    nc.gpsimd.tensor_tensor(lprob[:].rearrange("p (h l) -> p h l", h=LH), lexp[:],
                                            lrs[:].unsqueeze(2).broadcast_to([P, LH, NLAT]),
                                            ALU.mult).then_inc(s_lprob.sem, 1)

            schedule(pool, emit)

        @block.scalar
        def _(act):
            open_signals(act, "act", signals)
            for dst, src in weights:
                act.dma_start(dst, src).then_inc(s_w, 16)

            def emit(s):
                for g in range(UN):
                    if s.live:
                        act.wait_ge(s_ST.sem, s_ST.after(s, g + 1))
                        act.wait_ge(s_pv.sem, s_pv.after(s - 1, g // 2 + 1))
                        nc.scalar.activation(probs[:, g], psST[g % 2][:].rearrange("p a c -> p (a c)"), ACT.Exp,
                                             scale=SCALE).then_inc(s_exp.sem, 1)
                    if g == 2 and (s - 1).live:
                        n = s - 1
                        act.wait_ge(s_pv.sem, s_pv.after(n))
                        act.wait_ge(s_pvT.sem, s_pvT.after(n - 2))
                        nc.scalar.activation(pvs[:, n.mod(2)], psPV[:], ACT.Copy).then_inc(s_pvs.sem, 1)
                    if g == 3 and (s - 2).live:
                        n = s - 2
                        act.wait_ge(s_mixT.sem, s_mixT.after(n))
                        act.wait_ge(s_proj.sem, s_proj.after(n - 1))
                        nc.scalar.activation(mixedT[:], psB[:, 0:P], ACT.Copy).then_inc(s_mixTc.sem, 1)
                    if g == 4 and (s + 1).live:
                        n = s + 1
                        act.wait_ge(s_mT.sem, s_mT.after(n))
                        nc.scalar.activation(mT[:, n.mod(2), :], psB_bf[0:2 * H, :], ACT.Copy)\
                          .then_inc(s_mTc.sem, 1)
                    if g == 4 and s.live:
                        act.wait_ge(s_lmax.sem, s_lmax.after(s))
                        act.wait_ge(s_lprob.sem, s_lprob.after(s - 1))
                        for h in range(LH):
                            nc.scalar.activation(lexp[:, h], psA[:, h * NLAT:(h + 1) * NLAT], ACT.Exp,
                                                 bias=lbias[:, s.mod(2), h:h + 1], scale=SCALE,
                                                 accum_out=lsum[:, h:h + 1]).then_inc(s_lexp.sem, 1)
                    if g == 6 and (s - 1).live:
                        n = s - 1
                        act.wait_ge(s_z.sem, s_z.after(n))
                        act.wait_ge(s_gate.sem, s_gate.after(n - 1, 1))
                        nc.scalar.activation(ez[:], z[:], ACT.Exp, scale=-1.0).then_inc(s_ez.sem, 1)
                    if g == 7 and s.live:
                        act.wait_ge(s_lpT.sem, s_lpT.after(s))
                        act.wait_ge(s_rem.sem, s_rem.after(s - 1))
                        nc.scalar.activation(lprobT[:].rearrange("p f q -> p (f q)"), psB[:, 0:2 * P],
                                             ACT.Copy).then_inc(s_lpTc.sem, 1)

            schedule(act, emit)


def ffn(nc, W_router, W1, b1, Wo, bo, ln_gamma, ln_beta, c_sel, c_third, c_prio,
        ident, eps_col, eps12_col, mhalf, X, out_dram):
    with ExitStack() as ctx:
        def sb(name, shape, dt=F32):
            return ctx.enter_context(nc.sbuf_tensor(name, shape, dt))

        def ps(name, shape, dt=F32):
            return ctx.enter_context(nc.psum_tensor(name, shape, dt))

        def sem(name):
            return ctx.enter_context(nc.semaphore(name))

        signals = []

        def signal(name, owner, per=1):
            signals.append(Signal(sem(name), owner, per))
            return signals[-1]

        wr = sb("wr", [D, E])
        w1 = sb("w1", [D, E, I])
        wo = sb("wo", [P, IT, D])
        b1f = sb("b1f", [3 * E, I])
        b1rest = sb("b1rest", [3 * E, I])
        b1rest2 = sb("b1rest2", [3 * E, I])
        b1hi = sb("b1hi", [3 * E, I], BF16)
        b1mid = sb("b1mid", [3 * E, I], BF16)
        b1p = sb("b1p", [3 * E, I], BF16)
        third = sb("third", [3 * E, 3])
        sel_f = sb("sel_f", [3 * E, E, P])
        sel = sb("sel", [3 * E, E, P], BF16)
        prio = sb("prio", [P, E])
        bob = sb("bob", [P, D])
        gamma = sb("gamma", [P, D])
        beta = sb("beta", [P, D])

        stats = sb("fstats", [P, 3, CT, 6])
        mv1 = sb("mv1", [P, 2, CT, 2])
        mv2 = sb("mv2", [P, 2, CT, 2])
        mv3 = sb("mv3", [P, 2, CT, 2])
        ve = sb("ve", [P, 3, CT])
        rstd1 = sb("rstd1", [P, 2, CT])
        rstd2 = sb("rstd2", [P, 2, CT])
        rstd3 = sb("rstd3", [P, 2, CT])
        xf = sb("xf", [P, 2, CT, D])
        XF = sb("XF", [P, NB, D])
        xfT = sb("xfT", [D, 2, CH])
        lmx = sb("lmx", [P, CT])
        iseq = sb("iseq", [P, CT, E])
        rank = sb("rank", [P, CT, E])
        rmx = sb("rmx", [P, CT])
        onehot = sb("onehot", [P, 2, CT, 3 * E])
        onehotT = sb("onehotT", [3 * E, 2, CH], BF16)
        xe = sb("xe", [D, 2, E, CH])
        hT = sb("hT", [P, 2, IT, CH])
        y0 = sb("y0", [P, CT, D])
        y1 = sb("y1", [P, CT, D])
        y2 = sb("y2", [P, CT, D])
        y3 = sb("y3", [P, CT, D])
        y4 = sb("y4", [P, 2, CT, D])
        y5 = sb("y5", [P, CT, D])
        res = sb("res", [P, 2, CT, D])

        psT = ps("fpsT", [P, CH])
        psR = ps("fpsR", [P, CH])
        psO = ps("fpsO", [P, CH])
        psE = [ps(f"fpsE{u}", [P, CH]) for u in range(2)]
        psH = [ps(f"fpsH{u}", [P, CH]) for u in range(2)]
        psY = ps("fpsY", [P, CH])

        s_w = sem("s_w3")
        s_consts = sem("s_consts3")
        s_pass_dve = sem("s_pass_dve3")
        s_out = [sem(f"s_store{u}") for u in range(2)]
        s_st1 = signal("s_st1", "dve", 2 * CT)
        s_rs1 = signal("s_rs1", "pool", 2)
        s_xf = signal("s_xf", "dve")
        s_xfT = signal("s_xfT", "pe")
        s_xfTc = signal("s_xfTc", "act")
        s_XF = signal("s_XF", "act")
        s_logit = signal("s_logit", "pe")
        s_oh = signal("s_oh", "dve", 5)
        s_ohT = signal("s_ohT", "pe")
        s_ohTc = signal("s_ohTc", "act")
        s_spread = signal("s_spread", "pe", E)
        s_xe = signal("s_xe", "dve", E)
        s_h = signal("s_h", "pe", IT)
        s_gelu = signal("s_gelu", "act", IT)
        s_Y = signal("s_Y", "pe")
        s_y = signal("s_fy", "dve", 2)
        s_st2 = signal("s_st2", "dve", 2 * CT)
        s_rs2 = signal("s_rs2", "pool", 2)
        s_y2 = signal("s_y2", "dve")
        s_aff = signal("s_aff", "pool", 2)
        s_st3 = signal("s_st3", "dve", 2 * CT)
        s_rs3 = signal("s_rs3", "pool", 2)
        s_res = signal("s_fres", "dve", 2)

        weights = [(wr[:], W_router), (w1[:], W1.rearrange("e d i -> d e i")),
                   (wo[:], Wo.rearrange("(j p) d -> p j d", p=P)),
                   (b1f[0:E, :], b1), (b1f[E:2 * E, :], b1), (b1f[2 * E:3 * E, :], b1),
                   (third[:], c_third), (sel_f[:], c_sel), (prio[:], c_prio), (bob[:], bcast_rows(bo)),
                   (gamma[:], bcast_rows(ln_gamma)), (beta[:], bcast_rows(ln_beta))]
        all_weights = 16 * len(weights)
        CONSTS = 9

        def step(i, k):
            return Step(i, k, 2, NCH)

        def schedule(eng, emit):
            for c in range(-2, 2):
                emit(step(0, c))
            with eng.Fori(0, (NCH - 4) // 2) as i:
                for k in range(2, 4):
                    emit(step(i, k))
            for c in range(NCH - 2, NCH + 2):
                emit(step(0, c))

        block = ctx.enter_context(nc.Block())

        @block.sync
        def _(sp):
            for dst, src in weights:
                sp.dma_start(dst, src).then_inc(s_w, 16)

            def emit(c):
                n = c - 2
                if n.live:
                    u = n.mod(2)
                    sp.wait_ge(s_res.sem, s_res.after(n))
                    sp.dma_start(out_dram[:, bass.ds(n.times(CT), CT), :], res[:, u]).then_inc(s_out[u], 16)

            for u in range(2):
                sp.sem_inc(s_out[u], 16)
            schedule(sp, emit)
            for u in range(2):
                sp.wait_ge(s_out[u], 16 + 16 * (NCH // 2))

        @block.tensor
        def _(pe):
            open_signals(pe, "pe", signals)
            pe.wait_ge(s_w, all_weights)
            pe.wait_ge(s_consts, CONSTS)

            def hidden(c, j, e):
                u = c.mod(2)
                if e == 0:
                    pe.wait_ge(s_gelu.sem, s_gelu.after(c, j + 1 - 2))
                pe.wait_ge(s_xe.sem, s_xe.after(c, e + 1))
                nc.tensor.matmul(psH[j % 2][:], w1[:, e, j * P:(j + 1) * P], xe[:, u, e], start=(e == 0),
                                 stop=False)
                if e == E - 1:
                    nc.tensor.matmul(psH[j % 2][:], b1p[:, j * P:(j + 1) * P], onehotT[:, u], start=False,
                                     stop=True).then_inc(s_h.sem, 1)

            def spread(c, e):
                if e == 0:
                    pe.wait_ge(s_ohTc.sem, s_ohTc.after(c))
                pe.wait_ge(s_xe.sem, s_xe.after(c, e + 1 - 2))
                nc.tensor.matmul(psE[e % 2][:], sel[:, e], onehotT[:, c.mod(2)], start=True,
                                 stop=True).then_inc(s_spread.sem, 1)

            def emit(c):
                n = c + 1
                if n.live:
                    u = n.mod(2)
                    pe.wait_ge(s_xf.sem, s_xf.after(n))
                    pe.wait_ge(s_xfTc.sem, s_xfTc.after(n - 1))
                    for t in range(CT):
                        last = nc.tensor.transpose(psT[:, t * P:(t + 1) * P], xf[:, u, t], ident[:])
                    last.then_inc(s_xfT.sem, 1)
                if c.live:
                    for e in range(E):
                        hidden(c, 0, e)
                if n.live:
                    pe.wait_ge(s_xfTc.sem, s_xfTc.after(n))
                    pe.wait_ge(s_oh.sem, s_oh.after(n - 1))
                    for t in range(CT):
                        last = nc.tensor.matmul(psR[:, t * E:(t + 1) * E], xfT[:, u, t * P:(t + 1) * P], wr[:],
                                                start=True, stop=True)
                    last.then_inc(s_logit.sem, 1)
                if (c - 1).live:
                    m = c - 1
                    pe.wait_ge(s_gelu.sem, s_gelu.after(m))
                    pe.wait_ge(s_y.sem, s_y.after(m - 1))
                    for t in range(CT):
                        for j in range(IT):
                            last = nc.tensor.matmul(psY[:, t * P:(t + 1) * P], hT[:, m.mod(2), j, t * P:(t + 1) * P],
                                                    wo[:, j], start=(j == 0), stop=(j == IT - 1))
                    last.then_inc(s_Y.sem, 1)
                if c.live:
                    for e in range(E):
                        hidden(c, 1, e)
                if n.live:
                    pe.wait_ge(s_oh.sem, s_oh.after(n))
                    pe.wait_ge(s_ohTc.sem, s_ohTc.after(n - 1))
                    for t in range(CT):
                        last = nc.tensor.transpose(psO[0:3 * E, t * P:(t + 1) * P], onehot[:, u, t], ident[:])
                    last.then_inc(s_ohT.sem, 1)
                if c.live:
                    for e in range(E):
                        hidden(c, 2, e)
                if n.live:
                    spread(n, 0)
                    spread(n, 1)
                if c.live:
                    hidden(c, 3, 0)
                    hidden(c, 3, 1)
                if n.live:
                    spread(n, 2)
                    spread(n, 3)
                if c.live:
                    hidden(c, 3, 2)
                    hidden(c, 3, 3)

            schedule(pe, emit)

        @block.vector
        def _(dve):
            open_signals(dve, "dve", signals)
            dve.wait_ge(s_w, all_weights)
            nc.vector.tensor_copy(sel[:], sel_f[:]).then_inc(s_consts, 1)
            nc.vector.tensor_copy(b1hi[:], b1f[:]).then_inc(s_consts, 1)
            dve.wait_ge(s_consts, 2)
            nc.vector.tensor_tensor(b1rest[:], b1f[:], b1hi[:], ALU.subtract).then_inc(s_consts, 1)
            dve.wait_ge(s_consts, 3)
            nc.vector.tensor_copy(b1mid[:], b1rest[:]).then_inc(s_consts, 1)
            dve.wait_ge(s_consts, 4)
            nc.vector.tensor_tensor(b1rest2[:], b1rest[:], b1mid[:], ALU.subtract).then_inc(s_consts, 1)
            dve.wait_ge(s_consts, 5)
            nc.vector.tensor_scalar(b1rest2[:], b1rest2[:], third[:, 2:3], None, ALU.mult).then_inc(s_consts, 1)
            dve.wait_ge(s_consts, 6)
            nc.vector.scalar_tensor_tensor(out=b1rest[:], in0=b1mid[:], scalar=third[:, 1:2], in1=b1rest2[:],
                                           op0=ALU.mult, op1=ALU.add).then_inc(s_consts, 1)
            dve.wait_ge(s_consts, 7)
            nc.vector.scalar_tensor_tensor(out=b1f[:], in0=b1hi[:], scalar=third[:, 0:1], in1=b1rest[:],
                                           op0=ALU.mult, op1=ALU.add).then_inc(s_consts, 1)
            dve.wait_ge(s_consts, 8)
            nc.vector.tensor_copy(b1p[:], b1f[:]).then_inc(s_consts, 1)

            def statistics(sig, n, which, source, mv):
                for t in range(CT):
                    nc.vector.bn_stats(stats[:, which, t], source(t)).then_inc(sig.sem, 1)
                dve.wait_ge(sig.sem, sig.after(n, CT))
                stand(dve, s_pass_dve)
                for t in range(CT):
                    nc.vector.bn_aggr(mv[:, n.mod(2), t], stats[:, which, t]).then_inc(sig.sem, 1)

            def emit(c):
                if (c + 1).live:
                    n = c + 1
                    u = n.mod(2)
                    logits = psR[:, 0:CT * E].rearrange("p (t e) -> p t e", e=E)
                    dve.wait_ge(s_logit.sem, s_logit.after(n))
                    nc.vector.tensor_reduce(lmx[:], logits, AX.X, ALU.max).then_inc(s_oh.sem, 1)
                    dve.wait_ge(s_oh.sem, s_oh.after(n, 1))
                    nc.vector.tensor_tensor(iseq[:], logits, lmx[:].unsqueeze(2).broadcast_to([P, CT, E]),
                                            ALU.is_equal).then_inc(s_oh.sem, 1)
                    dve.wait_ge(s_oh.sem, s_oh.after(n, 2))
                    nc.vector.tensor_tensor(rank[:], iseq[:], prio[:].unsqueeze(1).broadcast_to([P, CT, E]),
                                            ALU.mult).then_inc(s_oh.sem, 1)
                    dve.wait_ge(s_oh.sem, s_oh.after(n, 3))
                    nc.vector.tensor_reduce(rmx[:], rank[:], AX.X, ALU.max).then_inc(s_oh.sem, 1)
                    dve.wait_ge(s_oh.sem, s_oh.after(n, 4))
                    nc.vector.tensor_tensor(onehot[:, u].rearrange("p t (a e) -> p t a e", a=3),
                                            rank[:].unsqueeze(2).broadcast_to([P, CT, 3, E]),
                                            rmx[:].unsqueeze(2).unsqueeze(3).broadcast_to([P, CT, 3, E]),
                                            ALU.is_equal).then_inc(s_oh.sem, 1)
                if (c - 1).live:
                    n = c - 1
                    dve.wait_ge(s_Y.sem, s_Y.after(n))
                    nc.vector.tensor_tensor(y0[:], psY[:].rearrange("p (t d) -> p t d", t=CT),
                                            bob[:].unsqueeze(1).broadcast_to([P, CT, D]), ALU.add)\
                      .then_inc(s_y.sem, 1)
                    dve.wait_ge(s_y.sem, s_y.after(n, 1))
                    nc.vector.tensor_tensor(y1[:], y0[:], XF[:, bass.ds(n.times(CT), CT), :], ALU.add)\
                      .then_inc(s_y.sem, 1)
                    dve.wait_ge(s_y.sem, s_y.after(n))
                    statistics(s_st2, n, 1, lambda t: y1[:, t], mv2)
                if (c + 1).live:
                    n = c + 1
                    u = n.mod(2)
                    for e in range(E):
                        dve.wait_ge(s_spread.sem, s_spread.after(n, e + 1))
                        if e == 0:
                            dve.wait_ge(s_h.sem, s_h.after(n - 2))
                        nc.vector.tensor_tensor(xe[:, u, e], psE[e % 2][:], xfT[:, u], ALU.mult)\
                          .then_inc(s_xe.sem, 1)
                if (c - 1).live:
                    n = c - 1
                    dve.wait_ge(s_rs2.sem, s_rs2.after(n))
                    dve.wait_ge(s_aff.sem, s_aff.after(n - 1, 1))
                    for t in range(CT):
                        last = nc.vector.tensor_scalar(y2[:, t], y1[:, t], mv2[:, n.mod(2), t, 0:1],
                                                       rstd2[:, n.mod(2), t:t + 1], ALU.subtract, ALU.mult)
                    last.then_inc(s_y2.sem, 1)
                if (c - 2).live:
                    n = c - 2
                    u = n.mod(2)
                    dve.wait_ge(s_aff.sem, s_aff.after(n))
                    statistics(s_st3, n, 2, lambda t: y4[:, u, t], mv3)
                if (c + 2).live:
                    n = c + 2
                    u = n.mod(2)
                    statistics(s_st1, n, 0, lambda t: X[:, n.times(CT, t), :], mv1)
                    dve.wait_ge(s_rs1.sem, s_rs1.after(n))
                    dve.wait_ge(s_xfT.sem, s_xfT.after(n - 2))
                    dve.wait_ge(s_XF.sem, s_XF.after(n - 2))
                    for t in range(CT):
                        last = nc.vector.tensor_scalar(xf[:, u, t], X[:, n.times(CT, t), :], mv1[:, u, t, 0:1],
                                                       rstd1[:, u, t:t + 1], ALU.subtract, ALU.mult)
                    last.then_inc(s_xf.sem, 1)
                if (c - 2).live:
                    n = c - 2
                    u = n.mod(2)
                    dve.wait_ge(s_rs3.sem, s_rs3.after(n))
                    for t in range(CT):
                        last = nc.vector.tensor_scalar(y5[:, t], y4[:, u, t], mv3[:, u, t, 0:1],
                                                       rstd3[:, u, t:t + 1], ALU.subtract, ALU.mult)
                    last.then_inc(s_res.sem, 1)
                    dve.wait_ge(s_res.sem, s_res.after(n, 1))
                    dve.wait_ge(s_out[u], n.over(2, 16, 16))
                    nc.vector.tensor_tensor(res[:, u], y5[:], X[:, bass.ds(n.times(CT), CT), :], ALU.add)\
                      .then_inc(s_res.sem, 1)

            schedule(dve, emit)

        @block.gpsimd
        def _(pool):
            open_signals(pool, "pool", signals)
            pool.wait_ge(s_w, all_weights)

            def deviations(sig, n, which, mv, eps, rstd):
                u = n.mod(2)
                nc.gpsimd.tensor_tensor(ve[:, which], mv[:, u, :, 1], eps[:], ALU.add).then_inc(sig.sem, 1)
                pool.wait_ge(sig.sem, sig.after(n, 1))
                nc.gpsimd.tensor_tensor(rstd[:, u], ve[:, which], mhalf[:], ALU.pow).then_inc(sig.sem, 1)

            def emit(c):
                if (c - 1).live:
                    n = c - 1
                    pool.wait_ge(s_st2.sem, s_st2.after(n))
                    deviations(s_rs2, n, 1, mv2, eps12_col, rstd2)
                if (c - 2).live:
                    n = c - 2
                    pool.wait_ge(s_st3.sem, s_st3.after(n))
                    deviations(s_rs3, n, 2, mv3, eps_col, rstd3)
                if (c + 2).live:
                    n = c + 2
                    pool.wait_ge(s_st1.sem, s_st1.after(n))
                    deviations(s_rs1, n, 0, mv1, eps_col, rstd1)
                if (c - 1).live:
                    n = c - 1
                    pool.wait_ge(s_y2.sem, s_y2.after(n))
                    nc.gpsimd.tensor_tensor(y3[:], y2[:], gamma[:].unsqueeze(1).broadcast_to([P, CT, D]),
                                            ALU.mult).then_inc(s_aff.sem, 1)
                    pool.wait_ge(s_aff.sem, s_aff.after(n, 1))
                    pool.wait_ge(s_res.sem, s_res.after(n - 2, 1))
                    nc.gpsimd.tensor_tensor(y4[:, n.mod(2)], y3[:], beta[:].unsqueeze(1).broadcast_to([P, CT, D]),
                                            ALU.add).then_inc(s_aff.sem, 1)

            schedule(pool, emit)

        @block.scalar
        def _(act):
            open_signals(act, "act", signals)

            def gelu(c, j):
                act.wait_ge(s_h.sem, s_h.after(c, j + 1))
                if j == 0:
                    act.wait_ge(s_Y.sem, s_Y.after(c - 2))
                nc.scalar.activation(hT[:, c.mod(2), j], psH[j % 2][:], ACT.Gelu).then_inc(s_gelu.sem, 1)

            def emit(c):
                n = c + 1
                if n.live:
                    u = n.mod(2)
                    act.wait_ge(s_xfT.sem, s_xfT.after(n))
                    act.wait_ge(s_xe.sem, s_xe.after(n - 2))
                    nc.scalar.activation(xfT[:, u], psT[:], ACT.Copy).then_inc(s_xfTc.sem, 1)
                    nc.scalar.activation(XF[:, bass.ds(n.times(CT), CT), :], xf[:, u], ACT.Copy)\
                      .then_inc(s_XF.sem, 1)
                if c.live:
                    gelu(c, 0)
                    gelu(c, 1)
                if n.live:
                    act.wait_ge(s_ohT.sem, s_ohT.after(n))
                    act.wait_ge(s_h.sem, s_h.after(n - 2))
                    nc.scalar.activation(onehotT[:, u], psO[0:3 * E, :], ACT.Copy).then_inc(s_ohTc.sem, 1)
                if c.live:
                    gelu(c, 2)
                    gelu(c, 3)

            schedule(act, emit)


_INS = ["x", "qkv_w", "qkv_b", "rq_w", "rq_b", "rkv_w", "rkv_b", "rout_w", "rout_b", "out_w", "out_b", "gl_w",
        "gr_w"]
_FFN = ["W_router", "W1", "b1", "Wo", "bo", "ln_gamma", "ln_beta"]


def constants(np):
    i, j = np.arange(P)[:, None], np.arange(P)[None, :]
    own = np.where(j < i, 0.0, NEG)
    before = np.where((j >= i) & ~((i == 0) & (j == 0)), 0.0, NEG)
    first = np.full((P, P), NEG)
    usual = np.concatenate([before, own], 1)
    opening = np.concatenate([first, own], 1)
    octets = [opening if o % (OCT // B) == 0 else usual for o in range(OCT)]
    flip = lambda m: np.concatenate([m[:, :P].T, m[:, P:].T], 1)
    valid = np.ones((P, 2, OCT))
    for o in range(0, OCT, OCT // B):
        valid[0, 0, o] = 0
        valid[:LCH, 1, o] = 0
    col = np.arange(LATW)[None, None, :] - PC * (RING - 1)
    o, r = np.arange(OCT)[None, :, None], np.arange(PC)[:, None, None]
    latcol = np.where(col < PC * RING * (o % (OCT // B)) + r, 0.0, NEG)
    rows = np.arange(3 * E)
    sel = np.zeros((3 * E, E, P))
    sel[np.arange(E), np.arange(E)] = 1
    return {
        "ident": np.eye(P),
        "maskq": np.stack([usual] + octets, 1),
        "maskk": np.stack([flip(usual)] + [flip(m) for m in octets], 1),
        "valid": valid,
        "heads": (np.arange(LD)[:, None] // LHD == np.arange(LH)[None, :]).astype(float),
        "latrow": (np.arange(P)[None, :] // LCH == np.arange(PC)[:, None]).astype(float),
        "latcol": latcol,
        "sel": sel,
        "third": (rows[:, None] // E == np.arange(3)[None, :]).astype(float),
        "prio": np.tile(np.arange(E, 0, -1.0), (P, 1)),
    }


def kernel(**inputs):
    import numpy as _np
    import concourse.bacc as _bacc
    from concourse.bass_utils import run_bass_kernel_spmd as _run

    nc = _bacc.Bacc("TRN2", target_bir_lowering=False, num_devices=1)
    arrays, args = {}, []
    named = [(f"L0_attn_{n}", inputs[f"L0_attn_{n}"]) for n in _INS]
    named += [(f"L0_ffn_{n}", inputs[f"L0_ffn_{n}"]) for n in _FFN]
    named += [(f"const_{n}", a.astype(_np.float32)) for n, a in constants(_np).items()]
    for name, a in named:
        a = _np.ascontiguousarray(a)
        arrays[f"in_{name}_dram"] = a
        args.append(nc.dram_tensor(f"in_{name}_dram", a.shape, mybir.dt.from_np(a.dtype), kind="ExternalInput").ap())
    args.append(nc.dram_tensor("out_0_dram", (B, S, D), F32, kind="ExternalOutput").ap())
    sandwich(nc, *args)
    r = _run(nc, [arrays], core_ids=[0])
    return r.results[0]["out_0_dram"]
```

```python
from contextlib import ExitStack

import concourse.bass as bass
from concourse import mybir

F32 = mybir.dt.float32
BF16 = mybir.dt.bfloat16
F32R = mybir.dt.float32r
ACT = mybir.ActivationFunctionType
ALU = mybir.AluOpType
AX = mybir.AxisListType

P = 128
B, S, D = 2, 2048, 128
T = B * S
NB = T // P
BB = S // P
H, HD = 16, 8
LH, LHD, LD = 4, 8, 32
NLAT = 64
LCH = S // NLAT
PC = P // LCH
E, I = 4, 512
IT = I // P
CH = 512
NCH = T // CH
CT = CH // P
RING = 8
OCT = NB // RING
LATW = PC * (RING - 1) + NLAT
LC = 2
STORES = 16 * 4
LOADS = 14
PARTS_Q = [0, 0, 0, 1, 1, 2]
PARTS_K = [0, 1, 2, 0, 1, 0]
KPROD = 68
MROW = 96
KALL = MROW + 2
NEG = -float(2 ** 100)
SCALE = HD ** -0.5
VW = HD + 1
UN = H // 2
EPS = 1e-5
LN_EPS = 1e-12


class Step:

    def __init__(self, i, k, period, count):
        self.i, self.k, self.period, self.count = i, k, period, count

    def __add__(self, d):
        return Step(self.i, self.k + d, self.period, self.count)

    def __sub__(self, d):
        return self + (-d)

    def mod(self, m):
        return self.k % m

    def times(self, a, b=0):
        if isinstance(self.i, int):
            return a * (self.period * self.i + self.k) + b
        return self.i * (a * self.period) + (a * self.k + b)

    def over(self, m, a=1, b=0):
        whole = a * (self.k // m) + b
        return whole if isinstance(self.i, int) else self.i * (a * self.period // m) + whole

    @property
    def live(self):
        return not isinstance(self.i, int) or 0 <= self.period * self.i + self.k < self.count


LAG = 5


class Signal:

    def __init__(self, sem, owner, per=1):
        self.sem, self.owner, self.per, self.credit = sem, owner, per, LAG * per

    def after(self, step, k=None):
        k = self.per if k is None else k
        if isinstance(step.i, int) and step.times(1) >= step.count:
            step, k = Step(0, step.count - 1, step.period, step.count), self.per
        value = step.times(self.per, k + self.credit)
        return max(value, 0) if isinstance(value, int) else value


def stand(eng, passed):
    eng.sem_inc(passed, 1)


def open_signals(eng, name, signals):
    for sig in signals:
        if sig.owner == name:
            eng.sem_inc(sig.sem, sig.credit)


class Held:

    def __init__(self, sb, sb_attend):
        self.of_ffn(sb)
        self.of_attend(sb_attend)

    def of_attend(self, sb):
        self.wout = sb("wout", [D, D])
        self.bout = sb("bout", [P, D])
        self.brout = sb("brout", [P, D])
        self.gl = sb("gl", [P, HD])
        self.gr = sb("gr", [P, HD])
        self.maskq_tab = sb("maskq_tab", [P, OCT, 2 * P])
        self.maskq = sb("maskq", [P, 2 * P])
        self.maskq0 = sb("maskq0", [P, 2 * P])
        self.maskk_f = sb("maskk_f", [P, OCT + 1, 2 * P])
        self.maskk = sb("maskk", [P, OCT + 1, 2 * P], BF16)
        self.valid = sb("valid", [P, 2, OCT])
        self.lat_row_f = sb("lat_row_f", [PC, P])
        self.lat_col_f = sb("lat_col_f", [PC, OCT, LATW])
        self.lat_row = sb("lat_row", [PC, P], BF16)
        self.lat_col = sb("lat_col", [PC, OCT, LATW], BF16)
        self.w1 = sb("w1", [D, E, I])
        self.qst = sb("qst", [P, H, RING * P], BF16)
        self.kst = sb("kst", [P, H, RING * P], BF16)
        self.vst = sb("vst", [P, RING, H, VW])
        self.rqT = sb("rqT", [LD, RING * P])
        self.ones = sb("ones", [2 * H, RING * P], BF16)

    def of_ffn(self, sb):
        self.wr = sb("wr", [D, E])
        self.w1hi = sb("w1hi", [D, E, I], F32R)
        self.w1lo = sb("w1lo", [D, E, I], F32R)
        self.wo = sb("wo", [P, IT, D])
        self.b1f = sb("b1f", [3 * E, I])
        self.b1rest = sb("b1rest", [3 * E, I])
        self.b1rest2 = sb("b1rest2", [3 * E, I])
        self.b1hi = sb("b1hi", [3 * E, I], BF16)
        self.b1mid = sb("b1mid", [3 * E, I], BF16)
        self.b1p = sb("b1p", [3 * E, I], BF16)
        self.third = sb("third", [3 * E, 3])
        self.sel_f = sb("sel_f", [3 * E, E, P])
        self.sel = sb("sel", [3 * E, E, P], BF16)
        self.prio = sb("prio", [P, E])
        self.bob = sb("bob", [P, D])
        self.gamma = sb("gamma", [P, D])
        self.beta = sb("beta", [P, D])


def load_parts(sp, n, side, held, scratch, s_load):
    r = n.mod(RING)
    src, dst = bass.ds(n.times(P), LC * P), slice(r * P, (r + LC) * P)
    tile, order = ((held.qst, PARTS_Q), (held.kst, PARTS_K))[side]
    for row, part in enumerate(order):
        sp.dma_start(tile[row * HD:(row + 1) * HD, :, dst],
                     scratch[side][part, :, src].rearrange("(h d) t -> d h t", d=HD)).then_inc(s_load[r // LC], 16)


def load_rest(sp, n, held, scratch, s_load):
    _, _, v_tok, rq_t = scratch
    r = n.mod(RING)
    src, dst = bass.ds(n.times(P), LC * P), slice(r * P, (r + LC) * P)
    sp.dma_start(held.vst[:, r:r + LC].rearrange("p t h e -> p t (h e)"),
                 v_tok[src, :].rearrange("(t p) n -> p t n", p=P)).then_inc(s_load[r // LC], 16)
    sp.dma_start(held.rqT[:, dst], rq_t[:, src]).then_inc(s_load[r // LC], 16)


def sandwich(nc, x, qkv_w, qkv_b, rq_w, rq_b, rkv_w, rkv_b, rout_w, rout_b, out_w, out_b, gl_w, gr_w,
             W_router, W1, b1, Wo, bo, ln_gamma, ln_beta,
             c_ident, c_maskq, c_maskk, c_valid, c_heads, c_latrow, c_latcol, c_sel, c_third, c_prio, out):
    with ExitStack() as ctx:
        def sb(name, shape, dt=F32):
            return ctx.enter_context(nc.sbuf_tensor(name, shape, dt))

        q_parts = nc.dram_tensor("q_parts", [3, P, T], BF16, kind="Internal").ap()
        k_parts = nc.dram_tensor("k_parts", [3, P, T], BF16, kind="Internal").ap()
        v_tok = nc.dram_tensor("v_tok", [T, H * VW], F32, kind="Internal").ap()
        rq_t = nc.dram_tensor("rq_t", [LD, T], F32, kind="Internal").ap()

        x_dram = x.rearrange("b (t p) d -> p (b t) d", p=P)
        out_dram = out.rearrange("b (t p) d -> p (b t) d", p=P)

        ident = sb("ident", [P, P])
        identb = sb("identb", [P, P], BF16)
        eps_col = sb("eps_col", [P, CT])
        eps12_col = sb("eps12_col", [P, CT])
        mhalf = sb("mhalf", [P, CT])
        X = sb("X", [P, NB, D])
        lat_k = sb("lat_k", [LD, OCT, LH * NLAT])
        lat_v = sb("lat_v", [P, OCT, 2, D])
        scratch = (q_parts, k_parts, v_tok, rq_t)
        s_load = [ctx.enter_context(nc.semaphore(f"s_load{r}")) for r in range(RING // LC)]
        until_attend = ctx.enter_context(ExitStack())
        held = Held(sb, lambda name, shape, dt=F32: until_attend.enter_context(nc.sbuf_tensor(name, shape, dt)))
        for_attend = [
            (held.maskk_f[:], c_maskk), (held.lat_row_f[:], c_latrow), (held.lat_col_f[:], c_latcol),
            (held.maskq_tab[:], c_maskq[:, 1:]), (held.maskq[:], c_maskq[:, 0]), (held.maskq0[:], c_maskq[:, 1]),
            (held.valid[:], c_valid), (held.wout[:], out_w), (held.bout[:], bcast_rows(out_b)),
            (held.brout[:], bcast_rows(rout_b)), (held.gl[:], bcast_rows(gl_w.rearrange("d o -> (d o)"))),
            (held.gr[:], bcast_rows(gr_w.rearrange("d o -> (d o)"))),
        ]
        for_ffn = [
            (held.b1f[0:E, :], b1), (held.b1f[E:2 * E, :], b1), (held.b1f[2 * E:3 * E, :], b1),
            (held.third[:], c_third), (held.sel_f[:], c_sel), (held.prio[:], c_prio),
            (held.wr[:], W_router), (held.w1[:], W1.rearrange("e d i -> d e i")),
            (held.wo[:], Wo.rearrange("(j p) d -> p j d", p=P)), (held.bob[:], bcast_rows(bo)),
            (held.gamma[:], bcast_rows(ln_gamma)), (held.beta[:], bcast_rows(ln_beta)),
        ]

        project(nc, x_dram, qkv_w, qkv_b, rq_w, rq_b, rkv_w, rkv_b, rout_w, c_ident, c_heads, for_attend, held,
                ident, identb, eps_col, eps12_col, mhalf, X, lat_k, lat_v, scratch, s_load)
        attend(nc, held, for_ffn, ident, identb, eps_col, mhalf, X, lat_k, lat_v, scratch, s_load)
        until_attend.close()
        ffn(nc, held, ident, eps_col, eps12_col, mhalf, X, out_dram)


def bcast_rows(ap):
    return ap.partition_broadcast(P)


def project(nc, x_dram, qkv_w, qkv_b, rq_w, rq_b, rkv_w, rkv_b, rout_w, c_ident, c_heads, for_attend, held,
            ident, identb, eps_col, eps12_col, mhalf, X, lat_k, lat_v, scratch, s_load):
    with ExitStack() as ctx:
        def sb(name, shape, dt=F32):
            return ctx.enter_context(nc.sbuf_tensor(name, shape, dt))

        def ps(name, shape, dt=F32):
            return ctx.enter_context(nc.psum_tensor(name, shape, dt))

        def sem(name):
            return ctx.enter_context(nc.semaphore(name))

        signals = []

        def signal(name, owner, per=1):
            signals.append(Signal(sem(name), owner, per))
            return signals[-1]

        q_parts, k_parts, v_tok, rq_t = scratch
        wqkv = sb("wqkv", [D, 3 * D])
        wrq = sb("wrq", [D, LD])
        wrkv = sb("wrkv", [D, 2 * LD])
        wrout = sb("wrout", [LD, D])
        bq = sb("bq", [P, 1])
        bk = sb("bk", [P, 1])
        bv = sb("bv", [P, D])
        brq = sb("brq", [LD, 1])
        brk = sb("brk", [LD, 1])
        brv = sb("brv", [LD, 1])
        head_rows = sb("head_rows", [LD, LH])

        warm = sb("warm", [P, CT])
        stats = sb("stats", [P, 2, CT, 6])
        mv = sb("mv", [P, 2, CT, 2])
        var_eps = sb("var_eps", [P, 2, CT])
        rstd = sb("rstd", [P, 2, CT])
        xn = sb("xn", [P, 2, CT, D])
        xnT = sb("xnT", [D, 2, CH])
        split = sb("split", [P, 2, 2, 3, CH], BF16)
        resid = sb("resid", [P, 2, 2, CH])
        vt = sb("vt", [P, 2, CT, H, VW])
        rqs = sb("rqs", [LD, 2, CH])
        pooled = sb("pooled", [D, B * NLAT])
        rkT = sb("rkT", [LD, B * NLAT])
        rvT = sb("rvT", [LD, B * NLAT])
        rv_bd = sb("rv_bd", [LD, B, LH, NLAT])

        psT = [ps(f"psT{u}", [P, CH]) for u in range(2)]
        psQ = ps("psQ", [P, CH])
        psK = ps("psK", [P, CH])
        psV = ps("psV", [P, CH])
        psR = ps("psR", [P, CH])
        psL = ps("psL", [P, CH])

        s_w = sem("s_w")
        s_x = [sem(f"s_x{u}") for u in range(2)]
        s_out = [sem(f"s_out{u}") for u in range(2)]
        s_consts = sem("s_consts")
        s_pass_dve, s_pass_sp = sem("s_pass_dve"), sem("s_pass_sp")
        s_stats = signal("s_stats", "dve", 2 * CT)
        s_rstd = signal("s_rstd", "pool", 2)
        s_xn = signal("s_xn", "dve")
        s_xT = signal("s_xT", "pe")
        s_xTc = signal("s_xTc", "act")
        s_q = signal("s_q", "pe")
        s_k = signal("s_k", "pe")
        s_v = signal("s_v", "pe")
        s_r = signal("s_r", "pe")
        s_hi = signal("s_hi", "act", 2)
        s_res = signal("s_res", "dve", 2)
        s_mid = signal("s_mid", "act", 2)
        s_lo = signal("s_lo", "pool", 2)
        s_vt = signal("s_vt", "dve")
        s_rqs = signal("s_rqs", "act")
        s_pool = signal("s_pool", "dve")
        s_later = sem("s_later")
        s_clear = sem("s_clear")
        s_ones = sem("s_ones")
        s_prep = sem("s_prep")
        s_lat = sem("s_lat")
        s_latc = sem("s_latc")

        weights = [
            (ident[:], c_ident), (wqkv[:], qkv_w), (bq[:], qkv_b[0:D].unsqueeze(1)),
            (bk[:], qkv_b[D:2 * D].unsqueeze(1)), (bv[:], bcast_rows(qkv_b[2 * D:3 * D])), (wrq[:], rq_w),
            (brq[:], rq_b.unsqueeze(1)),
        ]
        later = for_attend + [
            (wrkv[:], rkv_w), (brk[:], rkv_b[0:LD].unsqueeze(1)), (brv[:], rkv_b[LD:2 * LD].unsqueeze(1)),
            (wrout[:], rout_w), (head_rows[:], c_heads),
        ]
        all_weights = 16 * len(weights)
        CLEARED = ((0, 5), (5, 9), (9, H))

        def chunk(i, k):
            return Step(i, k, 2, NCH)

        def schedule(eng, emit):
            for c in range(-2, 0):
                emit(chunk(0, c))
            with eng.Fori(0, (NCH - 4) // 2) as i:
                for k in range(2):
                    emit(chunk(i, k))
            for c in range(NCH - 4, NCH):
                emit(chunk(0, c))

        def clear(eng, first, last):
            for tile in (held.qst, held.kst):
                eng.memset(tile[:, first:last, :].bitcast(F32), 0.0).then_inc(s_clear, 1)

        block = ctx.enter_context(nc.Block())

        @block.sync
        def _(sp):
            for u in range(2):
                sp.sem_inc(s_out[u], STORES)

            def load(c):
                u = c.mod(2)
                sp.dma_start(X[:, bass.ds(c.times(CT), CT), :],
                             x_dram[:, bass.ds(c.times(CT), CT), :]).then_inc(s_x[u], 16)

            for k in range(2):
                load(chunk(0, k))

            def store(c):
                u = c.mod(2)
                cols = bass.ds(c.times(CH), CH)
                for side, parts in enumerate((q_parts, k_parts)):
                    sp.wait_ge(s_lo.sem, s_lo.after(c, side + 1))
                    sp.dma_start(parts[:, :, cols].rearrange("a p t -> p a t"),
                                 split[:, u, side]).then_inc(s_out[u], 16)
                sp.wait_ge(s_vt.sem, s_vt.after(c))
                sp.dma_start(v_tok[cols, :].rearrange("(t p) n -> p t n", p=P),
                             vt[:, u].rearrange("p t h e -> p t (h e)")).then_inc(s_out[u], 16)
                sp.wait_ge(s_rqs.sem, s_rqs.after(c))
                stand(sp, s_pass_sp)
                sp.dma_start(rq_t[:, cols], rqs[:, u]).then_inc(s_out[u], 16)

            def emit(c):
                if (c + 4).live:
                    sp.wait_ge(s_stats.sem, s_stats.after(c + 2))
                    load(c + 4)
                if isinstance(c.i, int) and c.k < 0:
                    for dst, src in later[c.k + 2::2]:
                        sp.dma_start(dst, src).then_inc(s_later, 16)
                if c.live:
                    store(c)
                if isinstance(c.i, int) and c.k >= NCH - 4:
                    first_blocks(c.k - NCH + 4)

            def first_blocks(k):
                if k == 0:
                    sp.wait_ge(s_clear, 2 * len(CLEARED) + 2)
                    sp.dma_start(held.kst[MROW:MROW + 2], held.ones[:]).then_inc(s_ones, 16)
                    for u in range(2):
                        sp.wait_ge(s_out[u], STORES * 2)
                if k % 2 == 0:
                    load_parts(sp, Step(0, LC * (k // 2), RING, NB), 0, held, scratch, s_load)
                else:
                    load_parts(sp, Step(0, LC * (k // 2), RING, NB), 1, held, scratch, s_load)
                    load_rest(sp, Step(0, LC * (k // 2), RING, NB), held, scratch, s_load)

            schedule(sp, emit)
            sp.wait_ge(s_ones, 16)
            for u in range(2):
                sp.wait_ge(s_out[u], STORES * (1 + NCH // 2))

        @block.vector
        def _(dve):
            open_signals(dve, "dve", signals)
            nc.vector.memset(eps_col[:], EPS).then_inc(s_consts, 1)
            nc.vector.memset(eps12_col[:], LN_EPS).then_inc(s_consts, 1)
            nc.vector.memset(mhalf[:], -0.5).then_inc(s_consts, 1)
            nc.vector.memset(vt[:], 1.0).then_inc(s_consts, 1)
            clear(nc.vector, *CLEARED[0])
            dve.wait_ge(s_consts, 4)

            def statistics(c):
                u = c.mod(2)
                dve.wait_ge(s_x[u], c.over(2, 16, 16))
                dve.wait_ge(s_rstd.sem, s_rstd.after(c - 2))
                for t in range(CT):
                    nc.vector.bn_stats(stats[:, u, t, :], X[:, c.times(CT, t), :]).then_inc(s_stats.sem, 1)
                dve.wait_ge(s_stats.sem, s_stats.after(c, CT))
                stand(dve, s_pass_dve)
                for t in range(CT):
                    nc.vector.bn_aggr(mv[:, u, t, :], stats[:, u, t, :]).then_inc(s_stats.sem, 1)

            def norm(c):
                u = c.mod(2)
                dve.wait_ge(s_rstd.sem, s_rstd.after(c))
                dve.wait_ge(s_xT.sem, s_xT.after(c - 2))
                for t in range(CT):
                    last = nc.vector.tensor_scalar(xn[:, u, t, :], X[:, c.times(CT, t), :], mv[:, u, t, 0:1],
                                                   rstd[:, u, t:t + 1], ALU.subtract, ALU.mult)
                last.then_inc(s_xn.sem, 1)

            def evacuate(c):
                u = c.mod(2)
                for side, (bias, bank, ready) in enumerate(((bq, psQ, s_q), (bk, psK, s_k))):
                    dve.wait_ge(s_hi.sem, s_hi.after(c, side + 1))
                    dve.wait_ge(s_lo.sem, s_lo.after(c - 2, side + 1))
                    nc.vector.scalar_tensor_tensor(out=resid[:, u, side], in0=bank[:], scalar=bias[:, 0:1],
                                                   in1=split[:, u, side, 0], op0=ALU.add,
                                                   op1=ALU.subtract).then_inc(s_res.sem, 1)
                dve.wait_ge(s_v.sem, s_v.after(c))
                dve.wait_ge(s_out[u], c.over(2, STORES, STORES))
                nc.vector.tensor_tensor(
                    vt[:, u, :, :, 0:HD], psV[:].rearrange("p (t h e) -> p t h e", t=CT, h=H),
                    bv[:].rearrange("p (h e) -> p h e", h=H).unsqueeze(1).broadcast_to([P, CT, H, HD]),
                    ALU.add).then_inc(s_vt.sem, 1)
                dve.wait_ge(s_xTc.sem, s_xTc.after(c))
                nc.vector.tensor_reduce(pooled[:, bass.ds(c.times(CH // LCH), CH // LCH)],
                                        xnT[:, u].rearrange("p (l s) -> p l s", s=LCH), AX.X,
                                        ALU.add).then_inc(s_pool.sem, 1)

            def emit(c):
                if (c + 2).live:
                    statistics(c + 2)
                if isinstance(c.i, int) and c.k == 0:
                    dve.wait_ge(s_w, all_weights)
                if c.live:
                    evacuate(c)
                if (c + 2).live:
                    norm(c + 2)

            schedule(dve, emit)

            nc.vector.tensor_copy(identb[:], ident[:]).then_inc(s_consts, 1)
            dve.wait_ge(s_pool.sem, s_pool.credit + NCH)
            nc.vector.tensor_scalar(pooled[:], pooled[:], 1.0 / LCH, None, ALU.mult).then_inc(s_latc, 1)
            dve.wait_ge(s_later, 16 * len(later))
            dve.wait_ge(s_lat, 2)
            nc.vector.tensor_scalar(rkT[:], psL[0:LD, 0:B * NLAT], brk[:, 0:1], None,
                                    ALU.add).then_inc(s_latc, 1)
            nc.vector.tensor_scalar(rvT[:], psL[0:LD, P:P + B * NLAT], brv[:, 0:1], None,
                                    ALU.add).then_inc(s_latc, 1)
            dve.wait_ge(s_latc, 3)
            rows = head_rows[:].unsqueeze(2).broadcast_to([LD, LH, NLAT])

            def per_head(tile, b):
                return tile[:, b * NLAT:(b + 1) * NLAT].unsqueeze(1).broadcast_to([LD, LH, NLAT])

            for b in range(B):
                nc.vector.tensor_tensor(rv_bd[:, b], per_head(rvT, b), rows, ALU.mult).then_inc(s_latc, 1)
            for o in range(OCT):
                nc.vector.tensor_tensor(lat_k[:, o].rearrange("r (h l) -> r h l", h=LH),
                                        per_head(rkT, o * B // OCT), rows, ALU.mult).then_inc(s_latc, 1)
            dve.wait_ge(s_lat, 3)
            for o in range(OCT):
                b = o * B // OCT
                nc.vector.tensor_copy(lat_v[:, o], psR[:].rearrange("p (b g d) -> p b g d", b=B, g=2)[:, b])\
                  .then_inc(s_latc, 1)

        @block.gpsimd
        def _(pool):
            open_signals(pool, "pool", signals)
            pool.wait_ge(s_consts, 4)

            def deviations(c):
                u = c.mod(2)
                pool.wait_ge(s_stats.sem, s_stats.after(c))
                pool.wait_ge(s_xn.sem, s_xn.after(c - 2))
                nc.gpsimd.tensor_tensor(var_eps[:, u], mv[:, u, :, 1], eps_col[:], ALU.add).then_inc(s_rstd.sem, 1)
                pool.wait_ge(s_rstd.sem, s_rstd.after(c, 1))
                nc.gpsimd.tensor_tensor(rstd[:, u], var_eps[:, u], mhalf[:], ALU.pow).then_inc(s_rstd.sem, 1)

            def low_parts(c):
                u = c.mod(2)
                for side in range(2):
                    pool.wait_ge(s_mid.sem, s_mid.after(c, side + 1))
                    nc.gpsimd.tensor_tensor(split[:, u, side, 2], resid[:, u, side], split[:, u, side, 1],
                                            ALU.subtract).then_inc(s_lo.sem, 1)

            clear(nc.gpsimd, *CLEARED[1])

            def emit(c):
                if (c + 2).live:
                    deviations(c + 2)
                if c.live:
                    low_parts(c)
                if isinstance(c.i, int) and c.k == -1:
                    clear(nc.gpsimd, *CLEARED[2])
                    nc.gpsimd.memset(held.vst[:, RING - 1], 0.0).then_inc(s_clear, 1)
                    nc.gpsimd.memset(held.ones[:], 1.0).then_inc(s_clear, 1)

            schedule(pool, emit)

        @block.scalar
        def _(act):
            open_signals(act, "act", signals)
            for dst, src in weights:
                act.dma_start(dst, src).then_inc(s_w, 16)
            act.wait_ge(s_consts, 3)
            nc.scalar.activation(warm[:], eps_col[:], ACT.Copy)
            act.wait_ge(s_w, all_weights)

            def transposed(c):
                u = c.mod(2)
                act.wait_ge(s_xT.sem, s_xT.after(c))
                act.wait_ge(s_pool.sem, s_pool.after(c - 2))
                nc.scalar.activation(xnT[:, u], psT[u][:], ACT.Copy).then_inc(s_xTc.sem, 1)

            def high_parts(c):
                u = c.mod(2)
                act.wait_ge(s_out[u], c.over(2, STORES, STORES))
                for side, (bias, bank, ready) in enumerate(((bq, psQ, s_q), (bk, psK, s_k))):
                    act.wait_ge(ready.sem, ready.after(c))
                    nc.scalar.activation(split[:, u, side, 0], bank[:], ACT.Identity,
                                         bias=bias[:, 0:1]).then_inc(s_hi.sem, 1)

            def evacuate(c):
                u = c.mod(2)
                act.wait_ge(s_r.sem, s_r.after(c))
                nc.scalar.activation(rqs[:, u], psR[0:LD, :], ACT.Identity, bias=brq[:, 0:1])\
                  .then_inc(s_rqs.sem, 1)
                for side in range(2):
                    act.wait_ge(s_res.sem, s_res.after(c, side + 1))
                    nc.scalar.activation(split[:, u, side, 1], resid[:, u, side], ACT.Copy)\
                      .then_inc(s_mid.sem, 1)

            def emit(c):
                if c.live:
                    high_parts(c)
                if (c + 1).live:
                    transposed(c + 1)
                if c.live:
                    evacuate(c)

            schedule(act, emit)

            act.wait_ge(s_later, 16 * len(later))
            for dst, src in ((held.maskk, held.maskk_f), (held.lat_row, held.lat_row_f),
                             (held.lat_col, held.lat_col_f)):
                nc.scalar.activation(dst[:], src[:], ACT.Copy).then_inc(s_prep, 1)

        @block.tensor
        def _(pe):
            open_signals(pe, "pe", signals)
            pe.wait_ge(s_w, all_weights)

            def transpose(c):
                u = c.mod(2)
                pe.wait_ge(s_xn.sem, s_xn.after(c))
                pe.wait_ge(s_xTc.sem, s_xTc.after(c - 2))
                for t in range(CT):
                    last = nc.tensor.transpose(psT[u][:, t * P:(t + 1) * P], xn[:, u, t, :], ident[:])
                last.then_inc(s_xT.sem, 1)

            def products(c):
                u = c.mod(2)
                pe.wait_ge(s_xTc.sem, s_xTc.after(c))
                pe.wait_ge(s_res.sem, s_res.after(c - 1, 1))
                nc.tensor.matmul(psQ[:], wqkv[:, 0:D], xnT[:, u], start=True, stop=True).then_inc(s_q.sem, 1)
                pe.wait_ge(s_res.sem, s_res.after(c - 1, 2))
                nc.tensor.matmul(psK[:], wqkv[:, D:2 * D], xnT[:, u], start=True, stop=True).then_inc(s_k.sem, 1)

            def more_products(c):
                u = c.mod(2)
                pe.wait_ge(s_vt.sem, s_vt.after(c - 1))
                for t in range(CT):
                    last = nc.tensor.matmul(psV[:, t * P:(t + 1) * P], xnT[:, u, t * P:(t + 1) * P],
                                            wqkv[:, 2 * D:3 * D], start=True, stop=True)
                last.then_inc(s_v.sem, 1)
                pe.wait_ge(s_rqs.sem, s_rqs.after(c - 1))
                nc.tensor.matmul(psR[0:LD, :], wrq[:], xnT[:, u], start=True, stop=True).then_inc(s_r.sem, 1)

            def emit(c):
                if c.live:
                    products(c)
                if (c + 1).live:
                    transpose(c + 1)
                if c.live:
                    more_products(c)

            schedule(pe, emit)

            pe.wait_ge(s_later, 16 * len(later))
            pe.wait_ge(s_latc, 1)
            nc.tensor.matmul(psL[0:LD, 0:B * NLAT], wrkv[:, 0:LD], pooled[:], start=True,
                             stop=True).then_inc(s_lat, 1)
            nc.tensor.matmul(psL[0:LD, P:P + B * NLAT], wrkv[:, LD:2 * LD], pooled[:], start=True,
                             stop=True).then_inc(s_lat, 1)
            pe.wait_ge(s_latc, 3 + B)
            pe.wait_ge(s_rqs.sem, s_rqs.credit + NCH)
            for b in range(B):
                for g in range(2):
                    last = nc.tensor.matmul(psR[:, (2 * b + g) * D:(2 * b + g + 1) * D],
                                            rv_bd[:, b, 2 * g:2 * g + 2].rearrange("r h l -> r (h l)"),
                                            wrout[:], start=True, stop=True)
            last.then_inc(s_lat, 1)


def attend(nc, held, for_ffn, ident, identb, eps_col, mhalf, X, lat_k, lat_v, scratch, s_load):
    with ExitStack() as ctx:
        def sb(name, shape, dt=F32):
            return ctx.enter_context(nc.sbuf_tensor(name, shape, dt))

        def ps(name, shape, dt=F32):
            return ctx.enter_context(nc.psum_tensor(name, shape, dt))

        def sem(name):
            return ctx.enter_context(nc.semaphore(name))

        signals = []

        def signal(name, owner, per=1):
            signals.append(Signal(sem(name), owner, per))
            return signals[-1]

        wout, bout, brout, gl, gr = held.wout, held.bout, held.brout, held.gl, held.gr
        maskq_tab, maskq, maskq0, maskk, valid = held.maskq_tab, held.maskq, held.maskq0, held.maskk, held.valid
        lat_row, lat_col = held.lat_row, held.lat_col
        qst, kst, vst, rqT = held.qst, held.kst, held.vst, held.rqT

        added = sb("added", [P, H, 2 * P], BF16)
        rowmax = sb("rowmax", [P, 2, H])
        minus1 = sb("minus1", [P, H])
        mparts = sb("mparts", [P, 2, 2, H], BF16)
        mrest = sb("mrest", [P, H])
        mT = sb("mT", [2 * H, 2, P], BF16)
        probs = sb("probs", [P, UN, 2 * 2 * P])
        pvs = sb("pvs", [P, 2, 4 * P])
        den = sb("den", [P, 2, H])
        rden = sb("rden", [P, 2, H])
        local = sb("local", [P, 2, D])
        lmax = sb("lmax", [P, LH])
        lbias = sb("lbias", [P, 2, LH])
        lexp = sb("lexp", [P, LH, NLAT])
        lsum = sb("lsum", [P, LH])
        lrs = sb("lrs", [P, LH])
        lprob = sb("lprob", [P, LH * NLAT])
        lprobT = sb("lprobT", [P, 2, P])
        remote = sb("remote", [P, 4, D])
        gR = sb("gR", [P, D])
        gL = sb("gL", [P, D])
        gsum = sb("gsum", [P, D])
        z = sb("z", [P, H])
        ez = sb("ez", [P, H])
        ez1 = sb("ez1", [P, H])
        gate = sb("gate", [P, 2, H])
        diff = sb("diff", [P, D])
        gdiff = sb("gdiff", [P, D])
        mixed = sb("mixed", [P, D])
        mixedT = sb("mixedT", [P, P])
        y = sb("y", [P, 2, D])
        ystats = sb("ystats", [P, 6])
        ymv = sb("ymv", [P, 2, 2])
        yve = sb("yve", [P, 1])
        yrstd = sb("yrstd", [P, 1])
        yn = sb("yn", [P, D])

        psS = [ps(f"psS{u}", [P, 2, 2 * P]) for u in range(2)]
        psST = [ps(f"psST{u}", [P, 2, 2 * P]) for u in range(2)]
        psPV = ps("psPV", [P, 4 * P])
        psA = ps("psA", [P, 512])
        psB = ps("psB", [P, 512])
        psC = ps("psC", [P, 512])
        psLS = psA[:, 0:LH * NLAT]
        psRem = psC[:, 0:D]
        psLP = psB[:, 0:2 * P]
        psMix = psB[:, 2 * P:3 * P]
        psM = psB[0:2 * H, 3 * P:3 * P + P // 2].bitcast(BF16)

        s_consts = sem("s_consts2")
        s_pass_dve, s_pass_pe = sem("s_pass_dve2"), sem("s_pass_pe2")
        s_mrow = [sem(f"s_mrow{u}") for u in range(2)]
        s_b1 = sem("s_b1")
        s_w1hi = sem("s_w1hi")
        s_ffn = sem("s_ffn")
        s_fill = sem("s_fill")
        s_dval = sem("s_dval")
        s_lval = sem("s_lval")
        s_S = signal("s_S", "pe", UN)
        s_max = signal("s_max", "dve", UN)
        s_neg = signal("s_neg", "pool", 3)
        s_mT = signal("s_mT", "pe")
        s_mTc = signal("s_mTc", "act")
        s_ST = signal("s_ST", "pe", UN)
        s_exp = signal("s_exp", "act", UN)
        s_pv = signal("s_pv", "pe", 4)
        s_pvs = signal("s_pvs", "act")
        s_pvT = signal("s_pvT", "pe")
        s_den = signal("s_den", "dve", 2)
        s_local = signal("s_local", "dve")
        s_lsc = signal("s_lsc", "pe")
        s_lmax = signal("s_lmax", "dve", 2)
        s_lexp = signal("s_lexp", "act", LH)
        s_lrs = signal("s_lrs", "dve")
        s_lprob = signal("s_lprob", "pool")
        s_lpT = signal("s_lpT", "pe")
        s_lpTc = signal("s_lpTc", "act")
        s_rem = signal("s_rem", "pe")
        s_remote = signal("s_remote", "dve")
        s_gR = signal("s_gR", "pool")
        s_gL = signal("s_gL", "pool", 2)
        s_z = signal("s_z", "dve")
        s_ez = signal("s_ez", "act")
        s_gate = signal("s_gate", "dve", 2)
        s_mix = signal("s_mix", "pool", 3)
        s_mixT = signal("s_mixT", "pe")
        s_mixTc = signal("s_mixTc", "act")
        s_proj = signal("s_proj", "pe")
        s_y = signal("s_y", "dve")
        s_ystats = signal("s_ystats", "dve", 2)
        s_yrstd = signal("s_yrstd", "pool", 2)
        s_x1 = signal("s_x1", "dve", 2)

        CONSTS = 2

        def step(i, k):
            return Step(i, k, RING, NB)

        def ring(n, count=1):
            return slice(n.mod(RING) * P, (n.mod(RING) + count) * P)

        FIRST, LAST = -2, NB + 2
        LOOP = 3
        W1_FROM = LOOP + (OCT - 1) * RING
        B1_FROM = LOOP + (OCT - 1) * RING

        def schedule(eng, emit):
            for s in range(FIRST, LOOP):
                emit(step(0, s))
            with eng.Fori(0, OCT - 1) as i:
                for k in range(LOOP, LOOP + RING):
                    emit(step(i, k))
            for s in range(LOOP + (OCT - 1) * RING, LAST + 1):
                emit(step(0, s))

        block = ctx.enter_context(nc.Block())

        @block.sync
        def _(sp):
            third = step(0, 2 * LC)
            load_parts(sp, third, 0, held, scratch, s_load)
            load_parts(sp, third, 1, held, scratch, s_load)
            load_rest(sp, third, held, scratch, s_load)

            def emit(s):
                n = s + 1
                if n.live:
                    sp.wait_ge(s_mTc.sem, s_mTc.after(n))
                    sp.dma_start(qst[MROW:MROW + 2, :, ring(n)], mT[:, n.mod(2), :])\
                      .then_inc(s_mrow[n.mod(2)], 16)
                if isinstance(s.i, int) and 0 <= s.k < LOOP:
                    for dst, src in for_ffn[s.k::LOOP]:
                        sp.dma_start(dst, src).then_inc(s_ffn, 16)
                n = s + 5
                if n.mod(LC) == 0 and n.live and (s - 1).live:
                    sp.wait_ge(s_pv.sem, s_pv.after(s - 1))
                    load_parts(sp, n, 0, held, scratch, s_load)
                    load_parts(sp, n, 1, held, scratch, s_load)
                    load_rest(sp, n, held, scratch, s_load)

            schedule(sp, emit)

        @block.tensor
        def _(pe):
            open_signals(pe, "pe", signals)
            pe.wait_ge(s_consts, CONSTS)

            def scores(n, g):
                pe.wait_ge(s_max.sem, s_max.after(n, g + 1 - 2))
                bank = psS[g % 2]
                for a in range(2):
                    h = 2 * g + a
                    q = qst[0:KPROD, h, ring(n)]
                    if n.mod(RING):
                        last = nc.tensor.matmul(bank[:, a], q, kst[0:KPROD, h, ring(n - 1, 2)],
                                                start=True, stop=True)
                    else:
                        nc.tensor.matmul(bank[:, a, 0:P], q, kst[0:KPROD, h, ring(n - 1)], start=True, stop=True)
                        last = nc.tensor.matmul(bank[:, a, P:2 * P], q, kst[0:KPROD, h, ring(n)],
                                                start=True, stop=True)
                last.then_inc(s_S.sem, 1)

            def scores_t(n, g):
                pe.wait_ge(s_exp.sem, s_exp.after(n, g + 1 - 2))
                bank = psST[g % 2]
                which = n.over(RING, 1, 1) if n.mod(RING) == 0 else 0
                nc.tensor.matmul(bank[:], identb[:],
                                 maskk[:, which, :].unsqueeze(1).broadcast_to([P, 2, 2 * P]),
                                 start=True, stop=False)
                for a in range(2):
                    h = 2 * g + a
                    for side in range(2):
                        last = nc.tensor.matmul(bank[:, a, side * P:(side + 1) * P],
                                                kst[0:KALL, h, ring(n - 1 + side)], qst[0:KALL, h, ring(n)],
                                                start=False, stop=(a == 1 and side == 1))
                last.then_inc(s_ST.sem, 1)

            def values(n, G):
                pe.wait_ge(s_exp.sem, s_exp.after(n, 2 * G + 2))
                if G == 0:
                    pe.wait_ge(s_pvs.sem, s_pvs.after(n - 1))
                for side in range(2):
                    for t in range(4):
                        unit, a = 2 * G + t // 2, t % 2
                        last = nc.tensor.matmul(
                            psPV[32 * t:32 * t + VW, G * P:(G + 1) * P],
                            vst[:, (n - 1 + side).mod(RING), 4 * G + t, :],
                            probs[:, unit, (2 * a + side) * P:(2 * a + side + 1) * P],
                            start=(side == 0), stop=(side == 1), skip_group_check=True)
                last.then_inc(s_pv.sem, 1)

            def emit(s):
                for g in range(UN):
                    if (s + 2).live:
                        n = s + 2
                        if g == 0 and n.mod(LC) == 0:
                            pe.wait_ge(s_load[n.mod(RING) // LC], n.over(RING, 16 * LOADS, 16 * LOADS))
                        scores(n, g)
                    if s.live:
                        if g == 0:
                            pe.wait_ge(s_mrow[s.mod(2)], s.over(2, 16, 16))
                        scores_t(s, g)
                    if g == 0 and (s - 1).live:
                        n = s - 1
                        pe.wait_ge(s_lprob.sem, s_lprob.after(n))
                        pe.wait_ge(s_mixTc.sem, s_mixTc.after(n - 2))
                        for f in range(2):
                            last = nc.tensor.transpose(psLP[:, f * P:(f + 1) * P],
                                                       lprob[:, f * P:(f + 1) * P], ident[:])
                        last.then_inc(s_lpT.sem, 1)
                    if g == 1 and (s - 1).live:
                        values(s - 1, 3)
                    if g == 2 and (s + 1).live:
                        n = s + 1
                        pe.wait_ge(s_neg.sem, s_neg.after(n))
                        pe.wait_ge(s_lpTc.sem, s_lpTc.after(s - 1))
                        nc.tensor.transpose(psM, mparts[:, n.mod(2)].rearrange("p a h -> p (a h)"),
                                            identb[:]).then_inc(s_mT.sem, 1)
                    if g == 2 and (s - 1).live:
                        n = s - 1
                        pe.wait_ge(s_lpTc.sem, s_lpTc.after(n))
                        pe.wait_ge(s_y.sem, s_y.after(n - 2))
                        for f in range(2):
                            last = nc.tensor.matmul(psRem, lprobT[:, f, :],
                                                    lat_v[:, n.over(RING), f, :],
                                                    start=(f == 0), stop=(f == 1))
                        last.then_inc(s_rem.sem, 1)
                    if g == 2 and s.live:
                        pe.wait_ge(s_lexp.sem, s_lexp.after(s - 1))
                        stand(pe, s_pass_pe)
                        nc.tensor.matmul(psLS, rqT[:, ring(s)], lat_k[:, s.over(RING), :],
                                         start=True, stop=False)
                        first = PC * (RING - 1 - s.mod(RING))
                        window = lat_col[:, s.over(RING), first:first + NLAT]
                        nc.tensor.matmul(psLS, lat_row[:],
                                         window.unsqueeze(1).broadcast_to([PC, LH, NLAT]),
                                         start=False, stop=True).then_inc(s_lsc.sem, 1)
                    if g == 3 and s.live:
                        values(s, 0)
                    if g == 3 and (s - 2).live:
                        n = s - 2
                        pe.wait_ge(s_mix.sem, s_mix.after(n))
                        if (s + 1).live:
                            pe.wait_ge(s_mTc.sem, s_mTc.after(s + 1))
                        nc.tensor.transpose(psMix, mixed[:], ident[:]).then_inc(s_mixT.sem, 1)
                    if g == 4 and (s - 1).live:
                        n = s - 1
                        pe.wait_ge(s_pvs.sem, s_pvs.after(n))
                        pe.wait_ge(s_remote.sem, s_remote.after(n))
                        for G in range(4):
                            last = nc.tensor.transpose(psC[:, G * P:(G + 1) * P],
                                                       pvs[:, n.mod(2), G * P:(G + 1) * P], ident[:])
                        last.then_inc(s_pvT.sem, 1)
                    if g == 5 and s.live:
                        values(s, 1)
                    if g == 6 and (s - 2).live:
                        n = s - 2
                        pe.wait_ge(s_mixTc.sem, s_mixTc.after(n))
                        pe.wait_ge(s_local.sem, s_local.after(n + 1))
                        nc.tensor.matmul(psC[:, 0:D], mixedT[:], wout[:], start=True,
                                         stop=True).then_inc(s_proj.sem, 1)
                    if g == 7 and s.live:
                        values(s, 2)

            schedule(pe, emit)

        @block.vector
        def _(dve):
            open_signals(dve, "dve", signals)
            nc.vector.memset(psPV[:], 0.0).then_inc(s_consts, 1)
            nc.vector.memset(minus1[:], -1.0).then_inc(s_consts, 1)
            dve.wait_ge(s_consts, CONSTS)

            def maxima(n, g):
                dve.wait_ge(s_S.sem, s_S.after(n, g + 1))
                if g == 0:
                    dve.wait_ge(s_neg.sem, s_neg.after(n - 2))
                mask = maskq
                if n.mod(RING) == 0:
                    mask = maskq0
                    if g == 0:
                        dve.wait_ge(s_fill, n.over(RING, 1, 1))
                stand(dve, s_pass_dve)
                for a in range(2):
                    h = 2 * g + a
                    last = nc.vector.tensor_tensor_reduce(added[:, h], psS[g % 2][:, a], mask[:], 1.0, NEG * 4,
                                                          ALU.add, ALU.max, rowmax[:, n.mod(2), h:h + 1])
                last.then_inc(s_max.sem, 1)

            def emit(s):
                for g in range(UN):
                    if (s + 2).live:
                        maxima(s + 2, g)
                    if g == 0 and (s - 2).live:
                        n = s - 2
                        dve.wait_ge(s_ez.sem, s_ez.after(n))
                        nc.vector.tensor_scalar(ez1[:], ez[:], 1.0, None, ALU.add).then_inc(s_gate.sem, 1)
                        dve.wait_ge(s_gate.sem, s_gate.after(n, 1))
                        nc.vector.reciprocal(gate[:, n.mod(2)], ez1[:]).then_inc(s_gate.sem, 1)
                    if g == 3 and (s - 1).live:
                        n = s - 1
                        dve.wait_ge(s_rem.sem, s_rem.after(n))
                        dve.wait_ge(s_mix.sem, s_mix.after(n - 4))
                        nc.vector.tensor_tensor(remote[:, n.mod(4)], psRem, brout[:],
                                                ALU.add).then_inc(s_remote.sem, 1)
                    if g == 1 and (s - 3).live:
                        n = s - 3
                        dve.wait_ge(s_yrstd.sem, s_yrstd.after(n))
                        nc.vector.tensor_scalar(yn[:], y[:, n.mod(2)], ymv[:, n.mod(2), 0:1], yrstd[:, 0:1],
                                                ALU.subtract, ALU.mult).then_inc(s_x1.sem, 1)
                    if g == 3 and s.live:
                        dve.wait_ge(s_lsc.sem, s_lsc.after(s))
                        nc.vector.tensor_reduce(lmax[:], psLS.rearrange("p (h l) -> p h l", h=LH),
                                                AX.X, ALU.max).then_inc(s_lmax.sem, 1)
                        dve.wait_ge(s_lmax.sem, s_lmax.after(s, 1))
                        nc.vector.tensor_scalar(lbias[:, s.mod(2)], lmax[:], -SCALE, None,
                                                ALU.mult).then_inc(s_lmax.sem, 1)
                    if g == 2 and (s - 3).live:
                        n = s - 3
                        dve.wait_ge(s_x1.sem, s_x1.after(n, 1))
                        nc.vector.tensor_tensor(X[:, n.times(1), :], X[:, n.times(1), :], yn[:],
                                                ALU.add).then_inc(s_x1.sem, 1)
                    if g == 4 and (s - 1).live:
                        n = s - 1
                        u = n.mod(2)
                        heads = psC[:].rearrange("p (h e) -> p h e", h=H)
                        dve.wait_ge(s_pvT.sem, s_pvT.after(n))
                        nc.vector.tensor_scalar(den[:, u].unsqueeze(2), heads[:, :, HD:HD + 1], 1e-30, None,
                                                ALU.max).then_inc(s_den.sem, 1)
                        dve.wait_ge(s_den.sem, s_den.after(n, 1))
                        nc.vector.reciprocal(rden[:, u], den[:, u]).then_inc(s_den.sem, 1)
                        dve.wait_ge(s_den.sem, s_den.after(n, 2))
                        if n.mod(RING) == 0:
                            nc.vector.tensor_scalar(rden[:, u], rden[:, u],
                                                    valid[:, 0, bass.ds(n.over(RING), 1)],
                                                    None, ALU.mult).then_inc(s_dval, 1)
                            dve.wait_ge(s_dval, n.over(RING, 1, 1))
                        nc.vector.tensor_tensor(local[:, u].rearrange("p (h e) -> p h e", h=H),
                                                heads[:, :, 0:HD],
                                                rden[:, u].unsqueeze(2).broadcast_to([P, H, HD]),
                                                ALU.mult).then_inc(s_local.sem, 1)
                    if g == 6 and s.live:
                        dve.wait_ge(s_lexp.sem, s_lexp.after(s))
                        dve.wait_ge(s_lprob.sem, s_lprob.after(s - 1))
                        nc.vector.reciprocal(lrs[:], lsum[:]).then_inc(s_lrs.sem, 1)
                        if s.mod(RING) == 0:
                            dve.wait_ge(s_lrs.sem, s_lrs.after(s))
                            nc.vector.tensor_scalar(lrs[:], lrs[:], valid[:, 1, bass.ds(s.over(RING), 1)],
                                                    None, ALU.mult).then_inc(s_lval, 1)
                    if g == 6 and (s - 1).live:
                        n = s - 1
                        dve.wait_ge(s_gL.sem, s_gL.after(n))
                        nc.vector.tensor_reduce(z[:], gsum[:].rearrange("p (h e) -> p h e", h=H), AX.X,
                                                ALU.add).then_inc(s_z.sem, 1)
                    if g == 5 and isinstance(s.i, int) and 0 < s.k - W1_FROM <= E:
                        e = s.k - W1_FROM - 1
                        dve.wait_ge(s_w1hi, e + 1)
                        nc.vector.tensor_tensor(held.w1lo[:, e], held.w1[:, e], held.w1hi[:, e].bitcast(F32),
                                                ALU.subtract)
                    if g == 7 and (s - 2).live:
                        n = s - 2
                        u = n.mod(2)
                        dve.wait_ge(s_proj.sem, s_proj.after(n))
                        nc.vector.tensor_tensor(y[:, u], psC[:, 0:D], bout[:], ALU.add).then_inc(s_y.sem, 1)
                        dve.wait_ge(s_y.sem, s_y.after(n))
                        nc.vector.bn_stats(ystats[:], y[:, u]).then_inc(s_ystats.sem, 1)
                        dve.wait_ge(s_ystats.sem, s_ystats.after(n, 1))
                        stand(dve, s_pass_dve)
                        nc.vector.bn_aggr(ymv[:, u], ystats[:]).then_inc(s_ystats.sem, 1)

            schedule(dve, emit)

        @block.gpsimd
        def _(pool):
            open_signals(pool, "pool", signals)
            pool.wait_ge(s_consts, CONSTS)
            pool.sem_inc(s_fill, 1)

            b1f, b1hi, b1mid, b1rest, b1rest2 = held.b1f, held.b1hi, held.b1mid, held.b1rest, held.b1rest2

            def b1_parts(k):
                if k > 0:
                    pool.wait_ge(s_b1, k if k < 7 else 8)
                part = min(max(k - 4, 0), 2)
                third = held.third[:, part:part + 1].broadcast_to([3 * E, I])
                if k == 0:
                    pool.wait_ge(s_ffn, 16 * len(for_ffn))
                    nc.gpsimd.tensor_copy(held.sel[:], held.sel_f[:])
                    done = nc.gpsimd.tensor_copy(b1hi[:], b1f[:])
                elif k == 1:
                    done = nc.gpsimd.tensor_tensor(b1rest[:], b1f[:], b1hi[:], ALU.subtract)
                elif k == 2:
                    done = nc.gpsimd.tensor_copy(b1mid[:], b1rest[:])
                elif k == 3:
                    done = nc.gpsimd.tensor_tensor(b1rest2[:], b1rest[:], b1mid[:], ALU.subtract)
                elif k == 4:
                    done = nc.gpsimd.tensor_tensor(b1f[:], b1hi[:], third, ALU.mult)
                elif k == 5:
                    done = nc.gpsimd.tensor_tensor(b1rest[:], b1mid[:], third, ALU.mult)
                elif k == 6:
                    nc.gpsimd.tensor_tensor(b1hi[:], b1rest2[:], third, ALU.mult).then_inc(s_b1, 1)
                    pool.wait_ge(s_b1, 7)
                    done = nc.gpsimd.tensor_tensor(b1mid[:], b1rest[:], b1hi[:], ALU.add)
                else:
                    done = nc.gpsimd.tensor_tensor(held.b1p[:], b1f[:], b1mid[:], ALU.add)
                done.then_inc(s_b1, 1)

            def emit(s):
                if (s + 1).live:
                    n = s + 1
                    u = n.mod(2)
                    pool.wait_ge(s_max.sem, s_max.after(n))
                    pool.wait_ge(s_mT.sem, s_mT.after(n - 2))
                    nc.gpsimd.tensor_tensor(mparts[:, u, 0], rowmax[:, u], minus1[:], ALU.mult)\
                      .then_inc(s_neg.sem, 1)
                    pool.wait_ge(s_neg.sem, s_neg.after(n, 1))
                    nc.gpsimd.tensor_tensor(mrest[:], rowmax[:, u], mparts[:, u, 0], ALU.add).then_inc(s_neg.sem, 1)
                    pool.wait_ge(s_neg.sem, s_neg.after(n, 2))
                    nc.gpsimd.tensor_tensor(mparts[:, u, 1], mrest[:], minus1[:], ALU.mult).then_inc(s_neg.sem, 1)
                if (s - 3).live:
                    n = s - 3
                    pool.wait_ge(s_ystats.sem, s_ystats.after(n))
                    pool.wait_ge(s_x1.sem, s_x1.after(n - 1, 1))
                    nc.gpsimd.tensor_tensor(yve[:], ymv[:, n.mod(2), 1:2], eps_col[:, 0:1],
                                            ALU.add).then_inc(s_yrstd.sem, 1)
                    pool.wait_ge(s_yrstd.sem, s_yrstd.after(n, 1))
                    nc.gpsimd.tensor_tensor(yrstd[:], yve[:], mhalf[:, 0:1], ALU.pow).then_inc(s_yrstd.sem, 1)
                if (s - 2).live:
                    n = s - 2
                    u = n.mod(2)
                    rem = remote[:, n.mod(4)]
                    pool.wait_ge(s_local.sem, s_local.after(n))
                    pool.wait_ge(s_remote.sem, s_remote.after(n))
                    nc.gpsimd.tensor_tensor(diff[:], local[:, u], rem, ALU.subtract).then_inc(s_mix.sem, 1)
                    pool.wait_ge(s_gate.sem, s_gate.after(n))
                    pool.wait_ge(s_mix.sem, s_mix.after(n, 1))
                    nc.gpsimd.tensor_tensor(gdiff[:].rearrange("p (h e) -> p h e", h=H),
                                            diff[:].rearrange("p (h e) -> p h e", h=H),
                                            gate[:, u].unsqueeze(2).broadcast_to([P, H, HD]),
                                            ALU.mult).then_inc(s_mix.sem, 1)
                    pool.wait_ge(s_mix.sem, s_mix.after(n, 2))
                    pool.wait_ge(s_mixT.sem, s_mixT.after(n - 1))
                    nc.gpsimd.tensor_tensor(mixed[:], gdiff[:], rem, ALU.add).then_inc(s_mix.sem, 1)
                if (s + 3).mod(RING) == 0 and (s + 3).live:
                    nc.gpsimd.tensor_copy(maskq0[:], maskq_tab[:, (s + 3).over(RING), :])\
                      .then_inc(s_fill, 1)
                if (s - 1).live:
                    n = s - 1
                    pool.wait_ge(s_remote.sem, s_remote.after(n))
                    nc.gpsimd.tensor_tensor(gR[:].rearrange("p (h e) -> p h e", h=H),
                                            remote[:, n.mod(4)].rearrange("p (h e) -> p h e", h=H),
                                            gr[:].unsqueeze(1).broadcast_to([P, H, HD]),
                                            ALU.mult).then_inc(s_gR.sem, 1)
                    pool.wait_ge(s_local.sem, s_local.after(n))
                    nc.gpsimd.tensor_tensor(gL[:].rearrange("p (h e) -> p h e", h=H),
                                            local[:, n.mod(2)].rearrange("p (h e) -> p h e", h=H),
                                            gl[:].unsqueeze(1).broadcast_to([P, H, HD]),
                                            ALU.mult).then_inc(s_gL.sem, 1)
                    pool.wait_ge(s_gL.sem, s_gL.after(n, 1))
                    pool.wait_ge(s_gR.sem, s_gR.after(n))
                    pool.wait_ge(s_z.sem, s_z.after(n - 1))
                    nc.gpsimd.tensor_tensor(gsum[:], gL[:], gR[:], ALU.add).then_inc(s_gL.sem, 1)
                if isinstance(s.i, int) and 0 <= s.k - B1_FROM < 8:
                    b1_parts(s.k - B1_FROM)
                if s.live:
                    pool.wait_ge(s_lrs.sem, s_lrs.after(s))
                    if s.mod(RING) == 0:
                        pool.wait_ge(s_lval, s.over(RING, 1, 1))
                    pool.wait_ge(s_lpT.sem, s_lpT.after(s - 1))
                    nc.gpsimd.tensor_tensor(lprob[:].rearrange("p (h l) -> p h l", h=LH), lexp[:],
                                            lrs[:].unsqueeze(2).broadcast_to([P, LH, NLAT]),
                                            ALU.mult).then_inc(s_lprob.sem, 1)

            schedule(pool, emit)

        @block.scalar
        def _(act):
            open_signals(act, "act", signals)
            def emit(s):
                for g in range(UN):
                    if s.live:
                        act.wait_ge(s_ST.sem, s_ST.after(s, g + 1))
                        act.wait_ge(s_pv.sem, s_pv.after(s - 1, g // 2 + 1))
                        nc.scalar.activation(probs[:, g], psST[g % 2][:].rearrange("p a c -> p (a c)"), ACT.Exp,
                                             scale=SCALE).then_inc(s_exp.sem, 1)
                    if g == 0 and (s - 1).live:
                        n = s - 1
                        act.wait_ge(s_lpT.sem, s_lpT.after(n))
                        act.wait_ge(s_rem.sem, s_rem.after(n - 1))
                        nc.scalar.activation(lprobT[:].rearrange("p f q -> p (f q)"), psLP,
                                             ACT.Copy).then_inc(s_lpTc.sem, 1)
                    if g == 2 and (s + 1).live:
                        n = s + 1
                        act.wait_ge(s_mT.sem, s_mT.after(n))
                        nc.scalar.activation(mT[:, n.mod(2), :], psM, ACT.Copy).then_inc(s_mTc.sem, 1)
                    if g == 2 and (s - 1).live:
                        n = s - 1
                        act.wait_ge(s_pv.sem, s_pv.after(n))
                        act.wait_ge(s_pvT.sem, s_pvT.after(n - 2))
                        nc.scalar.activation(pvs[:, n.mod(2)], psPV[:], ACT.Copy).then_inc(s_pvs.sem, 1)
                    if g == 4 and (s - 2).live:
                        n = s - 2
                        act.wait_ge(s_mixT.sem, s_mixT.after(n))
                        act.wait_ge(s_proj.sem, s_proj.after(n - 1))
                        nc.scalar.activation(mixedT[:], psMix, ACT.Copy).then_inc(s_mixTc.sem, 1)
                    if g == 3 and isinstance(s.i, int) and 0 <= s.k - W1_FROM < E:
                        if s.k == W1_FROM:
                            act.wait_ge(s_ffn, 16 * len(for_ffn))
                        e = s.k - W1_FROM
                        nc.scalar.activation(held.w1hi[:, e], held.w1[:, e], ACT.Copy).then_inc(s_w1hi, 1)
                    if g in (4, 5) and s.live:
                        if g == 4:
                            act.wait_ge(s_lmax.sem, s_lmax.after(s))
                            act.wait_ge(s_lprob.sem, s_lprob.after(s - 1))
                        for h in range(2 * (g - 4), 2 * (g - 4) + 2):
                            nc.scalar.activation(lexp[:, h], psLS[:, h * NLAT:(h + 1) * NLAT], ACT.Exp,
                                                 bias=lbias[:, s.mod(2), h:h + 1], scale=SCALE,
                                                 accum_out=lsum[:, h:h + 1]).then_inc(s_lexp.sem, 1)
                    if g == 7 and (s - 1).live:
                        n = s - 1
                        act.wait_ge(s_z.sem, s_z.after(n))
                        act.wait_ge(s_gate.sem, s_gate.after(n - 1, 1))
                        nc.scalar.activation(ez[:], z[:], ACT.Exp, scale=-1.0).then_inc(s_ez.sem, 1)

            schedule(act, emit)


def ffn(nc, held, ident, eps_col, eps12_col, mhalf, X, out_dram):
    with ExitStack() as ctx:
        def sb(name, shape, dt=F32):
            return ctx.enter_context(nc.sbuf_tensor(name, shape, dt))

        def ps(name, shape, dt=F32):
            return ctx.enter_context(nc.psum_tensor(name, shape, dt))

        def sem(name):
            return ctx.enter_context(nc.semaphore(name))

        signals = []

        def signal(name, owner, per=1):
            signals.append(Signal(sem(name), owner, per))
            return signals[-1]

        wr, wo, b1p, sel, prio = held.wr, held.wo, held.b1p, held.sel, held.prio
        w1hi, w1lo = held.w1hi, held.w1lo
        bob, gamma, beta = held.bob, held.gamma, held.beta

        stats = sb("fstats", [P, 3, CT, 6])
        mv1 = sb("mv1", [P, 2, CT, 2])
        mv2 = sb("mv2", [P, 2, CT, 2])
        mv3 = sb("mv3", [P, 2, CT, 2])
        ve = sb("ve", [P, 3, CT])
        rstd1 = sb("rstd1", [P, 2, CT])
        rstd2 = sb("rstd2", [P, 2, CT])
        rstd3 = sb("rstd3", [P, 2, CT])
        xf = sb("xf", [P, 2, CT, D])
        XF = sb("XF", [P, 2, CT, D])
        xfT = sb("xfT", [D, 2, CH])
        xfThi = sb("xfThi", [D, 2, CH], F32R)
        xfTlo = sb("xfTlo", [D, 2, CH], F32R)
        lmx = sb("lmx", [P, CT])
        iseq = sb("iseq", [P, CT, E])
        rank = sb("rank", [P, CT, E])
        rmx = sb("rmx", [P, CT])
        onehot = sb("onehot", [P, 2, CT, 3 * E])
        onehotT = sb("onehotT", [3 * E, 2, CH], BF16)
        xehi = sb("xehi", [D, 2, E, CH], F32R)
        xelo = sb("xelo", [D, 2, E, CH], F32R)
        hT = sb("hT", [P, 2, IT, CH])
        y1 = sb("y1", [P, CT, D])
        y2 = sb("y2", [P, CT, D])
        y3 = sb("y3", [P, CT, D])
        y4 = sb("y4", [P, 2, CT, D])
        y5 = sb("y5", [P, CT, D])
        res = sb("res", [P, 2, CT, D])

        psT = ps("fpsT", [P, CH])
        psR = ps("fpsR", [P, CH])
        psO = ps("fpsO", [P, CH])
        psE = [ps(f"fpsE{u}", [P, CH]) for u in range(2)]
        psH = [ps(f"fpsH{u}", [P, CH]) for u in range(2)]
        psY = ps("fpsY", [P, CH])

        s_pass_dve = sem("s_pass_dve3")
        s_out = [sem(f"s_store{u}") for u in range(2)]
        s_st1 = signal("s_st1", "dve", 2 * CT)
        s_rs1 = signal("s_rs1", "pool", 2)
        s_xf = signal("s_xf", "dve")
        s_xfT = signal("s_xfT", "pe")
        s_xfTc = signal("s_xfTc", "act")
        s_xfThi = signal("s_xfThi", "act")
        s_xfTlo = signal("s_xfTlo", "dve")
        s_XF = signal("s_XF", "pool")
        s_logit = signal("s_logit", "pe")
        s_oh = signal("s_oh", "dve", 5)
        s_ohT = signal("s_ohT", "pe")
        s_ohTc = signal("s_ohTc", "act")
        s_spread = signal("s_spread", "pe", E)
        s_xe = signal("s_xe", "dve", E)
        s_h = signal("s_h", "pe", IT)
        s_gelu = signal("s_gelu", "act", IT)
        s_Y = signal("s_Y", "pe")
        s_y = signal("s_fy", "dve")
        s_st2 = signal("s_st2", "dve", 2 * CT)
        s_rs2 = signal("s_rs2", "pool", 2)
        s_y2 = signal("s_y2", "dve")
        s_aff = signal("s_aff", "pool", 2)
        s_st3 = signal("s_st3", "dve", 2 * CT)
        s_rs3 = signal("s_rs3", "pool", 2)
        s_res = signal("s_fres", "dve", 2)


        def step(i, k):
            return Step(i, k, 2, NCH)

        def schedule(eng, emit):
            for c in range(-2, 2):
                emit(step(0, c))
            with eng.Fori(0, (NCH - 4) // 2) as i:
                for k in range(2, 4):
                    emit(step(i, k))
            for c in range(NCH - 2, NCH + 2):
                emit(step(0, c))

        block = ctx.enter_context(nc.Block())

        @block.sync
        def _(sp):
            def emit(c):
                n = c - 2
                if n.live:
                    u = n.mod(2)
                    sp.wait_ge(s_res.sem, s_res.after(n))
                    sp.dma_start(out_dram[:, bass.ds(n.times(CT), CT), :], res[:, u]).then_inc(s_out[u], 16)

            for u in range(2):
                sp.sem_inc(s_out[u], 16)
            schedule(sp, emit)
            for u in range(2):
                sp.wait_ge(s_out[u], 16 + 16 * (NCH // 2))

        @block.tensor
        def _(pe):
            open_signals(pe, "pe", signals)

            def hidden(c, j, e):
                u = c.mod(2)
                if e == 0:
                    pe.wait_ge(s_gelu.sem, s_gelu.after(c, j + 1 - 2))
                pe.wait_ge(s_xe.sem, s_xe.after(c, e + 1))
                tile = slice(j * P, (j + 1) * P)
                for k, (w, x) in enumerate(((w1hi, xehi), (w1lo, xehi), (w1hi, xelo))):
                    nc.tensor.matmul(psH[j % 2][:], w[:, e, tile], x[:, u, e], start=(e == 0 and k == 0),
                                     stop=False)
                if e == E - 1:
                    nc.tensor.matmul(psH[j % 2][:], b1p[:, j * P:(j + 1) * P], onehotT[:, u], start=False,
                                     stop=True).then_inc(s_h.sem, 1)

            def spread(c, e):
                if e == 0:
                    pe.wait_ge(s_ohTc.sem, s_ohTc.after(c))
                pe.wait_ge(s_xe.sem, s_xe.after(c, e + 1 - 2))
                nc.tensor.matmul(psE[e % 2][:], sel[:, e], onehotT[:, c.mod(2)], start=True,
                                 stop=True).then_inc(s_spread.sem, 1)

            def emit(c):
                n = c + 1
                if n.live:
                    u = n.mod(2)
                    pe.wait_ge(s_xf.sem, s_xf.after(n))
                    pe.wait_ge(s_xfTc.sem, s_xfTc.after(n - 1))
                    for t in range(CT):
                        last = nc.tensor.transpose(psT[:, t * P:(t + 1) * P], xf[:, u, t], ident[:])
                    last.then_inc(s_xfT.sem, 1)
                if c.live:
                    for e in range(E):
                        hidden(c, 0, e)
                if n.live:
                    pe.wait_ge(s_xfTc.sem, s_xfTc.after(n))
                    pe.wait_ge(s_oh.sem, s_oh.after(n - 1))
                    for t in range(CT):
                        last = nc.tensor.matmul(psR[:, t * E:(t + 1) * E], xfT[:, u, t * P:(t + 1) * P], wr[:],
                                                start=True, stop=True)
                    last.then_inc(s_logit.sem, 1)
                if (c - 1).live:
                    m = c - 1
                    pe.wait_ge(s_gelu.sem, s_gelu.after(m))
                    pe.wait_ge(s_y.sem, s_y.after(m - 1))
                    for t in range(CT):
                        for j in range(IT):
                            last = nc.tensor.matmul(psY[:, t * P:(t + 1) * P], hT[:, m.mod(2), j, t * P:(t + 1) * P],
                                                    wo[:, j], start=(j == 0), stop=(j == IT - 1))
                    last.then_inc(s_Y.sem, 1)
                if c.live:
                    for e in range(E):
                        hidden(c, 1, e)
                if n.live:
                    pe.wait_ge(s_oh.sem, s_oh.after(n))
                    pe.wait_ge(s_ohTc.sem, s_ohTc.after(n - 1))
                    for t in range(CT):
                        last = nc.tensor.transpose(psO[0:3 * E, t * P:(t + 1) * P], onehot[:, u, t], ident[:])
                    last.then_inc(s_ohT.sem, 1)
                if c.live:
                    hidden(c, 2, 0)
                    hidden(c, 2, 1)
                if n.live:
                    spread(n, 0)
                    spread(n, 1)
                if c.live:
                    hidden(c, 2, 2)
                    hidden(c, 2, 3)
                    hidden(c, 3, 0)
                if n.live:
                    spread(n, 2)
                if c.live:
                    hidden(c, 3, 1)
                    hidden(c, 3, 2)
                if n.live:
                    spread(n, 3)
                if c.live:
                    hidden(c, 3, 3)

            schedule(pe, emit)

        @block.vector
        def _(dve):
            open_signals(dve, "dve", signals)
            def statistics(sig, n, which, source, mv):
                for t in range(CT):
                    nc.vector.bn_stats(stats[:, which, t], source(t)).then_inc(sig.sem, 1)
                dve.wait_ge(sig.sem, sig.after(n, CT))
                stand(dve, s_pass_dve)
                for t in range(CT):
                    nc.vector.bn_aggr(mv[:, n.mod(2), t], stats[:, which, t]).then_inc(sig.sem, 1)

            def emit(c):
                if (c + 2).live:
                    n = c + 2
                    statistics(s_st1, n, 0, lambda t: X[:, n.times(CT, t), :], mv1)
                if (c + 1).live:
                    n = c + 1
                    u = n.mod(2)
                    logits = psR[:, 0:CT * E].rearrange("p (t e) -> p t e", e=E)
                    dve.wait_ge(s_logit.sem, s_logit.after(n))
                    nc.vector.tensor_reduce(lmx[:], logits, AX.X, ALU.max).then_inc(s_oh.sem, 1)
                    dve.wait_ge(s_oh.sem, s_oh.after(n, 1))
                    nc.vector.tensor_tensor(iseq[:], logits, lmx[:].unsqueeze(2).broadcast_to([P, CT, E]),
                                            ALU.is_equal).then_inc(s_oh.sem, 1)
                    dve.wait_ge(s_oh.sem, s_oh.after(n, 2))
                    nc.vector.tensor_tensor(rank[:], iseq[:], prio[:].unsqueeze(1).broadcast_to([P, CT, E]),
                                            ALU.mult).then_inc(s_oh.sem, 1)
                    dve.wait_ge(s_oh.sem, s_oh.after(n, 3))
                    nc.vector.tensor_reduce(rmx[:], rank[:], AX.X, ALU.max).then_inc(s_oh.sem, 1)
                    dve.wait_ge(s_oh.sem, s_oh.after(n, 4))
                    nc.vector.tensor_tensor(onehot[:, u].rearrange("p t (a e) -> p t a e", a=3),
                                            rank[:].unsqueeze(2).broadcast_to([P, CT, 3, E]),
                                            rmx[:].unsqueeze(2).unsqueeze(3).broadcast_to([P, CT, 3, E]),
                                            ALU.is_equal).then_inc(s_oh.sem, 1)
                if (c - 2).live:
                    n = c - 2
                    u = n.mod(2)
                    dve.wait_ge(s_aff.sem, s_aff.after(n))
                    statistics(s_st3, n, 2, lambda t: y4[:, u, t], mv3)
                if (c + 2).live:
                    n = c + 2
                    u = n.mod(2)
                    dve.wait_ge(s_rs1.sem, s_rs1.after(n))
                    dve.wait_ge(s_xfT.sem, s_xfT.after(n - 2))
                    dve.wait_ge(s_XF.sem, s_XF.after(n - 2))
                    for t in range(CT):
                        last = nc.vector.tensor_scalar(xf[:, u, t], X[:, n.times(CT, t), :], mv1[:, u, t, 0:1],
                                                       rstd1[:, u, t:t + 1], ALU.subtract, ALU.mult)
                    last.then_inc(s_xf.sem, 1)
                if (c + 1).live:
                    n = c + 1
                    u = n.mod(2)
                    dve.wait_ge(s_xfThi.sem, s_xfThi.after(n))
                    nc.vector.tensor_tensor(xfTlo[:, u], xfT[:, u], xfThi[:, u].bitcast(F32), ALU.subtract)\
                      .then_inc(s_xfTlo.sem, 1)
                if (c - 1).live:
                    n = c - 1
                    dve.wait_ge(s_Y.sem, s_Y.after(n))
                    dve.wait_ge(s_XF.sem, s_XF.after(n))
                    nc.vector.tensor_tensor(y1[:], psY[:].rearrange("p (t d) -> p t d", t=CT), XF[:, n.mod(2)],
                                            ALU.add).then_inc(s_y.sem, 1)
                    dve.wait_ge(s_y.sem, s_y.after(n))
                    statistics(s_st2, n, 1, lambda t: y1[:, t], mv2)
                if (c - 2).live:
                    n = c - 2
                    u = n.mod(2)
                    dve.wait_ge(s_rs3.sem, s_rs3.after(n))
                    for t in range(CT):
                        last = nc.vector.tensor_scalar(y5[:, t], y4[:, u, t], mv3[:, u, t, 0:1],
                                                       rstd3[:, u, t:t + 1], ALU.subtract, ALU.mult)
                    last.then_inc(s_res.sem, 1)
                    dve.wait_ge(s_res.sem, s_res.after(n, 1))
                    dve.wait_ge(s_out[u], n.over(2, 16, 16))
                    nc.vector.tensor_tensor(res[:, u], y5[:], X[:, bass.ds(n.times(CT), CT), :], ALU.add)\
                      .then_inc(s_res.sem, 1)
                if (c + 1).live:
                    n = c + 1
                    u = n.mod(2)
                    dve.wait_ge(s_xfTlo.sem, s_xfTlo.after(n))
                    for e in range(E):
                        dve.wait_ge(s_spread.sem, s_spread.after(n, e + 1))
                        if e == 0:
                            dve.wait_ge(s_h.sem, s_h.after(n - 2))
                        nc.vector.tensor_tensor(xehi[:, u, e], psE[e % 2][:], xfThi[:, u].bitcast(F32), ALU.mult)
                        nc.vector.tensor_tensor(xelo[:, u, e], psE[e % 2][:], xfTlo[:, u].bitcast(F32), ALU.mult)\
                          .then_inc(s_xe.sem, 1)
                if (c - 1).live:
                    n = c - 1
                    dve.wait_ge(s_rs2.sem, s_rs2.after(n))
                    dve.wait_ge(s_aff.sem, s_aff.after(n - 1, 1))
                    for t in range(CT):
                        last = nc.vector.tensor_scalar(y2[:, t], y1[:, t], mv2[:, n.mod(2), t, 0:1],
                                                       rstd2[:, n.mod(2), t:t + 1], ALU.subtract, ALU.mult)
                    last.then_inc(s_y2.sem, 1)

            schedule(dve, emit)

        @block.gpsimd
        def _(pool):
            open_signals(pool, "pool", signals)

            def deviations(sig, n, which, mv, eps, rstd):
                u = n.mod(2)
                nc.gpsimd.tensor_tensor(ve[:, which], mv[:, u, :, 1], eps[:], ALU.add).then_inc(sig.sem, 1)
                pool.wait_ge(sig.sem, sig.after(n, 1))
                nc.gpsimd.tensor_tensor(rstd[:, u], ve[:, which], mhalf[:], ALU.pow).then_inc(sig.sem, 1)

            def emit(c):
                if (c + 2).live:
                    n = c + 2
                    pool.wait_ge(s_st1.sem, s_st1.after(n))
                    deviations(s_rs1, n, 0, mv1, eps_col, rstd1)
                if (c + 1).live:
                    n = c + 1
                    u = n.mod(2)
                    pool.wait_ge(s_xf.sem, s_xf.after(n))
                    pool.wait_ge(s_y.sem, s_y.after(n - 2))
                    nc.gpsimd.tensor_tensor(XF[:, u], xf[:, u], bob[:].unsqueeze(1).broadcast_to([P, CT, D]),
                                            ALU.add).then_inc(s_XF.sem, 1)
                if (c - 2).live:
                    n = c - 2
                    pool.wait_ge(s_st3.sem, s_st3.after(n))
                    deviations(s_rs3, n, 2, mv3, eps_col, rstd3)
                if (c - 1).live:
                    n = c - 1
                    pool.wait_ge(s_st2.sem, s_st2.after(n))
                    deviations(s_rs2, n, 1, mv2, eps12_col, rstd2)
                if (c - 1).live:
                    n = c - 1
                    pool.wait_ge(s_y2.sem, s_y2.after(n))
                    nc.gpsimd.tensor_tensor(y3[:], y2[:], gamma[:].unsqueeze(1).broadcast_to([P, CT, D]),
                                            ALU.mult).then_inc(s_aff.sem, 1)
                    pool.wait_ge(s_aff.sem, s_aff.after(n, 1))
                    pool.wait_ge(s_res.sem, s_res.after(n - 2, 1))
                    nc.gpsimd.tensor_tensor(y4[:, n.mod(2)], y3[:], beta[:].unsqueeze(1).broadcast_to([P, CT, D]),
                                            ALU.add).then_inc(s_aff.sem, 1)

            schedule(pool, emit)

        @block.scalar
        def _(act):
            open_signals(act, "act", signals)

            def gelu(c, j):
                act.wait_ge(s_h.sem, s_h.after(c, j + 1))
                if j == 0:
                    act.wait_ge(s_Y.sem, s_Y.after(c - 2))
                nc.scalar.activation(hT[:, c.mod(2), j], psH[j % 2][:], ACT.Gelu).then_inc(s_gelu.sem, 1)

            def emit(c):
                n = c + 1
                if n.live:
                    u = n.mod(2)
                    act.wait_ge(s_xfT.sem, s_xfT.after(n))
                    act.wait_ge(s_xe.sem, s_xe.after(n - 2))
                    nc.scalar.activation(xfT[:, u], psT[:], ACT.Copy).then_inc(s_xfTc.sem, 1)
                    act.wait_ge(s_xfTc.sem, s_xfTc.after(n))
                    nc.scalar.activation(xfThi[:, u], xfT[:, u], ACT.Copy).then_inc(s_xfThi.sem, 1)
                if c.live:
                    gelu(c, 0)
                    gelu(c, 1)
                if n.live:
                    act.wait_ge(s_ohT.sem, s_ohT.after(n))
                    act.wait_ge(s_h.sem, s_h.after(n - 2))
                    nc.scalar.activation(onehotT[:, u], psO[0:3 * E, :], ACT.Copy).then_inc(s_ohTc.sem, 1)
                if c.live:
                    gelu(c, 2)
                    gelu(c, 3)

            schedule(act, emit)


_INS = ["x", "qkv_w", "qkv_b", "rq_w", "rq_b", "rkv_w", "rkv_b", "rout_w", "rout_b", "out_w", "out_b", "gl_w",
        "gr_w"]
_FFN = ["W_router", "W1", "b1", "Wo", "bo", "ln_gamma", "ln_beta"]


def constants(np):
    i, j = np.arange(P)[:, None], np.arange(P)[None, :]
    own = np.where(j < i, 0.0, NEG)
    before = np.where((j >= i) & ~((i == 0) & (j == 0)), 0.0, NEG)
    first = np.full((P, P), NEG)
    usual = np.concatenate([before, own], 1)
    opening = np.concatenate([first, own], 1)
    octets = [opening if o % (OCT // B) == 0 else usual for o in range(OCT)]
    flip = lambda m: np.concatenate([m[:, :P].T, m[:, P:].T], 1)
    valid = np.ones((P, 2, OCT))
    for o in range(0, OCT, OCT // B):
        valid[0, 0, o] = 0
        valid[:LCH, 1, o] = 0
    col = np.arange(LATW)[None, None, :] - PC * (RING - 1)
    o, r = np.arange(OCT)[None, :, None], np.arange(PC)[:, None, None]
    latcol = np.where(col < PC * RING * (o % (OCT // B)) + r, 0.0, NEG)
    rows = np.arange(3 * E)
    sel = np.zeros((3 * E, E, P))
    sel[np.arange(E), np.arange(E)] = 1
    return {
        "ident": np.eye(P),
        "maskq": np.stack([usual] + octets, 1),
        "maskk": np.stack([flip(usual)] + [flip(m) for m in octets], 1),
        "valid": valid,
        "heads": (np.arange(LD)[:, None] // LHD == np.arange(LH)[None, :]).astype(float),
        "latrow": (np.arange(P)[None, :] // LCH == np.arange(PC)[:, None]).astype(float),
        "latcol": latcol,
        "sel": sel,
        "third": (rows[:, None] // E == np.arange(3)[None, :]).astype(float),
        "prio": np.tile(np.arange(E, 0, -1.0), (P, 1)),
    }


def kernel(**inputs):
    import numpy as _np
    import concourse.bacc as _bacc
    from concourse.bass_utils import run_bass_kernel_spmd as _run

    nc = _bacc.Bacc("TRN2", target_bir_lowering=False, num_devices=1)
    arrays, args = {}, []
    named = [(f"L0_attn_{n}", inputs[f"L0_attn_{n}"]) for n in _INS]
    named += [(f"L0_ffn_{n}", inputs[f"L0_ffn_{n}"]) for n in _FFN]
    named += [(f"const_{n}", a.astype(_np.float32)) for n, a in constants(_np).items()]
    for name, a in named:
        a = _np.ascontiguousarray(a)
        arrays[f"in_{name}_dram"] = a
        args.append(nc.dram_tensor(f"in_{name}_dram", a.shape, mybir.dt.from_np(a.dtype), kind="ExternalInput").ap())
    args.append(nc.dram_tensor("out_0_dram", (B, S, D), F32, kind="ExternalOutput").ap())
    sandwich(nc, *args)
    r = _run(nc, [arrays], core_ids=[0])
    return r.results[0]["out_0_dram"]
```

```python
from contextlib import ExitStack

import concourse.bass as bass
from concourse import mybir

F32 = mybir.dt.float32
BF16 = mybir.dt.bfloat16
F32R = mybir.dt.float32r
ACT = mybir.ActivationFunctionType
ALU = mybir.AluOpType
AX = mybir.AxisListType

P = 128
B, S, D = 2, 2048, 128
T = B * S
NB = T // P
BB = S // P
H, HD = 16, 8
LH, LHD, LD = 4, 8, 32
NLAT = 64
LCH = S // NLAT
PC = P // LCH
E, I = 4, 512
IT = I // P
CH = 512
NCH = T // CH
CT = CH // P
RING = 8
OCT = NB // RING
LATW = PC * (RING - 1) + NLAT
LC = 2
STORES = 16 * 4
LOADS = 14
PARTS_Q = [0, 0, 0, 1, 1, 2]
PARTS_K = [0, 1, 2, 0, 1, 0]
KPROD = 68
MROW = 96
KALL = MROW + 2
NEG = -float(2 ** 100)
SCALE = HD ** -0.5
VW = HD + 1
UN = H // 2
SELECTED = (0, 2, 3, 4, 6)
EPS = 1e-5
LN_EPS = 1e-12


class Step:

    def __init__(self, i, k, period, count):
        self.i, self.k, self.period, self.count = i, k, period, count

    def __add__(self, d):
        return Step(self.i, self.k + d, self.period, self.count)

    def __sub__(self, d):
        return self + (-d)

    def mod(self, m):
        return self.k % m

    def times(self, a, b=0):
        if isinstance(self.i, int):
            return a * (self.period * self.i + self.k) + b
        return self.i * (a * self.period) + (a * self.k + b)

    def over(self, m, a=1, b=0):
        whole = a * (self.k // m) + b
        return whole if isinstance(self.i, int) else self.i * (a * self.period // m) + whole

    @property
    def live(self):
        return not isinstance(self.i, int) or 0 <= self.period * self.i + self.k < self.count


LAG = 5


class Signal:

    def __init__(self, sem, owner, per=1):
        self.sem, self.owner, self.per, self.credit = sem, owner, per, LAG * per

    def after(self, step, k=None):
        k = self.per if k is None else k
        if isinstance(step.i, int) and step.times(1) >= step.count:
            step, k = Step(0, step.count - 1, step.period, step.count), self.per
        value = step.times(self.per, k + self.credit)
        return max(value, 0) if isinstance(value, int) else value


def stand(eng, passed):
    eng.sem_inc(passed, 1)


def keep_warm(nc, bank, filler, count):
    for _ in range(count):
        nc.tensor.matmul(bank, filler[:, 0:P], filler[:], start=True, stop=True)


def open_signals(eng, name, signals):
    for sig in signals:
        if sig.owner == name:
            eng.sem_inc(sig.sem, sig.credit)


class Held:

    def __init__(self, sb, sb_attend):
        self.of_ffn(sb)
        self.of_attend(sb_attend)

    def of_attend(self, sb):
        self.wout = sb("wout", [D, D])
        self.bout = sb("bout", [P, D])
        self.brout = sb("brout", [P, D])
        self.glr = sb("glr", [P, 2, HD])
        self.maskq_tab = sb("maskq_tab", [P, OCT, 2 * P])
        self.maskq = sb("maskq", [P, 2 * P])
        self.maskq0 = sb("maskq0", [P, 2 * P])
        self.maskk_f = sb("maskk_f", [P, OCT + 1, 2 * P])
        self.maskk = sb("maskk", [P, OCT + 1, 2 * P], BF16)
        self.valid = sb("valid", [P, 2, OCT])
        self.lat_row_f = sb("lat_row_f", [PC, P])
        self.lat_col_f = sb("lat_col_f", [PC, OCT, LATW])
        self.lat_row = sb("lat_row", [PC, P], BF16)
        self.lat_col = sb("lat_col", [PC, OCT, LATW], BF16)
        self.w1 = sb("w1", [D, E, I])
        self.qst = sb("qst", [P, H, RING * P], BF16)
        self.kst = sb("kst", [P, H, RING * P], BF16)
        self.vst = sb("vst", [P, RING, H, VW])
        self.rqT = sb("rqT", [LD, RING * P])
        self.ones = sb("ones", [2 * H, RING * P], BF16)

    def of_ffn(self, sb):
        self.wr = sb("wr", [D, E])
        self.w1hi = sb("w1hi", [D, E, I], F32R)
        self.w1lo = sb("w1lo", [D, E, I], F32R)
        self.wo = sb("wo", [P, IT, D])
        self.b1f = sb("b1f", [3 * E, I])
        self.b1rest = sb("b1rest", [3 * E, I])
        self.b1rest2 = sb("b1rest2", [3 * E, I])
        self.b1hi = sb("b1hi", [3 * E, I], BF16)
        self.b1mid = sb("b1mid", [3 * E, I], BF16)
        self.b1p = sb("b1p", [3 * E, I], BF16)
        self.third = sb("third", [3 * E, 3])
        self.sel_f = sb("sel_f", [3 * E, E, P])
        self.sel = sb("sel", [3 * E, E, P], BF16)
        self.prio = sb("prio", [P, E])
        self.bob = sb("bob", [P, D])
        self.gamma = sb("gamma", [P, D])
        self.beta = sb("beta", [P, D])


class InputNorm:

    def __init__(self, nc, sb, sem, X, eps_col, mhalf):
        self.nc, self.X, self.eps_col, self.mhalf = nc, X, eps_col, mhalf
        self.stats = sb("stats1", [P, CT, 6])
        self.mv = sb("mv1", [P, 2, CT, 2])
        self.ve = sb("ve1", [P, CT])
        self.rstd = sb("rstd1", [P, 2, CT])
        self.xf = sb("xf", [P, 2, CT, D])
        self.s_pass = sem("s_pass_norm")
        self.s_st = Signal(sem("s_st1"), "dve", 2 * CT)
        self.s_rs = Signal(sem("s_rs1"), "pool", 2)
        self.s_xf = Signal(sem("s_xf"), "dve")
        self.signals = [self.s_st, self.s_rs, self.s_xf]

    def statistics(self, dve, n):
        for t in range(CT):
            self.nc.vector.bn_stats(self.stats[:, t], self.X[:, n.times(CT, t), :]).then_inc(self.s_st.sem, 1)
        dve.wait_ge(self.s_st.sem, self.s_st.after(n, CT))
        stand(dve, self.s_pass)
        for t in range(CT):
            self.nc.vector.bn_aggr(self.mv[:, n.mod(2), t], self.stats[:, t]).then_inc(self.s_st.sem, 1)

    def deviations(self, pool, n):
        u = n.mod(2)
        pool.wait_ge(self.s_st.sem, self.s_st.after(n))
        self.nc.gpsimd.tensor_tensor(self.ve[:], self.mv[:, u, :, 1], self.eps_col[:], ALU.add)\
            .then_inc(self.s_rs.sem, 1)
        pool.wait_ge(self.s_rs.sem, self.s_rs.after(n, 1))
        self.nc.gpsimd.tensor_tensor(self.rstd[:, u], self.ve[:], self.mhalf[:], ALU.pow).then_inc(self.s_rs.sem, 1)

    def apply(self, dve, n):
        u = n.mod(2)
        dve.wait_ge(self.s_rs.sem, self.s_rs.after(n))
        for t in range(CT):
            last = self.nc.vector.tensor_scalar(self.xf[:, u, t], self.X[:, n.times(CT, t), :],
                                                self.mv[:, u, t, 0:1], self.rstd[:, u, t:t + 1],
                                                ALU.subtract, ALU.mult)
        last.then_inc(self.s_xf.sem, 1)


def load_parts(sp, n, side, held, scratch, s_load):
    r = n.mod(RING)
    src, dst = bass.ds(n.times(P), LC * P), slice(r * P, (r + LC) * P)
    tile, order = ((held.qst, PARTS_Q), (held.kst, PARTS_K))[side]
    for row, part in enumerate(order):
        sp.dma_start(tile[row * HD:(row + 1) * HD, :, dst],
                     scratch[side][part, :, src].rearrange("(h d) t -> d h t", d=HD)).then_inc(s_load[r // LC], 16)


def load_rest(sp, n, held, scratch, s_load):
    _, _, v_tok, rq_t = scratch
    r = n.mod(RING)
    src, dst = bass.ds(n.times(P), LC * P), slice(r * P, (r + LC) * P)
    sp.dma_start(held.vst[:, r:r + LC].rearrange("p t h e -> p t (h e)"),
                 v_tok[src, :].rearrange("(t p) n -> p t n", p=P)).then_inc(s_load[r // LC], 16)
    sp.dma_start(held.rqT[:, dst], rq_t[:, src]).then_inc(s_load[r // LC], 16)


def sandwich(nc, x, qkv_w, qkv_b, rq_w, rq_b, rkv_w, rkv_b, rout_w, rout_b, out_w, out_b, gl_w, gr_w,
             W_router, W1, b1, Wo, bo, ln_gamma, ln_beta,
             c_ident, c_maskq, c_maskk, c_valid, c_heads, c_latrow, c_latcol, c_inpool, c_sel, c_third, c_prio, out):
    with ExitStack() as ctx:
        def sb(name, shape, dt=F32):
            return ctx.enter_context(nc.sbuf_tensor(name, shape, dt))

        q_parts = nc.dram_tensor("q_parts", [3, P, T], BF16, kind="Internal").ap()
        k_parts = nc.dram_tensor("k_parts", [3, P, T], BF16, kind="Internal").ap()
        v_tok = nc.dram_tensor("v_tok", [T, H * VW], F32, kind="Internal").ap()
        rq_t = nc.dram_tensor("rq_t", [LD, T], F32, kind="Internal").ap()

        x_dram = x.rearrange("b (t p) d -> p (b t) d", p=P)
        out_dram = out.rearrange("b (t p) d -> p (b t) d", p=P)

        ident = sb("ident", [P, P])
        identb = sb("identb", [P, P], BF16)
        eps_col = sb("eps_col", [P, CT])
        eps12_col = sb("eps12_col", [P, CT])
        mhalf = sb("mhalf", [P, CT])
        filler = sb("filler", [P, CH], BF16)
        X = sb("X", [P, NB, D])
        lat_k = sb("lat_k", [LD, OCT, LH * NLAT])
        lat_v = sb("lat_v", [P, OCT, 2, D])
        scratch = (q_parts, k_parts, v_tok, rq_t)
        norm = InputNorm(nc, sb, lambda name: ctx.enter_context(nc.semaphore(name)), X, eps_col, mhalf)
        s_load = [ctx.enter_context(nc.semaphore(f"s_load{r}")) for r in range(RING // LC)]
        until_attend = ctx.enter_context(ExitStack())
        held = Held(sb, lambda name, shape, dt=F32: until_attend.enter_context(nc.sbuf_tensor(name, shape, dt)))
        for_attend = [
            (held.maskk_f[:], c_maskk), (held.lat_row_f[:], c_latrow), (held.lat_col_f[:], c_latcol),
            (held.maskq_tab[:], c_maskq[:, 1:]), (held.maskq[:], c_maskq[:, 0]), (held.maskq0[:], c_maskq[:, 1]),
            (held.valid[:], c_valid), (held.wout[:], out_w), (held.bout[:], bcast_rows(out_b)),
            (held.brout[:], bcast_rows(rout_b)), (held.glr[:, 0], bcast_rows(gl_w.rearrange("d o -> (d o)"))),
            (held.glr[:, 1], bcast_rows(gr_w.rearrange("d o -> (d o)"))),
        ]
        for_ffn = [
            (held.b1f[0:E, :], b1), (held.b1f[E:2 * E, :], b1), (held.b1f[2 * E:3 * E, :], b1),
            (held.third[:], c_third), (held.sel_f[:], c_sel), (held.prio[:], c_prio),
            (held.wr[:], W_router), (held.w1[:], W1.rearrange("e d i -> d e i")),
            (held.wo[:], Wo.rearrange("(j p) d -> p j d", p=P)), (held.bob[:], bcast_rows(bo)),
            (held.gamma[:], bcast_rows(ln_gamma)), (held.beta[:], bcast_rows(ln_beta)),
        ]

        project(nc, x_dram, qkv_w, qkv_b, rq_w, rq_b, rkv_w, rkv_b, rout_w, c_ident, c_inpool, c_heads, for_attend, held,
                ident, identb, filler, eps_col, eps12_col, mhalf, X, lat_k, lat_v, scratch, s_load)
        attend(nc, held, for_ffn, norm, ident, identb, filler, eps_col, mhalf, X, lat_k, lat_v, scratch, s_load)
        until_attend.close()
        ffn(nc, held, norm, ident, filler, eps_col, eps12_col, mhalf, X, out_dram)


def bcast_rows(ap):
    return ap.partition_broadcast(P)


def project(nc, x_dram, qkv_w, qkv_b, rq_w, rq_b, rkv_w, rkv_b, rout_w, c_ident, c_inpool, c_heads, for_attend, held,
            ident, identb, filler, eps_col, eps12_col, mhalf, X, lat_k, lat_v, scratch, s_load):
    with ExitStack() as ctx:
        def sb(name, shape, dt=F32):
            return ctx.enter_context(nc.sbuf_tensor(name, shape, dt))

        def ps(name, shape, dt=F32):
            return ctx.enter_context(nc.psum_tensor(name, shape, dt))

        def sem(name):
            return ctx.enter_context(nc.semaphore(name))

        signals = []

        def signal(name, owner, per=1):
            signals.append(Signal(sem(name), owner, per))
            return signals[-1]

        q_parts, k_parts, v_tok, rq_t = scratch
        wqkv = sb("wqkv", [D, 3 * D])
        wrq = sb("wrq", [D, LD])
        wrkv = sb("wrkv", [D, 2 * LD])
        wrout = sb("wrout", [LD, D])
        bq = sb("bq", [P, 1])
        bk = sb("bk", [P, 1])
        bv = sb("bv", [P, D])
        brq = sb("brq", [LD, 1])
        brk = sb("brk", [LD, 1])
        brv = sb("brv", [LD, 1])
        head_rows = sb("head_rows", [LD, LH])

        warm = sb("warm", [P, CT])
        stats = sb("stats", [P, 2, CT, 6])
        mv = sb("mv", [P, 2, CT, 2])
        var_eps = sb("var_eps", [P, 2, CT])
        rstd = sb("rstd", [P, 2, CT])
        xn = sb("xn", [P, 2, CT, D])
        xnT = sb("xnT", [D, 2, CH])
        split = sb("split", [P, 2, 2, 3, CH], BF16)
        resid = sb("resid", [P, 2, 2, CH])
        vt = sb("vt", [P, 2, CT, H, VW])
        rqs = sb("rqs", [LD, 2, CH])
        in_pool = sb("in_pool", [P, PC])
        pooled = sb("pooled", [D, B * NLAT])
        rkT = sb("rkT", [LD, B * NLAT])
        rvT = sb("rvT", [LD, B * NLAT])
        rv_bd = sb("rv_bd", [LD, B, LH, NLAT])

        psT = [ps(f"psT{u}", [P, CH]) for u in range(2)]
        psQ = ps("psQ", [P, CH])
        psK = ps("psK", [P, CH])
        psV = ps("psV", [P, CH])
        psR = ps("psR", [P, CH])
        psL = ps("psL", [P, CH])
        psW = ps("psW", [P, CH])

        s_w = sem("s_w")
        s_filler = sem("s_filler")
        s_x = [sem(f"s_x{u}") for u in range(2)]
        s_out = [sem(f"s_out{u}") for u in range(2)]
        s_consts = sem("s_consts")
        s_pass_dve, s_pass_sp = sem("s_pass_dve"), sem("s_pass_sp")
        s_stats = signal("s_stats", "dve", 2 * CT)
        s_rstd = signal("s_rstd", "pool", 2)
        s_xn = signal("s_xn", "dve")
        s_xT = signal("s_xT", "pe")
        s_xTc = signal("s_xTc", "act")
        s_q = signal("s_q", "pe")
        s_k = signal("s_k", "pe")
        s_v = signal("s_v", "pe")
        s_r = signal("s_r", "pe")
        s_hi = signal("s_hi", "act", 2)
        s_res = signal("s_res", "dve", 2)
        s_mid = signal("s_mid", "act", 2)
        s_lo = signal("s_lo", "pool", 2)
        s_vt = signal("s_vt", "dve")
        s_rqs = signal("s_rqs", "act")
        s_pool = signal("s_pool", "pe")
        s_later = sem("s_later")
        s_clear = sem("s_clear")
        s_clear_late = sem("s_clear_late")
        s_ones = sem("s_ones")
        s_prep = sem("s_prep")
        s_lat = sem("s_lat")
        s_latc = sem("s_latc")

        weights = [
            (ident[:], c_ident), (in_pool[:], c_inpool), (wqkv[:], qkv_w), (bq[:], qkv_b[0:D].unsqueeze(1)),
            (bk[:], qkv_b[D:2 * D].unsqueeze(1)), (bv[:], bcast_rows(qkv_b[2 * D:3 * D])), (wrq[:], rq_w),
            (brq[:], rq_b.unsqueeze(1)),
        ]
        later = for_attend + [
            (wrkv[:], rkv_w), (brk[:], rkv_b[0:LD].unsqueeze(1)), (brv[:], rkv_b[LD:2 * LD].unsqueeze(1)),
            (wrout[:], rout_w), (head_rows[:], c_heads),
        ]
        all_weights = 16 * len(weights)
        HALF = RING * P // 2
        CLEARED = ((0, 5), (5, 9), (9, H))

        def chunk(i, k):
            return Step(i, k, 2, NCH)

        def schedule(eng, emit):
            for c in range(-2, 0):
                emit(chunk(0, c))
            with eng.Fori(0, (NCH - 4) // 2) as i:
                for k in range(2):
                    emit(chunk(i, k))
            for c in range(NCH - 4, NCH):
                emit(chunk(0, c))

        def clear(eng, first, last, tiles=(), tokens=slice(0, RING * P), done=s_clear):
            for tile in tiles or (held.qst, held.kst):
                eng.memset(tile[:, first:last, tokens].bitcast(F32), 0.0).then_inc(done, 1)

        block = ctx.enter_context(nc.Block())

        @block.sync
        def _(sp):
            for u in range(2):
                sp.sem_inc(s_out[u], STORES)

            def load(c):
                u = c.mod(2)
                sp.dma_start(X[:, bass.ds(c.times(CT), CT), :],
                             x_dram[:, bass.ds(c.times(CT), CT), :]).then_inc(s_x[u], 16)

            for k in range(2):
                load(chunk(0, k))

            def store(c):
                u = c.mod(2)
                cols = bass.ds(c.times(CH), CH)
                for side, parts in enumerate((q_parts, k_parts)):
                    sp.wait_ge(s_lo.sem, s_lo.after(c, side + 1))
                    sp.dma_start(parts[:, :, cols].rearrange("a p t -> p a t"),
                                 split[:, u, side]).then_inc(s_out[u], 16)
                sp.wait_ge(s_vt.sem, s_vt.after(c))
                sp.dma_start(v_tok[cols, :].rearrange("(t p) n -> p t n", p=P),
                             vt[:, u].rearrange("p t h e -> p t (h e)")).then_inc(s_out[u], 16)
                sp.wait_ge(s_rqs.sem, s_rqs.after(c))
                stand(sp, s_pass_sp)
                sp.dma_start(rq_t[:, cols], rqs[:, u]).then_inc(s_out[u], 16)

            def emit(c):
                if (c + 4).live:
                    sp.wait_ge(s_stats.sem, s_stats.after(c + 2))
                    load(c + 4)
                if isinstance(c.i, int) and c.k < 0:
                    for dst, src in later[c.k + 2::2]:
                        sp.dma_start(dst, src).then_inc(s_later, 16)
                if c.live:
                    store(c)
                if isinstance(c.i, int) and c.k >= NCH - 4:
                    first_blocks(c.k - NCH + 4)

            def first_blocks(k):
                if k == 0:
                    sp.wait_ge(s_clear, 2 * len(CLEARED))
                    for u in range(2):
                        sp.wait_ge(s_out[u], STORES * 2)
                if k == 2:
                    sp.wait_ge(s_clear_late, 2 + 1)
                    sp.dma_start(held.kst[MROW:MROW + 2], held.ones[:]).then_inc(s_ones, 16)
                if k % 2 == 0:
                    load_parts(sp, Step(0, LC * (k // 2), RING, NB), 0, held, scratch, s_load)
                else:
                    load_parts(sp, Step(0, LC * (k // 2), RING, NB), 1, held, scratch, s_load)
                    load_rest(sp, Step(0, LC * (k // 2), RING, NB), held, scratch, s_load)

            schedule(sp, emit)
            sp.wait_ge(s_ones, 16)
            for u in range(2):
                sp.wait_ge(s_out[u], STORES * (1 + NCH // 2))

        @block.vector
        def _(dve):
            open_signals(dve, "dve", signals)
            nc.vector.memset(filler[:], 1.0).then_inc(s_filler, 1)
            nc.vector.memset(eps_col[:], EPS).then_inc(s_consts, 1)
            nc.vector.memset(eps12_col[:], LN_EPS).then_inc(s_consts, 1)
            nc.vector.memset(mhalf[:], -0.5).then_inc(s_consts, 1)
            nc.vector.memset(vt[:], 1.0).then_inc(s_consts, 1)
            clear(nc.vector, *CLEARED[0])
            dve.wait_ge(s_consts, 4)

            def statistics(c):
                u = c.mod(2)
                dve.wait_ge(s_x[u], c.over(2, 16, 16))
                dve.wait_ge(s_rstd.sem, s_rstd.after(c - 2))
                for t in range(CT):
                    nc.vector.bn_stats(stats[:, u, t, :], X[:, c.times(CT, t), :]).then_inc(s_stats.sem, 1)
                dve.wait_ge(s_stats.sem, s_stats.after(c, CT))
                stand(dve, s_pass_dve)
                for t in range(CT):
                    nc.vector.bn_aggr(mv[:, u, t, :], stats[:, u, t, :]).then_inc(s_stats.sem, 1)

            def norm(c):
                u = c.mod(2)
                dve.wait_ge(s_rstd.sem, s_rstd.after(c))
                dve.wait_ge(s_pool.sem, s_pool.after(c - 2))
                for t in range(CT):
                    last = nc.vector.tensor_scalar(xn[:, u, t, :], X[:, c.times(CT, t), :], mv[:, u, t, 0:1],
                                                   rstd[:, u, t:t + 1], ALU.subtract, ALU.mult)
                last.then_inc(s_xn.sem, 1)

            def evacuate(c):
                u = c.mod(2)
                for side, (bias, bank, ready) in enumerate(((bq, psQ, s_q), (bk, psK, s_k))):
                    dve.wait_ge(s_hi.sem, s_hi.after(c, side + 1))
                    dve.wait_ge(s_lo.sem, s_lo.after(c - 2, side + 1))
                    nc.vector.scalar_tensor_tensor(out=resid[:, u, side], in0=bank[:], scalar=bias[:, 0:1],
                                                   in1=split[:, u, side, 0], op0=ALU.add,
                                                   op1=ALU.subtract).then_inc(s_res.sem, 1)
                dve.wait_ge(s_v.sem, s_v.after(c))
                dve.wait_ge(s_out[u], c.over(2, STORES, STORES))
                nc.vector.tensor_tensor(
                    vt[:, u, :, :, 0:HD], psV[:].rearrange("p (t h e) -> p t h e", t=CT, h=H),
                    bv[:].rearrange("p (h e) -> p h e", h=H).unsqueeze(1).broadcast_to([P, CT, H, HD]),
                    ALU.add).then_inc(s_vt.sem, 1)

            def emit(c):
                if (c + 2).live:
                    statistics(c + 2)
                if isinstance(c.i, int) and c.k == 0:
                    dve.wait_ge(s_w, all_weights)
                if c.live:
                    evacuate(c)
                if (c + 2).live:
                    norm(c + 2)

            schedule(dve, emit)

            nc.vector.tensor_copy(identb[:], ident[:]).then_inc(s_consts, 1)
            dve.wait_ge(s_pool.sem, s_pool.credit + NCH)
            nc.vector.tensor_scalar(pooled[:], psL[:, 2 * P:2 * P + B * NLAT], 1.0 / LCH, None, ALU.mult).then_inc(s_latc, 1)
            dve.wait_ge(s_later, 16 * len(later))
            dve.wait_ge(s_lat, 2)
            nc.vector.tensor_scalar(rkT[:], psL[0:LD, 0:B * NLAT], brk[:, 0:1], None,
                                    ALU.add).then_inc(s_latc, 1)
            nc.vector.tensor_scalar(rvT[:], psL[0:LD, P:P + B * NLAT], brv[:, 0:1], None,
                                    ALU.add).then_inc(s_latc, 1)
            dve.wait_ge(s_latc, 3)
            rows = head_rows[:].unsqueeze(2).broadcast_to([LD, LH, NLAT])

            def per_head(tile, b):
                return tile[:, b * NLAT:(b + 1) * NLAT].unsqueeze(1).broadcast_to([LD, LH, NLAT])

            for b in range(B):
                nc.vector.tensor_tensor(rv_bd[:, b], per_head(rvT, b), rows, ALU.mult).then_inc(s_latc, 1)
            for o in range(OCT):
                nc.vector.tensor_tensor(lat_k[:, o].rearrange("r (h l) -> r h l", h=LH),
                                        per_head(rkT, o * B // OCT), rows, ALU.mult).then_inc(s_latc, 1)
            dve.wait_ge(s_lat, 3)
            for o in range(OCT):
                b = o * B // OCT
                nc.vector.tensor_copy(lat_v[:, o], psR[:].rearrange("p (b g d) -> p b g d", b=B, g=2)[:, b])\
                  .then_inc(s_latc, 1)

        @block.gpsimd
        def _(pool):
            open_signals(pool, "pool", signals)
            pool.wait_ge(s_consts, 4)

            def deviations(c):
                u = c.mod(2)
                pool.wait_ge(s_stats.sem, s_stats.after(c))
                pool.wait_ge(s_xn.sem, s_xn.after(c - 2))
                nc.gpsimd.tensor_tensor(var_eps[:, u], mv[:, u, :, 1], eps_col[:], ALU.add).then_inc(s_rstd.sem, 1)
                pool.wait_ge(s_rstd.sem, s_rstd.after(c, 1))
                nc.gpsimd.tensor_tensor(rstd[:, u], var_eps[:, u], mhalf[:], ALU.pow).then_inc(s_rstd.sem, 1)

            def low_parts(c):
                u = c.mod(2)
                for side in range(2):
                    pool.wait_ge(s_mid.sem, s_mid.after(c, side + 1))
                    nc.gpsimd.tensor_tensor(split[:, u, side, 2], resid[:, u, side], split[:, u, side, 1],
                                            ALU.subtract).then_inc(s_lo.sem, 1)

            clear(nc.gpsimd, *CLEARED[1])

            def emit(c):
                if (c + 2).live:
                    deviations(c + 2)
                if c.live:
                    low_parts(c)
                if isinstance(c.i, int) and c.k == -1:
                    clear(nc.gpsimd, *CLEARED[2], tokens=slice(0, HALF))
                if isinstance(c.i, int) and c.k == -2:
                    nc.gpsimd.memset(held.vst[:, RING - 1], 0.0).then_inc(s_clear_late, 1)
                    nc.gpsimd.memset(held.ones[:], 1.0).then_inc(s_clear_late, 1)
                for step, tile in ((NCH - 4, held.kst), (NCH - 3, held.qst)):
                    if isinstance(c.i, int) and c.k == step:
                        clear(nc.gpsimd, *CLEARED[2], (tile,), slice(HALF, RING * P), s_clear_late)

            schedule(pool, emit)

        @block.scalar
        def _(act):
            open_signals(act, "act", signals)
            for dst, src in weights:
                act.dma_start(dst, src).then_inc(s_w, 16)
            act.wait_ge(s_consts, 3)
            nc.scalar.activation(warm[:], eps_col[:], ACT.Copy)
            act.wait_ge(s_w, all_weights)

            def transposed(c):
                u = c.mod(2)
                act.wait_ge(s_xT.sem, s_xT.after(c))
                nc.scalar.activation(xnT[:, u], psT[u][:], ACT.Copy).then_inc(s_xTc.sem, 1)

            def high_parts(c):
                u = c.mod(2)
                act.wait_ge(s_out[u], c.over(2, STORES, STORES))
                for side, (bias, bank, ready) in enumerate(((bq, psQ, s_q), (bk, psK, s_k))):
                    act.wait_ge(ready.sem, ready.after(c))
                    nc.scalar.activation(split[:, u, side, 0], bank[:], ACT.Identity,
                                         bias=bias[:, 0:1]).then_inc(s_hi.sem, 1)

            def evacuate(c):
                u = c.mod(2)
                act.wait_ge(s_r.sem, s_r.after(c))
                nc.scalar.activation(rqs[:, u], psR[0:LD, :], ACT.Identity, bias=brq[:, 0:1])\
                  .then_inc(s_rqs.sem, 1)
                for side in range(2):
                    act.wait_ge(s_res.sem, s_res.after(c, side + 1))
                    nc.scalar.activation(split[:, u, side, 1], resid[:, u, side], ACT.Copy)\
                      .then_inc(s_mid.sem, 1)

            def emit(c):
                if c.live:
                    high_parts(c)
                if (c + 1).live:
                    transposed(c + 1)
                if c.live:
                    evacuate(c)

            schedule(act, emit)

            act.wait_ge(s_later, 16 * len(later))
            for dst, src in ((held.maskk, held.maskk_f), (held.lat_row, held.lat_row_f),
                             (held.lat_col, held.lat_col_f)):
                nc.scalar.activation(dst[:], src[:], ACT.Copy).then_inc(s_prep, 1)

        @block.tensor
        def _(pe):
            open_signals(pe, "pe", signals)
            pe.wait_ge(s_filler, 1)
            keep_warm(nc, psW[:], filler, 35)
            pe.wait_ge(s_w, all_weights)

            def transpose(c):
                u = c.mod(2)
                pe.wait_ge(s_xn.sem, s_xn.after(c))
                pe.wait_ge(s_xTc.sem, s_xTc.after(c - 2))
                for t in range(CT):
                    last = nc.tensor.transpose(psT[u][:, t * P:(t + 1) * P], xn[:, u, t, :], ident[:])
                last.then_inc(s_xT.sem, 1)
                for t in range(CT):
                    last = nc.tensor.matmul(psL[:, bass.ds(c.times(CT * PC, 2 * P + t * PC), PC)],
                                            xn[:, u, t, :], in_pool[:], start=True, stop=True)
                last.then_inc(s_pool.sem, 1)

            def products(c):
                u = c.mod(2)
                pe.wait_ge(s_xTc.sem, s_xTc.after(c))
                pe.wait_ge(s_res.sem, s_res.after(c - 1, 1))
                nc.tensor.matmul(psQ[:], wqkv[:, 0:D], xnT[:, u], start=True, stop=True).then_inc(s_q.sem, 1)
                pe.wait_ge(s_res.sem, s_res.after(c - 1, 2))
                nc.tensor.matmul(psK[:], wqkv[:, D:2 * D], xnT[:, u], start=True, stop=True).then_inc(s_k.sem, 1)

            def more_products(c):
                u = c.mod(2)
                pe.wait_ge(s_vt.sem, s_vt.after(c - 1))
                for t in range(CT):
                    last = nc.tensor.matmul(psV[:, t * P:(t + 1) * P], xnT[:, u, t * P:(t + 1) * P],
                                            wqkv[:, 2 * D:3 * D], start=True, stop=True)
                last.then_inc(s_v.sem, 1)
                pe.wait_ge(s_rqs.sem, s_rqs.after(c - 1))
                nc.tensor.matmul(psR[0:LD, :], wrq[:], xnT[:, u], start=True, stop=True).then_inc(s_r.sem, 1)

            def emit(c):
                if c.live:
                    products(c)
                if (c + 1).live:
                    transpose(c + 1)
                if c.live:
                    more_products(c)

            schedule(pe, emit)

            keep_warm(nc, psW[:], filler, 8)
            pe.wait_ge(s_later, 16 * len(later))
            pe.wait_ge(s_latc, 1)
            nc.tensor.matmul(psL[0:LD, 0:B * NLAT], wrkv[:, 0:LD], pooled[:], start=True,
                             stop=True).then_inc(s_lat, 1)
            nc.tensor.matmul(psL[0:LD, P:P + B * NLAT], wrkv[:, LD:2 * LD], pooled[:], start=True,
                             stop=True).then_inc(s_lat, 1)
            keep_warm(nc, psW[:], filler, 7)
            pe.wait_ge(s_latc, 3 + B)
            pe.wait_ge(s_rqs.sem, s_rqs.credit + NCH)
            for b in range(B):
                for g in range(2):
                    last = nc.tensor.matmul(psR[:, (2 * b + g) * D:(2 * b + g + 1) * D],
                                            rv_bd[:, b, 2 * g:2 * g + 2].rearrange("r h l -> r (h l)"),
                                            wrout[:], start=True, stop=True)
            last.then_inc(s_lat, 1)
            keep_warm(nc, psW[:], filler, 25)


def attend(nc, held, for_ffn, norm, ident, identb, filler, eps_col, mhalf, X, lat_k, lat_v, scratch, s_load):
    with ExitStack() as ctx:
        def sb(name, shape, dt=F32):
            return ctx.enter_context(nc.sbuf_tensor(name, shape, dt))

        def ps(name, shape, dt=F32):
            return ctx.enter_context(nc.psum_tensor(name, shape, dt))

        def sem(name):
            return ctx.enter_context(nc.semaphore(name))

        signals = []

        def signal(name, owner, per=1):
            signals.append(Signal(sem(name), owner, per))
            return signals[-1]

        wout, bout, brout, glr = held.wout, held.bout, held.brout, held.glr
        maskq_tab, maskq, maskq0, maskk, valid = held.maskq_tab, held.maskq, held.maskq0, held.maskk, held.valid
        lat_row, lat_col = held.lat_row, held.lat_col
        qst, kst, vst, rqT = held.qst, held.kst, held.vst, held.rqT

        added = sb("added", [P, H, 2 * P], BF16)
        rowmax = sb("rowmax", [P, 2, H])
        minus1 = sb("minus1", [P, H])
        mparts = sb("mparts", [P, 2, 2, H], BF16)
        mrest = sb("mrest", [P, H])
        mT = sb("mT", [2 * H, 2, P], BF16)
        probs = sb("probs", [P, UN, 2 * 2 * P])
        pvs = sb("pvs", [P, 2, 4 * P])
        den = sb("den", [P, H])
        rden = sb("rden", [P, H])
        both = sb("both", [P, 4, 2, D])
        lmax = sb("lmax", [P, LH])
        lbias = sb("lbias", [P, 2, LH])
        lexp = sb("lexp", [P, LH, NLAT])
        lsum = sb("lsum", [P, LH])
        lrs = sb("lrs", [P, LH])
        lprob = sb("lprob", [P, LH * NLAT])
        lprobT = sb("lprobT", [P, 2, P])
        gated = sb("gated", [P, H, 2 * HD])
        z = sb("z", [P, H])
        ez = sb("ez", [P, H])
        ez1 = sb("ez1", [P, H])
        gate = sb("gate", [P, 2, H])
        diff = sb("diff", [P, D])
        gdiff = sb("gdiff", [P, D])
        mixed = sb("mixed", [P, D])
        mixedT = sb("mixedT", [P, P])
        y = sb("y", [P, 2, D])
        ystats = sb("ystats", [P, 6])
        ymv = sb("ymv", [P, 2, 2])
        yve = sb("yve", [P, 1])
        yrstd = sb("yrstd", [P, 1])
        yn = sb("yn", [P, D])

        psS = [ps(f"psS{u}", [P, 2, 2 * P]) for u in range(2)]
        psST = [ps(f"psST{u}", [P, 2, 2 * P]) for u in range(2)]
        psPV = ps("psPV", [P, 4 * P])
        psA = ps("psA", [P, 512])
        psB = ps("psB", [P, 512])
        psC = ps("psC", [P, 512])
        psLS = psA[:, 0:LH * NLAT]
        psRem = psC[:, 0:D]
        psLP = psB[:, 0:2 * P]
        psMix = psB[:, 2 * P:3 * P]
        psM = psB[0:2 * H, 3 * P:3 * P + P // 2].bitcast(BF16)

        s_consts = sem("s_consts2")
        s_pass_dve, s_pass_pe, s_pass_pool = sem("s_pass_dve2"), sem("s_pass_pe2"), sem("s_pass_pool2")
        s_mrow = [sem(f"s_mrow{u}") for u in range(2)]
        s_b1 = sem("s_b1")
        s_w1hi = sem("s_w1hi")
        s_ffn = sem("s_ffn")
        s_fill = sem("s_fill")
        s_first = sem("s_first")
        s_lval = sem("s_lval")
        s_S = signal("s_S", "pe", UN)
        s_max = signal("s_max", "dve", UN)
        s_neg = signal("s_neg", "pool", 3)
        s_mT = signal("s_mT", "pe")
        s_mTc = signal("s_mTc", "act")
        s_ST = signal("s_ST", "pe", UN)
        s_exp = signal("s_exp", "act", UN)
        s_sel = signal("s_sel", "pool", len(SELECTED))
        s_pv = signal("s_pv", "pe", 4)
        s_pvs = signal("s_pvs", "act")
        s_pvT = signal("s_pvT", "pe")
        s_den = signal("s_den", "dve")
        s_local = signal("s_local", "dve")
        s_lsc = signal("s_lsc", "pe")
        s_lmax = signal("s_lmax", "dve", 2)
        s_lexp = signal("s_lexp", "act", LH)
        s_lrs = signal("s_lrs", "dve")
        s_lprob = signal("s_lprob", "pool")
        s_lpT = signal("s_lpT", "pe")
        s_lpTc = signal("s_lpTc", "act")
        s_rem = signal("s_rem", "pe")
        s_remote = signal("s_remote", "dve")
        s_gated = signal("s_gated", "pool")
        s_z = signal("s_z", "dve")
        s_ez = signal("s_ez", "act")
        s_gate = signal("s_gate", "dve", 2)
        s_mix = signal("s_mix", "pool", 3)
        s_mixT = signal("s_mixT", "pe")
        s_mixTc = signal("s_mixTc", "act")
        s_proj = signal("s_proj", "pe")
        s_y = signal("s_y", "dve")
        s_ystats = signal("s_ystats", "dve", 2)
        s_yrstd = signal("s_yrstd", "pool", 2)
        s_yn = signal("s_yn", "dve")
        s_x1 = signal("s_x1", "pool")

        CONSTS = 2

        def step(i, k):
            return Step(i, k, RING, NB)

        def chunk(c):
            return Step(0, c, 2, NCH)

        def ring(n, count=1):
            return slice(n.mod(RING) * P, (n.mod(RING) + count) * P)

        FIRST, LAST = -2, NB + 2
        LOOP = 3
        W1_FROM = LOOP + (OCT - 1) * RING
        PREPARE = NB - 2

        def schedule(eng, emit):
            for s in range(FIRST, LOOP):
                emit(step(0, s))
            with eng.Fori(0, OCT - 1) as i:
                for k in range(LOOP, LOOP + RING):
                    emit(step(i, k))
            for s in range(LOOP + (OCT - 1) * RING, LAST + 1):
                emit(step(0, s))

        block = ctx.enter_context(nc.Block())

        @block.sync
        def _(sp):
            third = step(0, 2 * LC)
            load_parts(sp, third, 0, held, scratch, s_load)
            load_parts(sp, third, 1, held, scratch, s_load)
            load_rest(sp, third, held, scratch, s_load)

            def emit(s):
                n = s + 1
                if n.live:
                    sp.wait_ge(s_mTc.sem, s_mTc.after(n))
                    sp.dma_start(qst[MROW:MROW + 2, :, ring(n)], mT[:, n.mod(2), :])\
                      .then_inc(s_mrow[n.mod(2)], 16)
                if isinstance(s.i, int) and 0 <= s.k < LOOP:
                    for dst, src in for_ffn[s.k::LOOP]:
                        sp.dma_start(dst, src).then_inc(s_ffn, 16)
                n = s + 5
                if n.mod(LC) == 0 and n.live and (s - 1).live:
                    sp.wait_ge(s_pv.sem, s_pv.after(s - 1))
                    load_parts(sp, n, 0, held, scratch, s_load)
                    load_parts(sp, n, 1, held, scratch, s_load)
                    load_rest(sp, n, held, scratch, s_load)

            schedule(sp, emit)

        @block.tensor
        def _(pe):
            open_signals(pe, "pe", signals)
            pe.wait_ge(s_consts, CONSTS)
            last_bank = psS[0][:].rearrange("p a k -> p (a k)")

            def scores(n, g):
                pe.wait_ge(s_max.sem, s_max.after(n, g + 1 - 2))
                bank = psS[g % 2]
                for a in range(2):
                    h = 2 * g + a
                    q = qst[0:KPROD, h, ring(n)]
                    if n.mod(RING):
                        last = nc.tensor.matmul(bank[:, a], q, kst[0:KPROD, h, ring(n - 1, 2)],
                                                start=True, stop=True)
                    else:
                        nc.tensor.matmul(bank[:, a, 0:P], q, kst[0:KPROD, h, ring(n - 1)], start=True, stop=True)
                        last = nc.tensor.matmul(bank[:, a, P:2 * P], q, kst[0:KPROD, h, ring(n)],
                                                start=True, stop=True)
                last.then_inc(s_S.sem, 1)

            def scores_t(n, g):
                pe.wait_ge(s_exp.sem, s_exp.after(n, g + 1 - 2))
                bank = psST[g % 2]
                masked = n.mod(RING) == 0 or g not in SELECTED
                if masked:
                    which = n.over(RING, 1, 1) if n.mod(RING) == 0 else 0
                    nc.tensor.matmul(bank[:], identb[:],
                                     maskk[:, which, :].unsqueeze(1).broadcast_to([P, 2, 2 * P]),
                                     start=True, stop=False)
                for a in range(2):
                    h = 2 * g + a
                    for side in range(2):
                        last = nc.tensor.matmul(bank[:, a, side * P:(side + 1) * P],
                                                kst[0:KALL, h, ring(n - 1 + side)], qst[0:KALL, h, ring(n)],
                                                start=not masked, stop=(not masked or (a == 1 and side == 1)))
                last.then_inc(s_ST.sem, 1)

            def values(n, G):
                pe.wait_ge(s_exp.sem, s_exp.after(n, 2 * G + 2))
                cleared = [k + 1 for k, unit in enumerate(SELECTED) if unit // 2 == G]
                if cleared:
                    pe.wait_ge(s_sel.sem, s_sel.after(n, cleared[-1]))
                if G == 0:
                    pe.wait_ge(s_pvs.sem, s_pvs.after(n - 1))
                for side in range(2):
                    for t in range(4):
                        unit, a = 2 * G + t // 2, t % 2
                        last = nc.tensor.matmul(
                            psPV[32 * t:32 * t + VW, G * P:(G + 1) * P],
                            vst[:, (n - 1 + side).mod(RING), 4 * G + t, :],
                            probs[:, unit, (2 * a + side) * P:(2 * a + side + 1) * P],
                            start=(side == 0), stop=(side == 1), skip_group_check=True)
                last.then_inc(s_pv.sem, 1)

            def emit(s):
                for g in range(UN):
                    if (s + 2).live:
                        n = s + 2
                        if g == 0 and n.mod(LC) == 0:
                            pe.wait_ge(s_load[n.mod(RING) // LC], n.over(RING, 16 * LOADS, 16 * LOADS))
                        scores(n, g)
                        if not s.live:
                            keep_warm(nc, psC[:], filler, 2 if s.k == FIRST else 1)
                    if s.live:
                        if g == 0:
                            pe.wait_ge(s_mrow[s.mod(2)], s.over(2, 16, 16))
                        scores_t(s, g)
                    if g == 0 and (s - 1).live:
                        n = s - 1
                        pe.wait_ge(s_lprob.sem, s_lprob.after(n))
                        pe.wait_ge(s_mixTc.sem, s_mixTc.after(n - 2))
                        for f in range(2):
                            last = nc.tensor.transpose(psLP[:, f * P:(f + 1) * P],
                                                       lprob[:, f * P:(f + 1) * P], ident[:])
                        last.then_inc(s_lpT.sem, 1)
                    if g == 1 and (s - 1).live:
                        values(s - 1, 3)
                    if g == 2 and (s + 1).live:
                        n = s + 1
                        pe.wait_ge(s_neg.sem, s_neg.after(n))
                        pe.wait_ge(s_lpTc.sem, s_lpTc.after(s - 1))
                        nc.tensor.transpose(psM, mparts[:, n.mod(2)].rearrange("p a h -> p (a h)"),
                                            identb[:]).then_inc(s_mT.sem, 1)
                    if g == 2 and (s - 1).live:
                        n = s - 1
                        pe.wait_ge(s_lpTc.sem, s_lpTc.after(n))
                        pe.wait_ge(s_y.sem, s_y.after(n - 2))
                        for f in range(2):
                            last = nc.tensor.matmul(psRem, lprobT[:, f, :],
                                                    lat_v[:, n.over(RING), f, :],
                                                    start=(f == 0), stop=(f == 1))
                        last.then_inc(s_rem.sem, 1)
                    if g == 2 and s.live:
                        pe.wait_ge(s_lexp.sem, s_lexp.after(s - 1))
                        stand(pe, s_pass_pe)
                        nc.tensor.matmul(psLS, rqT[:, ring(s)], lat_k[:, s.over(RING), :],
                                         start=True, stop=False)
                        first = PC * (RING - 1 - s.mod(RING))
                        window = lat_col[:, s.over(RING), first:first + NLAT]
                        nc.tensor.matmul(psLS, lat_row[:],
                                         window.unsqueeze(1).broadcast_to([PC, LH, NLAT]),
                                         start=False, stop=True).then_inc(s_lsc.sem, 1)
                    if g == 3 and s.live:
                        values(s, 0)
                    if g == 3 and (s - 2).live:
                        n = s - 2
                        if not (s - 1).live:
                            keep_warm(nc, last_bank, filler, 15)
                        pe.wait_ge(s_mix.sem, s_mix.after(n))
                        if (s + 1).live:
                            pe.wait_ge(s_mTc.sem, s_mTc.after(s + 1))
                        nc.tensor.transpose(psMix, mixed[:], ident[:]).then_inc(s_mixT.sem, 1)
                    if g == 4 and (s - 1).live:
                        n = s - 1
                        pe.wait_ge(s_pvs.sem, s_pvs.after(n))
                        pe.wait_ge(s_remote.sem, s_remote.after(n))
                        for G in range(4):
                            last = nc.tensor.transpose(psC[:, G * P:(G + 1) * P],
                                                       pvs[:, n.mod(2), G * P:(G + 1) * P], ident[:])
                        last.then_inc(s_pvT.sem, 1)
                    if g == 5 and s.live:
                        values(s, 1)
                    if g == 6 and (s - 2).live:
                        n = s - 2
                        pe.wait_ge(s_mixTc.sem, s_mixTc.after(n))
                        pe.wait_ge(s_local.sem, s_local.after(n + 1))
                        nc.tensor.matmul(psC[:, 0:D], mixedT[:], wout[:], start=True,
                                         stop=True).then_inc(s_proj.sem, 1)
                    if g == 7 and s.live:
                        values(s, 2)

            schedule(pe, emit)
            keep_warm(nc, last_bank, filler, 11)

        @block.vector
        def _(dve):
            open_signals(dve, "dve", signals + norm.signals)
            nc.vector.memset(psPV[:], 0.0).then_inc(s_consts, 1)
            nc.vector.memset(minus1[:], -1.0).then_inc(s_consts, 1)
            dve.wait_ge(s_consts, CONSTS)

            def maximum(n, g, a):
                mask = maskq if n.mod(RING) else maskq0
                if a == 0:
                    dve.wait_ge(s_S.sem, s_S.after(n, g + 1))
                    if g == 0:
                        dve.wait_ge(s_neg.sem, s_neg.after(n - 2))
                        if n.mod(RING) == 0:
                            dve.wait_ge(s_fill, n.over(RING, 1, 1))
                    stand(dve, s_pass_dve)
                h = 2 * g + a
                taken = nc.vector.tensor_tensor_reduce(added[:, h], psS[g % 2][:, a], mask[:], 1.0, NEG * 4,
                                                       ALU.add, ALU.max, rowmax[:, n.mod(2), h:h + 1])
                if a == 1:
                    taken.then_inc(s_max.sem, 1)

            def prepare(k):
                b1f, b1hi, b1mid, b1rest, b1rest2 = held.b1f, held.b1hi, held.b1mid, held.b1rest, held.b1rest2
                if k == 0:
                    dve.wait_ge(s_ffn, 16 * len(for_ffn))
                    done = nc.vector.tensor_copy(b1hi[:], b1f[:])
                elif k < 9:
                    dve.wait_ge(s_b1, k)
                if k == 1:
                    done = nc.vector.tensor_tensor(b1rest[:], b1f[:], b1hi[:], ALU.subtract)
                elif k == 2:
                    done = nc.vector.tensor_copy(b1mid[:], b1rest[:])
                elif k == 3:
                    done = nc.vector.tensor_tensor(b1rest2[:], b1rest[:], b1mid[:], ALU.subtract)
                elif k == 4:
                    done = nc.vector.tensor_scalar(b1f[:], b1hi[:], held.third[:, 0:1], None, ALU.mult)
                elif k == 5:
                    done = nc.vector.tensor_scalar(b1rest[:], b1mid[:], held.third[:, 1:2], None, ALU.mult)
                elif k == 6:
                    done = nc.vector.tensor_scalar(b1hi[:], b1rest2[:], held.third[:, 2:3], None, ALU.mult)
                elif k == 7:
                    done = nc.vector.tensor_tensor(b1mid[:], b1rest[:], b1hi[:], ALU.add)
                elif k == 8:
                    done = nc.vector.tensor_tensor(held.b1p[:], b1f[:], b1mid[:], ALU.add)
                elif 9 <= k < 9 + E:
                    e = k - 9
                    dve.wait_ge(s_w1hi, e + 1)
                    done = nc.vector.tensor_tensor(held.w1lo[:, e], held.w1[:, e], held.w1hi[:, e].bitcast(F32),
                                                   ALU.subtract)
                if k < 9 + E:
                    done.then_inc(s_b1, 1)

            def emit(s):
                for g, a in ((g, a) for g in range(UN) for a in range(2)):
                    if (s + 2).live:
                        maximum(s + 2, g, a)
                    if a == 0 and isinstance(s.i, int) and PREPARE <= s.k < PREPARE + 2:
                        prepare(UN * (s.k - PREPARE) + g)
                    if (g, a) == (1, 0) and isinstance(s.i, int) and s.k > NB:
                        norm.apply(dve, chunk(s.k - NB - 1))
                    if (g, a) == (1, 0) and isinstance(s.i, int) and NB <= s.k < NB + 2:
                        dve.wait_ge(s_x1.sem, s_x1.after(step(0, CT * (s.k - NB + 1) - 1)))
                        norm.statistics(dve, chunk(s.k - NB))
                    if (g, a) == (0, 0) and (s - 3).live:
                        n = s - 3
                        dve.wait_ge(s_ystats.sem, s_ystats.after(n, 1))
                        stand(dve, s_pass_dve)
                        nc.vector.bn_aggr(ymv[:, n.mod(2)], ystats[:]).then_inc(s_ystats.sem, 1)
                    if (g, a) == (0, 0) and (s - 2).live:
                        n = s - 2
                        dve.wait_ge(s_ez.sem, s_ez.after(n))
                        nc.vector.tensor_scalar(ez1[:], ez[:], 1.0, None, ALU.add).then_inc(s_gate.sem, 1)
                    if (g, a) == (0, 1) and (s - 2).live:
                        n = s - 2
                        dve.wait_ge(s_gate.sem, s_gate.after(n, 1))
                        nc.vector.reciprocal(gate[:, n.mod(2)], ez1[:]).then_inc(s_gate.sem, 1)
                    if (g, a) == (2, 0) and (s - 3).live:
                        n = s - 3
                        dve.wait_ge(s_yrstd.sem, s_yrstd.after(n))
                        dve.wait_ge(s_x1.sem, s_x1.after(n - 1))
                        nc.vector.tensor_scalar(yn[:], y[:, n.mod(2)], ymv[:, n.mod(2), 0:1], yrstd[:, 0:1],
                                                ALU.subtract, ALU.mult).then_inc(s_yn.sem, 1)
                    if (g, a) == (3, 0) and (s - 1).live:
                        n = s - 1
                        dve.wait_ge(s_rem.sem, s_rem.after(n))
                        dve.wait_ge(s_mix.sem, s_mix.after(n - 4))
                        nc.vector.tensor_tensor(both[:, n.mod(4), 1], psRem, brout[:],
                                                ALU.add).then_inc(s_remote.sem, 1)
                    if (g, a) == (3, 1) and s.live:
                        dve.wait_ge(s_lsc.sem, s_lsc.after(s))
                        nc.vector.tensor_reduce(lmax[:], psLS.rearrange("p (h l) -> p h l", h=LH),
                                                AX.X, ALU.max).then_inc(s_lmax.sem, 1)
                    if (g, a) == (4, 0) and s.live:
                        dve.wait_ge(s_lmax.sem, s_lmax.after(s, 1))
                        nc.vector.tensor_scalar(lbias[:, s.mod(2)], lmax[:], -SCALE, None,
                                                ALU.mult).then_inc(s_lmax.sem, 1)
                    heads = psC[:].rearrange("p (h e) -> p h e", h=H)
                    if (g, a) == (4, 1) and (s - 1).live:
                        n = s - 1
                        dve.wait_ge(s_pvT.sem, s_pvT.after(n))
                        sums = heads[:, :, HD:HD + 1]
                        if n.mod(RING) == 0:
                            nc.vector.tensor_scalar(den[:].unsqueeze(2), sums, 1e-30, None, ALU.max)\
                              .then_inc(s_first, 1)
                            dve.wait_ge(s_first, n.over(RING, 2, 1))
                            nc.vector.reciprocal(den[:], den[:]).then_inc(s_first, 1)
                            dve.wait_ge(s_first, n.over(RING, 2, 2))
                            nc.vector.tensor_scalar(rden[:], den[:], valid[:, 0, bass.ds(n.over(RING), 1)],
                                                    None, ALU.mult).then_inc(s_den.sem, 1)
                        else:
                            nc.vector.reciprocal(rden[:].unsqueeze(2), sums).then_inc(s_den.sem, 1)
                    if (g, a) == (5, 0) and (s - 1).live:
                        n = s - 1
                        dve.wait_ge(s_den.sem, s_den.after(n))
                        nc.vector.tensor_tensor(both[:, n.mod(4), 0].rearrange("p (h e) -> p h e", h=H),
                                                heads[:, :, 0:HD], rden[:].unsqueeze(2).broadcast_to([P, H, HD]),
                                                ALU.mult).then_inc(s_local.sem, 1)
                    if (g, a) == (6, 0) and s.live:
                        dve.wait_ge(s_lexp.sem, s_lexp.after(s))
                        dve.wait_ge(s_lprob.sem, s_lprob.after(s - 1))
                        nc.vector.reciprocal(lrs[:], lsum[:]).then_inc(s_lrs.sem, 1)
                        if s.mod(RING) == 0:
                            dve.wait_ge(s_lrs.sem, s_lrs.after(s))
                            nc.vector.tensor_scalar(lrs[:], lrs[:], valid[:, 1, bass.ds(s.over(RING), 1)],
                                                    None, ALU.mult).then_inc(s_lval, 1)
                    if (g, a) == (6, 1) and (s - 1).live:
                        n = s - 1
                        dve.wait_ge(s_gated.sem, s_gated.after(n))
                        nc.vector.tensor_reduce(z[:], gated[:], AX.X, ALU.add).then_inc(s_z.sem, 1)
                    if (g, a) == (7, 0) and (s - 2).live:
                        n = s - 2
                        dve.wait_ge(s_proj.sem, s_proj.after(n))
                        nc.vector.tensor_tensor(y[:, n.mod(2)], psC[:, 0:D], bout[:], ALU.add).then_inc(s_y.sem, 1)
                    if (g, a) == (7, 1) and (s - 2).live:
                        n = s - 2
                        dve.wait_ge(s_y.sem, s_y.after(n))
                        nc.vector.bn_stats(ystats[:], y[:, n.mod(2)]).then_inc(s_ystats.sem, 1)

            schedule(dve, emit)

        @block.gpsimd
        def _(pool):
            open_signals(pool, "pool", signals + norm.signals)
            pool.wait_ge(s_consts, CONSTS)
            pool.sem_inc(s_fill, 1)

            def select(n, g):
                if n.mod(RING) == 0:
                    pool.sem_inc(s_sel.sem, 1)
                    return
                pool.wait_ge(s_exp.sem, s_exp.after(n, g + 1))
                stand(pool, s_pass_pool)
                before, own = (probs[:, g].rearrange("p (a side q) -> p a side q", a=2, side=2)[:, :, side]
                               for side in range(2))
                nc.gpsimd.affine_select(out=before, in_=before, compare_op=ALU.is_gt, fill=0.0, base=0,
                                        pattern=[[0, 2], [1 - P, P]], channel_multiplier=P)
                nc.gpsimd.affine_select(out=own, in_=own, compare_op=ALU.is_gt, fill=0.0, base=0,
                                        pattern=[[0, 2], [1, P]], channel_multiplier=-1).then_inc(s_sel.sem, 1)

            def emit(s):
                if (s + 1).live:
                    n = s + 1
                    u = n.mod(2)
                    pool.wait_ge(s_max.sem, s_max.after(n))
                    pool.wait_ge(s_mT.sem, s_mT.after(n - 2))
                    nc.gpsimd.tensor_tensor(mparts[:, u, 0], rowmax[:, u], minus1[:], ALU.mult)\
                      .then_inc(s_neg.sem, 1)
                    pool.wait_ge(s_neg.sem, s_neg.after(n, 1))
                    nc.gpsimd.tensor_tensor(mrest[:], rowmax[:, u], mparts[:, u, 0], ALU.add).then_inc(s_neg.sem, 1)
                    pool.wait_ge(s_neg.sem, s_neg.after(n, 2))
                    nc.gpsimd.tensor_tensor(mparts[:, u, 1], mrest[:], minus1[:], ALU.mult).then_inc(s_neg.sem, 1)
                if isinstance(s.i, int) and s.k > NB:
                    norm.deviations(pool, chunk(s.k - NB - 1))
                if (s - 3).live:
                    n = s - 3
                    pool.wait_ge(s_ystats.sem, s_ystats.after(n))
                    pool.wait_ge(s_yn.sem, s_yn.after(n - 1))
                    nc.gpsimd.tensor_tensor(yve[:], ymv[:, n.mod(2), 1:2], eps_col[:, 0:1],
                                            ALU.add).then_inc(s_yrstd.sem, 1)
                    pool.wait_ge(s_yrstd.sem, s_yrstd.after(n, 1))
                    nc.gpsimd.tensor_tensor(yrstd[:], yve[:], mhalf[:, 0:1], ALU.pow).then_inc(s_yrstd.sem, 1)
                if s.live:
                    select(s, SELECTED[0])
                if (s - 2).live:
                    n = s - 2
                    u = n.mod(2)
                    loc, rem = both[:, n.mod(4), 0], both[:, n.mod(4), 1]
                    pool.wait_ge(s_local.sem, s_local.after(n))
                    pool.wait_ge(s_remote.sem, s_remote.after(n))
                    nc.gpsimd.tensor_tensor(diff[:], loc, rem, ALU.subtract).then_inc(s_mix.sem, 1)
                    pool.wait_ge(s_gate.sem, s_gate.after(n))
                    pool.wait_ge(s_mix.sem, s_mix.after(n, 1))
                    nc.gpsimd.tensor_tensor(gdiff[:].rearrange("p (h e) -> p h e", h=H),
                                            diff[:].rearrange("p (h e) -> p h e", h=H),
                                            gate[:, u].unsqueeze(2).broadcast_to([P, H, HD]),
                                            ALU.mult).then_inc(s_mix.sem, 1)
                    pool.wait_ge(s_mix.sem, s_mix.after(n, 2))
                    pool.wait_ge(s_mixT.sem, s_mixT.after(n - 1))
                    nc.gpsimd.tensor_tensor(mixed[:], gdiff[:], rem, ALU.add).then_inc(s_mix.sem, 1)
                if (s + 3).mod(RING) == 0 and (s + 3).live:
                    nc.gpsimd.tensor_copy(maskq0[:], maskq_tab[:, (s + 3).over(RING), :])\
                      .then_inc(s_fill, 1)
                if s.live:
                    select(s, SELECTED[1])
                    select(s, SELECTED[2])
                    select(s, SELECTED[3])
                if (s - 1).live:
                    n = s - 1
                    pool.wait_ge(s_local.sem, s_local.after(n))
                    pool.wait_ge(s_remote.sem, s_remote.after(n))
                    pool.wait_ge(s_z.sem, s_z.after(n - 1))
                    nc.gpsimd.tensor_tensor(gated[:].rearrange("p h (a e) -> p a h e", a=2),
                                            both[:, n.mod(4)].rearrange("p a (h e) -> p a h e", h=H),
                                            glr[:].unsqueeze(2).broadcast_to([P, 2, H, HD]),
                                            ALU.mult).then_inc(s_gated.sem, 1)
                if (s - 3).live:
                    n = s - 3
                    pool.wait_ge(s_yn.sem, s_yn.after(n))
                    nc.gpsimd.tensor_tensor(X[:, n.times(1), :], X[:, n.times(1), :], yn[:],
                                            ALU.add).then_inc(s_x1.sem, 1)
                if s.live:
                    pool.wait_ge(s_lrs.sem, s_lrs.after(s))
                    if s.mod(RING) == 0:
                        pool.wait_ge(s_lval, s.over(RING, 1, 1))
                    pool.wait_ge(s_lpT.sem, s_lpT.after(s - 1))
                    nc.gpsimd.tensor_tensor(lprob[:].rearrange("p (h l) -> p h l", h=LH), lexp[:],
                                            lrs[:].unsqueeze(2).broadcast_to([P, LH, NLAT]),
                                            ALU.mult).then_inc(s_lprob.sem, 1)
                    select(s, SELECTED[4])

            schedule(pool, emit)

        @block.scalar
        def _(act):
            open_signals(act, "act", signals)
            def emit(s):
                for g in range(UN):
                    if s.live:
                        act.wait_ge(s_ST.sem, s_ST.after(s, g + 1))
                        act.wait_ge(s_pv.sem, s_pv.after(s - 1, g // 2 + 1))
                        nc.scalar.activation(probs[:, g], psST[g % 2][:].rearrange("p a c -> p (a c)"), ACT.Exp,
                                             scale=SCALE).then_inc(s_exp.sem, 1)
                    if g == 0 and (s - 1).live:
                        n = s - 1
                        act.wait_ge(s_lpT.sem, s_lpT.after(n))
                        act.wait_ge(s_rem.sem, s_rem.after(n - 1))
                        nc.scalar.activation(lprobT[:].rearrange("p f q -> p (f q)"), psLP,
                                             ACT.Copy).then_inc(s_lpTc.sem, 1)
                    if g == 2 and (s + 1).live:
                        n = s + 1
                        act.wait_ge(s_mT.sem, s_mT.after(n))
                        nc.scalar.activation(mT[:, n.mod(2), :], psM, ACT.Copy).then_inc(s_mTc.sem, 1)
                    if g == 2 and (s - 1).live:
                        n = s - 1
                        act.wait_ge(s_pv.sem, s_pv.after(n))
                        act.wait_ge(s_pvT.sem, s_pvT.after(n - 2))
                        nc.scalar.activation(pvs[:, n.mod(2)], psPV[:], ACT.Copy).then_inc(s_pvs.sem, 1)
                    if g == 4 and (s - 2).live:
                        n = s - 2
                        act.wait_ge(s_mixT.sem, s_mixT.after(n))
                        act.wait_ge(s_proj.sem, s_proj.after(n - 1))
                        nc.scalar.activation(mixedT[:], psMix, ACT.Copy).then_inc(s_mixTc.sem, 1)
                    if g == 3 and isinstance(s.i, int) and 0 <= s.k - W1_FROM < E:
                        if s.k == W1_FROM:
                            act.wait_ge(s_ffn, 16 * len(for_ffn))
                            nc.scalar.activation(held.sel[:], held.sel_f[:], ACT.Copy)
                        e = s.k - W1_FROM
                        nc.scalar.activation(held.w1hi[:, e], held.w1[:, e], ACT.Copy).then_inc(s_w1hi, 1)
                    if g in (4, 5) and s.live:
                        if g == 4:
                            act.wait_ge(s_lmax.sem, s_lmax.after(s))
                            act.wait_ge(s_lprob.sem, s_lprob.after(s - 1))
                        for h in range(2 * (g - 4), 2 * (g - 4) + 2):
                            nc.scalar.activation(lexp[:, h], psLS[:, h * NLAT:(h + 1) * NLAT], ACT.Exp,
                                                 bias=lbias[:, s.mod(2), h:h + 1], scale=SCALE,
                                                 accum_out=lsum[:, h:h + 1]).then_inc(s_lexp.sem, 1)
                    if g == 7 and (s - 1).live:
                        n = s - 1
                        act.wait_ge(s_z.sem, s_z.after(n))
                        act.wait_ge(s_gate.sem, s_gate.after(n - 1, 1))
                        nc.scalar.activation(ez[:], z[:], ACT.Exp, scale=-1.0).then_inc(s_ez.sem, 1)

            schedule(act, emit)


def ffn(nc, held, norm, ident, filler, eps_col, eps12_col, mhalf, X, out_dram):
    with ExitStack() as ctx:
        def sb(name, shape, dt=F32):
            return ctx.enter_context(nc.sbuf_tensor(name, shape, dt))

        def ps(name, shape, dt=F32):
            return ctx.enter_context(nc.psum_tensor(name, shape, dt))

        def sem(name):
            return ctx.enter_context(nc.semaphore(name))

        signals = []

        def signal(name, owner, per=1):
            signals.append(Signal(sem(name), owner, per))
            return signals[-1]

        wr, wo, b1p, sel, prio = held.wr, held.wo, held.b1p, held.sel, held.prio
        w1hi, w1lo = held.w1hi, held.w1lo
        bob, gamma, beta = held.bob, held.gamma, held.beta

        stats = sb("fstats", [P, 2, CT, 6])
        mv2 = sb("mv2", [P, 2, CT, 2])
        mv3 = sb("mv3", [P, 2, CT, 2])
        ve = sb("ve", [P, 2, CT])
        rstd2 = sb("rstd2", [P, 2, CT])
        rstd3 = sb("rstd3", [P, 2, CT])
        xf, s_xf = norm.xf, norm.s_xf
        XF = sb("XF", [P, 2, CT, D])
        xfT = sb("xfT", [D, 2, CH])
        xfThi = sb("xfThi", [D, 2, CH], F32R)
        xfTlo = sb("xfTlo", [D, 2, CH], F32R)
        lmx = sb("lmx", [P, CT])
        iseq = sb("iseq", [P, CT, E])
        rank = sb("rank", [P, CT, E])
        rmx = sb("rmx", [P, CT])
        onehot = sb("onehot", [P, 2, CT, 3 * E])
        onehotT = sb("onehotT", [3 * E, 2, CH], BF16)
        xehi = sb("xehi", [D, 2, E, CH], F32R)
        xelo = sb("xelo", [D, 2, E, CH], F32R)
        hT = sb("hT", [P, 2, IT, CH])
        y1 = sb("y1", [P, CT, D])
        y2 = sb("y2", [P, CT, D])
        y3 = sb("y3", [P, CT, D])
        y4 = sb("y4", [P, 2, CT, D])
        y5 = sb("y5", [P, CT, D])
        res = sb("res", [P, 2, CT, D])

        psT = ps("fpsT", [P, CH])
        psR = ps("fpsR", [P, CH])
        psO = ps("fpsO", [P, CH])
        psE = [ps(f"fpsE{u}", [P, CH]) for u in range(2)]
        psH = [ps(f"fpsH{u}", [P, CH]) for u in range(2)]
        psY = ps("fpsY", [P, CH])

        s_pass_dve = sem("s_pass_dve3")
        s_out = [sem(f"s_store{u}") for u in range(2)]
        s_xfT = signal("s_xfT", "pe")
        s_xfTc = signal("s_xfTc", "act")
        s_xfThi = signal("s_xfThi", "act")
        s_xfTlo = signal("s_xfTlo", "dve")
        s_XF = signal("s_XF", "pool")
        s_logit = signal("s_logit", "pe")
        s_oh = signal("s_oh", "dve", 5)
        s_ohT = signal("s_ohT", "pe")
        s_ohTc = signal("s_ohTc", "act")
        s_spread = signal("s_spread", "pe", E)
        s_xe = signal("s_xe", "dve", E)
        s_h = signal("s_h", "pe", IT)
        s_gelu = signal("s_gelu", "act", IT)
        s_Y = signal("s_Y", "pe")
        s_y = signal("s_fy", "dve")
        s_st2 = signal("s_st2", "dve", 2 * CT)
        s_rs2 = signal("s_rs2", "pool", 2)
        s_y2 = signal("s_y2", "dve")
        s_aff = signal("s_aff", "pool", 2)
        s_st3 = signal("s_st3", "dve", 2 * CT)
        s_rs3 = signal("s_rs3", "pool", 2)
        s_res = signal("s_fres", "dve", 2)


        def step(i, k):
            return Step(i, k, 2, NCH)

        def schedule(eng, emit):
            for c in range(-1, 2):
                emit(step(0, c))
            with eng.Fori(0, (NCH - 4) // 2) as i:
                for k in range(2, 4):
                    emit(step(i, k))
            for c in range(NCH - 2, NCH + 2):
                emit(step(0, c))

        def last_chunk(n):
            return isinstance(n.i, int) and n.k == NCH - 1

        block = ctx.enter_context(nc.Block())

        @block.sync
        def _(sp):
            def emit(c):
                n = c - 2
                if n.live:
                    u = n.mod(2)
                    sp.wait_ge(s_res.sem, s_res.after(n))
                    sp.dma_start(out_dram[:, bass.ds(n.times(CT), CT), :], res[:, u]).then_inc(s_out[u], 16)

            for u in range(2):
                sp.sem_inc(s_out[u], 16)
            schedule(sp, emit)
            for u in range(2):
                sp.wait_ge(s_out[u], 16 + 16 * (NCH // 2))

        @block.tensor
        def _(pe):
            open_signals(pe, "pe", signals)

            def hidden(c, j, e):
                u = c.mod(2)
                if e == 0:
                    pe.wait_ge(s_gelu.sem, s_gelu.after(c, j + 1 - 2))
                pe.wait_ge(s_xe.sem, s_xe.after(c, e + 1))
                tile = slice(j * P, (j + 1) * P)
                for k, (w, x) in enumerate(((w1hi, xehi), (w1lo, xehi), (w1hi, xelo))):
                    nc.tensor.matmul(psH[j % 2][:], w[:, e, tile], x[:, u, e], start=(e == 0 and k == 0),
                                     stop=False)
                if e == E - 1:
                    nc.tensor.matmul(psH[j % 2][:], b1p[:, j * P:(j + 1) * P], onehotT[:, u], start=False,
                                     stop=True).then_inc(s_h.sem, 1)

            def spread(c, e):
                if e == 0:
                    pe.wait_ge(s_ohTc.sem, s_ohTc.after(c))
                pe.wait_ge(s_xe.sem, s_xe.after(c, e + 1 - 2))
                nc.tensor.matmul(psE[e % 2][:], sel[:, e], onehotT[:, c.mod(2)], start=True,
                                 stop=True).then_inc(s_spread.sem, 1)

            def emit(c):
                n = c + 1
                if n.live:
                    u = n.mod(2)
                    pe.wait_ge(s_xf.sem, s_xf.after(n))
                    pe.wait_ge(s_xfTc.sem, s_xfTc.after(n - 1))
                    for t in range(CT):
                        last = nc.tensor.transpose(psT[:, t * P:(t + 1) * P], xf[:, u, t], ident[:])
                    last.then_inc(s_xfT.sem, 1)
                    if not c.live:
                        keep_warm(nc, psY[:], filler, 4)
                if c.live:
                    for e in range(E):
                        hidden(c, 0, e)
                if n.live:
                    pe.wait_ge(s_xfTc.sem, s_xfTc.after(n))
                    pe.wait_ge(s_oh.sem, s_oh.after(n - 1))
                    for t in range(CT):
                        last = nc.tensor.matmul(psR[:, t * E:(t + 1) * E], xfT[:, u, t * P:(t + 1) * P], wr[:],
                                                start=True, stop=True)
                    last.then_inc(s_logit.sem, 1)
                    if not c.live:
                        keep_warm(nc, psY[:], filler, 10)
                if (c - 1).live:
                    m = c - 1
                    pe.wait_ge(s_gelu.sem, s_gelu.after(m))
                    pe.wait_ge(s_y.sem, s_y.after(m - 1))
                    for t in range(CT):
                        for j in range(IT):
                            last = nc.tensor.matmul(psY[:, t * P:(t + 1) * P], hT[:, m.mod(2), j, t * P:(t + 1) * P],
                                                    wo[:, j], start=(j == 0), stop=(j == IT - 1))
                    last.then_inc(s_Y.sem, 1)
                if c.live:
                    for e in range(E):
                        hidden(c, 1, e)
                if n.live:
                    pe.wait_ge(s_oh.sem, s_oh.after(n))
                    pe.wait_ge(s_ohTc.sem, s_ohTc.after(n - 1))
                    for t in range(CT):
                        last = nc.tensor.transpose(psO[0:3 * E, t * P:(t + 1) * P], onehot[:, u, t], ident[:])
                    last.then_inc(s_ohT.sem, 1)
                    if not c.live:
                        keep_warm(nc, psY[:], filler, 4)
                if c.live:
                    hidden(c, 2, 0)
                    hidden(c, 2, 1)
                if n.live:
                    spread(n, 0)
                    spread(n, 1)
                if c.live:
                    hidden(c, 2, 2)
                    hidden(c, 2, 3)
                    hidden(c, 3, 0)
                if n.live:
                    if not c.live:
                        keep_warm(nc, psY[:], filler, 3)
                    spread(n, 2)
                if c.live:
                    hidden(c, 3, 1)
                    hidden(c, 3, 2)
                if n.live:
                    if not c.live:
                        keep_warm(nc, psY[:], filler, 3)
                    spread(n, 3)
                if c.live:
                    hidden(c, 3, 3)

            schedule(pe, emit)

        @block.vector
        def _(dve):
            open_signals(dve, "dve", signals)
            def statistics(sig, n, which, source, mv):
                for t in range(CT):
                    nc.vector.bn_stats(stats[:, which, t], source(t)).then_inc(sig.sem, 1)
                dve.wait_ge(sig.sem, sig.after(n, CT))
                stand(dve, s_pass_dve)
                for t in range(CT):
                    nc.vector.bn_aggr(mv[:, n.mod(2), t], stats[:, which, t]).then_inc(sig.sem, 1)

            def finish(n):
                u = n.mod(2)
                if not last_chunk(n):
                    dve.wait_ge(s_rs3.sem, s_rs3.after(n))
                    for t in range(CT):
                        last = nc.vector.tensor_scalar(y5[:, t], y4[:, u, t], mv3[:, u, t, 0:1],
                                                       rstd3[:, u, t:t + 1], ALU.subtract, ALU.mult)
                    last.then_inc(s_res.sem, 1)
                    dve.wait_ge(s_res.sem, s_res.after(n, 1))
                    dve.wait_ge(s_out[u], n.over(2, 16, 16))
                    nc.vector.tensor_tensor(res[:, u], y5[:], X[:, bass.ds(n.times(CT), CT), :], ALU.add)\
                      .then_inc(s_res.sem, 1)
                    return
                dve.wait_ge(s_st3.sem, s_st3.after(n))
                for t in range(CT):
                    last = nc.vector.tensor_scalar(y5[:, t], y4[:, u, t], mv3[:, u, t, 0:1], None, ALU.subtract)
                last.then_inc(s_res.sem, 1)
                dve.wait_ge(s_res.sem, s_res.after(n, 1))
                dve.wait_ge(s_rs3.sem, s_rs3.after(n))
                dve.wait_ge(s_out[u], n.over(2, 16, 16))
                for t in range(CT):
                    last = nc.vector.scalar_tensor_tensor(out=res[:, u, t], in0=y5[:, t],
                                                          scalar=rstd3[:, u, t:t + 1],
                                                          in1=X[:, n.times(CT, t), :], op0=ALU.mult, op1=ALU.add)
                last.then_inc(s_res.sem, 1)

            def emit(c):
                if (c + 2).live and c.live:
                    norm.statistics(dve, c + 2)
                if (c + 1).live:
                    n = c + 1
                    u = n.mod(2)
                    logits = psR[:, 0:CT * E].rearrange("p (t e) -> p t e", e=E)
                    dve.wait_ge(s_logit.sem, s_logit.after(n))
                    nc.vector.tensor_reduce(lmx[:], logits, AX.X, ALU.max).then_inc(s_oh.sem, 1)
                    dve.wait_ge(s_oh.sem, s_oh.after(n, 1))
                    nc.vector.tensor_tensor(iseq[:], logits, lmx[:].unsqueeze(2).broadcast_to([P, CT, E]),
                                            ALU.is_equal).then_inc(s_oh.sem, 1)
                    dve.wait_ge(s_oh.sem, s_oh.after(n, 2))
                    nc.vector.tensor_tensor(rank[:], iseq[:], prio[:].unsqueeze(1).broadcast_to([P, CT, E]),
                                            ALU.mult).then_inc(s_oh.sem, 1)
                    dve.wait_ge(s_oh.sem, s_oh.after(n, 3))
                    nc.vector.tensor_reduce(rmx[:], rank[:], AX.X, ALU.max).then_inc(s_oh.sem, 1)
                    dve.wait_ge(s_oh.sem, s_oh.after(n, 4))
                    nc.vector.tensor_tensor(onehot[:, u].rearrange("p t (a e) -> p t a e", a=3),
                                            rank[:].unsqueeze(2).broadcast_to([P, CT, 3, E]),
                                            rmx[:].unsqueeze(2).unsqueeze(3).broadcast_to([P, CT, 3, E]),
                                            ALU.is_equal).then_inc(s_oh.sem, 1)
                if (c - 2).live:
                    n = c - 2
                    u = n.mod(2)
                    dve.wait_ge(s_aff.sem, s_aff.after(n))
                    statistics(s_st3, n, 1, lambda t: y4[:, u, t], mv3)
                if (c + 2).live and c.live:
                    dve.wait_ge(s_xfT.sem, s_xfT.after(c))
                    dve.wait_ge(s_XF.sem, s_XF.after(c))
                    norm.apply(dve, c + 2)
                if (c + 1).live:
                    n = c + 1
                    u = n.mod(2)
                    dve.wait_ge(s_xfThi.sem, s_xfThi.after(n))
                    nc.vector.tensor_tensor(xfTlo[:, u], xfT[:, u], xfThi[:, u].bitcast(F32), ALU.subtract)\
                      .then_inc(s_xfTlo.sem, 1)
                if (c - 2).live and last_chunk(c - 1):
                    finish(c - 2)
                if (c - 1).live:
                    n = c - 1
                    dve.wait_ge(s_Y.sem, s_Y.after(n))
                    dve.wait_ge(s_XF.sem, s_XF.after(n))
                    nc.vector.tensor_tensor(y1[:], psY[:].rearrange("p (t d) -> p t d", t=CT), XF[:, n.mod(2)],
                                            ALU.add).then_inc(s_y.sem, 1)
                    dve.wait_ge(s_y.sem, s_y.after(n))
                    statistics(s_st2, n, 0, lambda t: y1[:, t], mv2)
                if (c - 2).live and not last_chunk(c - 1):
                    finish(c - 2)
                if (c + 1).live:
                    n = c + 1
                    u = n.mod(2)
                    dve.wait_ge(s_xfTlo.sem, s_xfTlo.after(n))
                    for e in range(E):
                        dve.wait_ge(s_spread.sem, s_spread.after(n, e + 1))
                        if e == 0:
                            dve.wait_ge(s_h.sem, s_h.after(n - 2))
                        nc.vector.tensor_tensor(xehi[:, u, e], psE[e % 2][:], xfThi[:, u].bitcast(F32), ALU.mult)
                        nc.vector.tensor_tensor(xelo[:, u, e], psE[e % 2][:], xfTlo[:, u].bitcast(F32), ALU.mult)\
                          .then_inc(s_xe.sem, 1)
                if (c - 1).live and not last_chunk(c - 1):
                    n = c - 1
                    dve.wait_ge(s_rs2.sem, s_rs2.after(n))
                    dve.wait_ge(s_aff.sem, s_aff.after(n - 1, 1))
                    for t in range(CT):
                        last = nc.vector.tensor_scalar(y2[:, t], y1[:, t], mv2[:, n.mod(2), t, 0:1],
                                                       rstd2[:, n.mod(2), t:t + 1], ALU.subtract, ALU.mult)
                    last.then_inc(s_y2.sem, 1)
                if last_chunk(c - 1):
                    n = c - 1
                    u = n.mod(2)
                    dve.wait_ge(s_st2.sem, s_st2.after(n))
                    dve.wait_ge(s_aff.sem, s_aff.after(n - 1, 1))
                    for t in range(CT):
                        last = nc.vector.scalar_tensor_tensor(out=y2[:, t], in0=y1[:, t], scalar=mv2[:, u, t, 0:1],
                                                              in1=gamma[:], op0=ALU.subtract, op1=ALU.mult)
                    last.then_inc(s_y2.sem, 1)
                    dve.wait_ge(s_y2.sem, s_y2.after(n))
                    dve.wait_ge(s_rs2.sem, s_rs2.after(n))
                    for t in range(CT):
                        last = nc.vector.scalar_tensor_tensor(out=y4[:, u, t], in0=y2[:, t],
                                                              scalar=rstd2[:, u, t:t + 1], in1=beta[:],
                                                              op0=ALU.mult, op1=ALU.add)
                    last.then_inc(s_aff.sem, 2)

            schedule(dve, emit)

        @block.gpsimd
        def _(pool):
            open_signals(pool, "pool", signals)

            def deviations(sig, n, which, mv, eps, rstd):
                u = n.mod(2)
                nc.gpsimd.tensor_tensor(ve[:, which], mv[:, u, :, 1], eps[:], ALU.add).then_inc(sig.sem, 1)
                pool.wait_ge(sig.sem, sig.after(n, 1))
                nc.gpsimd.tensor_tensor(rstd[:, u], ve[:, which], mhalf[:], ALU.pow).then_inc(sig.sem, 1)

            def emit(c):
                if (c + 2).live and c.live:
                    norm.deviations(pool, c + 2)
                if (c + 1).live:
                    n = c + 1
                    u = n.mod(2)
                    pool.wait_ge(s_xf.sem, s_xf.after(n))
                    pool.wait_ge(s_y.sem, s_y.after(n - 2))
                    nc.gpsimd.tensor_tensor(XF[:, u], xf[:, u], bob[:].unsqueeze(1).broadcast_to([P, CT, D]),
                                            ALU.add).then_inc(s_XF.sem, 1)
                if (c - 2).live:
                    n = c - 2
                    pool.wait_ge(s_st3.sem, s_st3.after(n))
                    deviations(s_rs3, n, 1, mv3, eps_col, rstd3)
                if (c - 1).live:
                    n = c - 1
                    pool.wait_ge(s_st2.sem, s_st2.after(n))
                    deviations(s_rs2, n, 0, mv2, eps12_col, rstd2)
                if (c - 1).live and not last_chunk(c - 1):
                    n = c - 1
                    pool.wait_ge(s_y2.sem, s_y2.after(n))
                    nc.gpsimd.tensor_tensor(y3[:], y2[:], gamma[:].unsqueeze(1).broadcast_to([P, CT, D]),
                                            ALU.mult).then_inc(s_aff.sem, 1)
                    pool.wait_ge(s_aff.sem, s_aff.after(n, 1))
                    pool.wait_ge(s_res.sem, s_res.after(n - 2, 1))
                    nc.gpsimd.tensor_tensor(y4[:, n.mod(2)], y3[:], beta[:].unsqueeze(1).broadcast_to([P, CT, D]),
                                            ALU.add).then_inc(s_aff.sem, 1)

            schedule(pool, emit)

        @block.scalar
        def _(act):
            open_signals(act, "act", signals)

            def gelu(c, j):
                act.wait_ge(s_h.sem, s_h.after(c, j + 1))
                if j == 0:
                    act.wait_ge(s_Y.sem, s_Y.after(c - 2))
                nc.scalar.activation(hT[:, c.mod(2), j], psH[j % 2][:], ACT.Gelu).then_inc(s_gelu.sem, 1)

            def emit(c):
                n = c + 1
                if n.live:
                    u = n.mod(2)
                    act.wait_ge(s_xfT.sem, s_xfT.after(n))
                    act.wait_ge(s_xe.sem, s_xe.after(n - 2))
                    nc.scalar.activation(xfT[:, u], psT[:], ACT.Copy).then_inc(s_xfTc.sem, 1)
                    act.wait_ge(s_xfTc.sem, s_xfTc.after(n))
                    nc.scalar.activation(xfThi[:, u], xfT[:, u], ACT.Copy).then_inc(s_xfThi.sem, 1)
                if c.live:
                    gelu(c, 0)
                    gelu(c, 1)
                if n.live:
                    act.wait_ge(s_ohT.sem, s_ohT.after(n))
                    act.wait_ge(s_h.sem, s_h.after(n - 2))
                    nc.scalar.activation(onehotT[:, u], psO[0:3 * E, :], ACT.Copy).then_inc(s_ohTc.sem, 1)
                if c.live:
                    gelu(c, 2)
                    gelu(c, 3)

            schedule(act, emit)


_INS = ["x", "qkv_w", "qkv_b", "rq_w", "rq_b", "rkv_w", "rkv_b", "rout_w", "rout_b", "out_w", "out_b", "gl_w",
        "gr_w"]
_FFN = ["W_router", "W1", "b1", "Wo", "bo", "ln_gamma", "ln_beta"]


def constants(np):
    i, j = np.arange(P)[:, None], np.arange(P)[None, :]
    own = np.where(j < i, 0.0, NEG)
    before = np.where((j >= i) & ~((i == 0) & (j == 0)), 0.0, NEG)
    first = np.full((P, P), NEG)
    usual = np.concatenate([before, own], 1)
    opening = np.concatenate([first, own], 1)
    octets = [opening if o % (OCT // B) == 0 else usual for o in range(OCT)]
    flip = lambda m: np.concatenate([m[:, :P].T, m[:, P:].T], 1)
    valid = np.ones((P, 2, OCT))
    for o in range(0, OCT, OCT // B):
        valid[0, 0, o] = 0
        valid[:LCH, 1, o] = 0
    col = np.arange(LATW)[None, None, :] - PC * (RING - 1)
    o, r = np.arange(OCT)[None, :, None], np.arange(PC)[:, None, None]
    latcol = np.where(col < PC * RING * (o % (OCT // B)) + r, 0.0, NEG)
    rows = np.arange(3 * E)
    sel = np.zeros((3 * E, E, P))
    sel[np.arange(E), np.arange(E)] = 1
    return {
        "ident": np.eye(P),
        "maskq": np.stack([usual] + octets, 1),
        "maskk": np.stack([flip(usual)] + [flip(m) for m in octets], 1),
        "valid": valid,
        "heads": (np.arange(LD)[:, None] // LHD == np.arange(LH)[None, :]).astype(float),
        "latrow": (np.arange(P)[None, :] // LCH == np.arange(PC)[:, None]).astype(float),
        "latcol": latcol,
        "inpool": (np.arange(P)[:, None] // LCH == np.arange(PC)[None, :]).astype(float),
        "sel": sel,
        "third": (rows[:, None] // E == np.arange(3)[None, :]).astype(float),
        "prio": np.tile(np.arange(E, 0, -1.0), (P, 1)),
    }


def kernel(**inputs):
    import numpy as _np
    import concourse.bacc as _bacc
    from concourse.bass_utils import run_bass_kernel_spmd as _run

    nc = _bacc.Bacc("TRN2", target_bir_lowering=False, num_devices=1)
    arrays, args = {}, []
    named = [(f"L0_attn_{n}", inputs[f"L0_attn_{n}"]) for n in _INS]
    named += [(f"L0_ffn_{n}", inputs[f"L0_ffn_{n}"]) for n in _FFN]
    named += [(f"const_{n}", a.astype(_np.float32)) for n, a in constants(_np).items()]
    for name, a in named:
        a = _np.ascontiguousarray(a)
        arrays[f"in_{name}_dram"] = a
        args.append(nc.dram_tensor(f"in_{name}_dram", a.shape, mybir.dt.from_np(a.dtype), kind="ExternalInput").ap())
    args.append(nc.dram_tensor("out_0_dram", (B, S, D), F32, kind="ExternalOutput").ap())
    sandwich(nc, *args)
    r = _run(nc, [arrays], core_ids=[0])
    return r.results[0]["out_0_dram"]
```
